# Optimizing a Trainium2 kernel written in Bass

```python
import numpy as np
import jax
import jax.numpy as jnp

def _softmax(x, axis=-1):
    return jax.nn.softmax(x, axis=axis)

def _gelu(x):
    return jax.nn.gelu(x, approximate=True)

def _silu(x):
    return jax.nn.silu(x)

def _sigmoid(x):
    return jax.nn.sigmoid(x)

def _layernorm(x, axis=-1, eps=1e-05):
    m = jnp.mean(x, axis=axis, keepdims=True)
    v = jnp.var(x, axis=axis, keepdims=True)
    return (x - m) / jnp.sqrt(v + eps)

def _scatter_add(tgt, idx, src, axis=0):
    return tgt.at[idx].add(src)

def _segment_sum(src, seg, n):
    return jax.ops.segment_sum(src, seg, n)
kernel_name = 'mk_adaln_d1_jaxref_r8_3d26af'

def setup_inputs(seed: int=0):
    np.random.seed(seed)
    _w = jnp.asarray

    def _L0_attn_setup():
        import jax, jax.numpy as jnp
        import numpy as np
        NORM_EPS = 1e-06
        QK_SCALE = 1.0 / 128.0
        ROTARY_BASE = 1250
        INFTY_APPROX = 1e+30
        B, T, M, H, D = (2, 256, 128, 8, 128)

        def _rmsnorm(x, eps=NORM_EPS):
            ms = jnp.mean(jnp.square(x), axis=-1, keepdims=True)
            return x / jnp.sqrt(ms + eps)

        def _rope(x, base=ROTARY_BASE):
            length, width = (x.shape[-2], x.shape[-1])
            half = width // 2
            pos = jnp.arange(length, dtype=x.dtype)[:, None]
            freqs = jnp.power(jnp.asarray(base, x.dtype), -jnp.arange(half, dtype=x.dtype) / half)[None, :]
            rad = pos * freqs
            cos = jnp.cos(rad)[None, None]
            sin = jnp.sin(rad)[None, None]
            even, odd = jnp.split(x, 2, axis=-1)
            return jnp.concatenate([even * cos - odd * sin, even * sin + odd * cos], axis=-1)
        key = jax.random.key(seed)
        ks = jax.random.split(key, 5)
        std = M ** (-0.5)
        return {'x': jax.random.normal(ks[0], (B, T, M), jnp.float32), 'wq': jax.random.normal(ks[1], (M, H, D), jnp.float32) * std, 'wk': jax.random.normal(ks[2], (M, H, D), jnp.float32) * std, 'wv': jax.random.normal(ks[3], (M, H, D), jnp.float32) * std, 'wo': jax.random.normal(ks[4], (H, D, M), jnp.float32) * std}
    _L0_attn_in = _L0_attn_setup()

    def _L0_ffn_setup():
        import jax, jax.numpy as jnp
        import numpy as np
        B, T, C = (2, 256, 128)
        E = 8
        K = 2
        DFF = 4 * C
        key = jax.random.key(seed)
        ks = jax.random.split(key, 7)
        s_in = 1.0 / np.sqrt(C)
        s_ff = 1.0 / np.sqrt(DFF)
        return {'inputs': jax.random.normal(ks[0], (B, T, C), dtype=jnp.float32), 'Wr': jax.random.uniform(ks[1], (C, E), jnp.float32, -s_in, s_in), 'br': jax.random.uniform(ks[2], (E,), jnp.float32, -s_in, s_in), 'W1': jax.random.uniform(ks[3], (E, C, DFF), jnp.float32, -s_in, s_in), 'b1': jax.random.uniform(ks[4], (E, DFF), jnp.float32, -s_in, s_in), 'W2': jax.random.uniform(ks[5], (E, DFF, C), jnp.float32, -s_ff, s_ff), 'b2': jax.random.uniform(ks[6], (E, C), jnp.float32, -s_ff, s_ff)}
    _L0_ffn_in = _L0_ffn_setup()
    _L0_c = _w((lambda *s: np.random.randn(*s).astype(np.float32) * 0.05)(32, 128))
    _L0_wmod = _w((lambda *s: np.random.randn(*s).astype(np.float32) * 0.05)(128, 6 * 128) * 128 ** (-0.5))
    _d = {'L0_attn_x': _L0_attn_in['x'], 'L0_attn_wq': _L0_attn_in['wq'], 'L0_attn_wk': _L0_attn_in['wk'], 'L0_attn_wv': _L0_attn_in['wv'], 'L0_attn_wo': _L0_attn_in['wo'], 'L0_ffn_Wr': _L0_ffn_in['Wr'], 'L0_ffn_br': _L0_ffn_in['br'], 'L0_ffn_W1': _L0_ffn_in['W1'], 'L0_ffn_b1': _L0_ffn_in['b1'], 'L0_ffn_W2': _L0_ffn_in['W2'], 'L0_ffn_b2': _L0_ffn_in['b2'], 'L0_c': _L0_c, 'L0_wmod': _L0_wmod}
    _x0 = _d['L0_attn_x']
    _d['L0_attn_x'] = jax.random.normal(jax.random.fold_in(jax.random.key(seed), 1), (32, 256, 128), dtype=_x0.dtype)
    del _x0
    return _d

def reference(L0_attn_x, L0_attn_wq, L0_attn_wk, L0_attn_wv, L0_attn_wo, L0_ffn_Wr, L0_ffn_br, L0_ffn_W1, L0_ffn_b1, L0_ffn_W2, L0_ffn_b2, L0_c, L0_wmod):

    def _L0_attn_ref(x, wq, wk, wv, wo):
        import jax, jax.numpy as jnp
        import numpy as np
        NORM_EPS = 1e-06
        QK_SCALE = 1.0 / 128.0
        ROTARY_BASE = 1250
        INFTY_APPROX = 1e+30
        B, T, M, H, D = (2, 256, 128, 8, 128)

        def _rmsnorm(x, eps=NORM_EPS):
            ms = jnp.mean(jnp.square(x), axis=-1, keepdims=True)
            return x / jnp.sqrt(ms + eps)

        def _rope(x, base=ROTARY_BASE):
            length, width = (x.shape[-2], x.shape[-1])
            half = width // 2
            pos = jnp.arange(length, dtype=x.dtype)[:, None]
            freqs = jnp.power(jnp.asarray(base, x.dtype), -jnp.arange(half, dtype=x.dtype) / half)[None, :]
            rad = pos * freqs
            cos = jnp.cos(rad)[None, None]
            sin = jnp.sin(rad)[None, None]
            even, odd = jnp.split(x, 2, axis=-1)
            return jnp.concatenate([even * cos - odd * sin, even * sin + odd * cos], axis=-1)
        q = jnp.einsum('bim,mhd->bhid', x, wq)
        k = jnp.einsum('bim,mhd->bhid', x, wk)
        v = jnp.einsum('bim,mhd->bhid', x, wv)
        q = _rmsnorm(q)
        k = _rmsnorm(k)
        q = _rope(q)
        k = _rope(k)
        mult = jnp.asarray(QK_SCALE ** 0.5, q.dtype)
        s = jnp.einsum('bhid,bhjd->bhij', q * mult, k * mult)
        t = s.shape[-1]
        mask = (jnp.arange(t)[:, None] < jnp.arange(t)[None, :]).astype(s.dtype)
        s = s - jnp.asarray(INFTY_APPROX, s.dtype) * mask[None, None]
        p = jax.nn.softmax(s, axis=-1)
        o = jnp.einsum('bhij,bhjd->bhid', p, v)
        return jnp.einsum('bhid,hdm->bim', o, wo)

    def _L0_ffn_ref(inputs, Wr, br, W1, b1, W2, b2):
        import jax, jax.numpy as jnp
        import numpy as np
        B, T, C = (2, 256, 128)
        E = 8
        K = 2
        DFF = 4 * C
        scores = jax.nn.softmax(inputs @ Wr + br, axis=-1)
        _, top_idx = jax.lax.top_k(scores, K)
        mask = jax.nn.one_hot(top_idx, E, dtype=scores.dtype).sum(-2)
        masked = jnp.where(mask > 0, scores, -jnp.inf)
        weights = jax.nn.softmax(masked, axis=-1)
        hid = jax.nn.gelu(jnp.einsum('btc,ecd->bted', inputs, W1) + b1, approximate=False)
        expert_out = jnp.einsum('bted,edc->btec', hid, W2) + b2
        expert_out = jnp.where(jnp.isnan(expert_out), 0.0, expert_out)
        return jnp.einsum('bte,btec->btc', weights, expert_out)
    x = L0_attn_x
    mod = (_silu(L0_c) @ L0_wmod).reshape(L0_c.shape[0], 6, 1, -1)
    sa, ca, ga, sb, cb, gb = (mod[:, 0], mod[:, 1], mod[:, 2], mod[:, 3], mod[:, 4], mod[:, 5])
    ga = (2 * (ga >= 0) - 1) * jnp.maximum(jnp.abs(ga), 0.25)
    gb = (2 * (gb >= 0) - 1) * jnp.maximum(jnp.abs(gb), 0.25)
    h = _layernorm(x, axis=-1) * (1 + ca) + sa
    x = x + ga * _L0_attn_ref(h, L0_attn_wq, L0_attn_wk, L0_attn_wv, L0_attn_wo)
    h = _layernorm(x, axis=-1) * (1 + cb) + sb
    x = x + gb * _L0_ffn_ref(h, L0_ffn_Wr, L0_ffn_br, L0_ffn_W1, L0_ffn_b1, L0_ffn_W2, L0_ffn_b2)
    return x

_drawn_inputs = setup_inputs


def setup_inputs(seed=0):
    import zlib

    import numpy as np

    out = dict(_drawn_inputs(seed))
    spreads = {}
    factors = {'L0_attn_wq': 5.968,
     'L0_attn_wk': 5.999,
     'L0_ffn_br': 5.926,
     'L0_ffn_b1': 8.0,
     'L0_ffn_b2': 8.0}
    for name, (base, spread) in spreads.items():
        noise = np.random.default_rng([zlib.crc32(name.encode()), seed]).standard_normal(out[name].shape)
        drawn = base * np.exp(spread * noise) if base else spread * noise
        out[name] = jnp.asarray(drawn.astype(out[name].dtype))
    for name, factor in factors.items():
        out[name] = (out[name] * factor).astype(out[name].dtype)
    return out
```

```python
import math
from contextlib import ExitStack

import numpy as np

import concourse.bass as bass
from concourse import mybir

F32 = mybir.dt.float32
F16 = mybir.dt.float16
BF16 = mybir.dt.bfloat16
I32 = mybir.dt.int32
U32 = mybir.dt.uint32
ALU = mybir.AluOpType
ACT = mybir.ActivationFunctionType
AX = mybir.AxisListType


def adaln_block(nc, x, wq, wk, wv, wo, wr, br, w1, b1, w2, b2, c, wmod, rope_cos, rope_sin, out,
                debug=None, stop_after=None):
    NB, T, M = x.shape
    H, D = wq.shape[1], wq.shape[2]
    P = 128
    TT = T // P
    HD = H * D
    NU = 2 * TT
    LN_EPS, RMS_EPS = 1e-5, 1e-6
    WS = 64.0
    MASKED = -1e30
    MAGIC = 0x5F3759DF
    NCH = NU * H + 2 * TT
    E = wr.shape[1]
    K = 2
    F = w1.shape[2]
    FC = F // P
    NTOK = NB * T
    NTT = NB * TT
    TILE = 2 * P
    NTILES = (K * NTOK + E * (TILE - 1)) // TILE
    SPARE = NTILES - K * NTOK // TILE
    REGION = NTOK + TILE
    RW = M + 1
    SKIP = float(1 << 20)

    ctx = ExitStack()
    with ctx:
        phase = [ctx]

        def sb(name, shape, dt=F32):
            return phase[0].enter_context(nc.sbuf_tensor(name, shape, dt))

        def ps(name, shape, dt=F32):
            return phase[0].enter_context(nc.psum_tensor(name, shape, dt))

        def sem(name):
            return ctx.enter_context(nc.semaphore(name))

        x_all = sb("x_all", [P, NB * TT, M])
        weights = sb("weights", [P, NTT, K])
        token_at = sb("token_at", [P, NTT, K])
        table = sb("table", [P, 2, NTILES], I32)
        counts_i = sb("counts_i", [P, E], I32)
        x_rows = nc.dram_tensor("x_rows", [(E * REGION + SPARE * TILE), RW], F32).ap()
        y_rows = nc.dram_tensor("y_rows", [K * NTOK, M], F32).ap()
        mod_dram = nc.dram_tensor("mod_dram", [NB, 4 * M], F32).ap()

        phase[0] = attention = ExitStack()
        wqk_hi = sb("wqk_hi", [P, 2 * HD], F16)
        wqk_lo = sb("wqk_lo", [P, 2 * HD], F16)
        wvo_hi = sb("wvo_hi", [P, HD], F16)
        wvo_lo = sb("wvo_lo", [P, HD], F16)
        ident = sb("ident", [P, P])
        ident_bf = sb("ident_bf", [P, P], BF16)
        causal_bf = sb("causal_bf", [P, P], BF16)
        cos_sb = sb("cos_sb", [P, TT, D // 2])
        sin_sb = sb("sin_sb", [P, TT, D])
        mod_t = sb("mod_t", [P, 2, NB])
        mod_rows = sb("mod_rows", [NB, 4 * M])
        silu_c = sb("silu_c", [NB, M])
        c_sb = sb("c_sb", [NB, M])
        silu_ct = sb("silu_ct", [P, NB])
        wmod_sb = sb("wmod_sb", [P, 6 * M])
        guard_a = sb("guard_a", [NB, 2 * M])
        guard_b = sb("guard_b", [NB, 2 * M])
        roped = [sb(f"roped{k}", [P, NU, HD]) for k in range(2)]
        rope_b = sb("rope_b", [P, 2, HD])
        squares = sb("squares", [P, 2, HD])
        q_t = [sb(f"q_t{k}", [P, H, T]) for k in range(2)]
        k_t = [sb(f"k_t{k}", [P, H, T]) for k in range(2)]
        VW = D + 2
        vals = [sb(f"vals{k}", [P, TT, H, VW]) for k in range(2)]
        NPR = 4
        probs = sb("probs", [P, NPR, T + P])
        h_t = sb("h_t", [P, T])
        h_hi = [sb(f"h_hi{k}", [P, T], F16) for k in range(2)]
        h_lo = [sb(f"h_lo{k}", [P, T], F16) for k in range(2)]
        xn = sb("xn", [P, TT, M])
        acc = sb("acc", [P, TT, M])
        den = sb("den", [P, 2, TT])
        ssq = [sb(f"ssq{k}", [P, NU * H]) for k in range(2)]
        bst = sb("bst", [P, TT, 6])
        mv = [sb(f"mv{k}", [P, TT, 2]) for k in range(2)]
        vx = sb("vx", [P, NCH])
        half_bits = sb("half_bits", [P, NCH], I32)
        y_a = sb("y_a", [P, NCH])
        y_t = sb("y_t", [P, NCH])
        rr = [sb(f"rr{k}", [P, NCH]) for k in range(2)]
        ga_b = [sb(f"ga_b{k}", [P, M]) for k in range(2)]
        sbcb_b = [sb(f"sbcb_b{k}", [P, 2 * M]) for k in range(2)]
        mv2 = [sb(f"mv2{k}", [P, TT, 2]) for k in range(2)]
        bst2 = sb("bst2", [P, TT, 6])
        xn2 = sb("xn2", [P, TT, M])
        rows = [[sb(f"rows{j}{k}", [P, TT, RW]) for k in range(2)] for j in range(K)]
        h2_t = sb("h2_t", [P, T])
        wr_sb = sb("wr_sb", [P, E])
        br_b = sb("br_b", [P, E])
        lg = [sb(f"lg{k}", [P, TT, E]) for k in range(2)]
        top_l = sb("top_l", [P, TT, 8])
        lg_m = sb("lg_m", [P, TT, E])
        e_lg = sb("e_lg", [P, TT, E])
        e_sum = sb("e_sum", [P, TT])
        e_rec = sb("e_rec", [P, TT])
        score = sb("score", [P, TT, E])
        top_s = sb("top_s", [P, TT, 8])
        top_i = sb("top_i", [P, TT, 8], U32)
        top_f = sb("top_f", [P, TT, K])
        gap = sb("gap", [P, TT])
        e_gap = sb("e_gap", [P, TT])
        w_den = sb("w_den", [P, TT])
        iota_e = sb("iota_e", [P, E])
        base_e = sb("base_e", [P, E])
        one_hot = sb("one_hot", [P, TT * K, E])
        chosen = sb("chosen", [P, TT, E], BF16)
        counts = [sb(f"counts{k}", [P, E], BF16) for k in range(2)]
        before_bf = sb("before_bf", [P, P], BF16)
        ones_bf = sb("ones_bf", [P, P], BF16)
        place_e = sb("place_e", [P, TT, E])
        place_k = sb("place_k", [P, TT * K, E])
        place_f = sb("place_f", [P, TT * K])
        place = [sb(f"place{k}", [P, TT * K], I32) for k in range(2)]
        ones_e = sb("ones_e", [P, E])
        iota_t = sb("iota_t", [P, NTILES])
        tiles_i = sb("tiles_i", [P, E], I32)
        tiles_f = sb("tiles_f", [P, E])
        tiles_to = sb("tiles_to", [P, E])
        behind = sb("behind", [P, NTILES, E])
        tile_e = sb("tile_e", [P, NTILES])
        tile_r = sb("tile_r", [P, NTILES])
        filler = sb("filler", [P, TILE // P, RW])
        UN = [ps(f"unit{k}", [P, 2 * 512]) for k in range(2)]
        SC = [ps(f"scores{k}", [P, 512]) for k in range(2)]
        OP = [ps(f"pv{k}", [P, 512]) for k in range(2)]

        names = """w_in c_in wv_in const_in x_in0 x_in1 ga_in0 ga_in1 consts_ready ones_ready silu_done ct_done
            ct_ready mod_done mod_copied guard_done mod_stored wvt_done wvt_ready wvo_done wvo_ready
            hi_done split_done wvo_scaled wvo_hi_done
            tx_done p_done tr_done vw_done s_done o_done
            ht32_done hhi_done h_ready sq_done ssq_done ropea_done rope_done add_done qs_done
            tr_copied vals_ready exp_done den_done acc_done x2_done stat_done mv_done chain_done rr_done xn_ready
            out_done router_in sbcb_in0 sbcb_in1 iota_done scattered0 scattered1 filled
            mv2_done stat2_done xn2_done h2_ready rows_copied h2t_done h2t_copied rt_done lg_ready
            route_step route_exp px_done count_done table_step tail_filled
            b1_turned b1_ready w1_in w2_in w1_hi_done w1_split b_in tile_in0 tile_in1 tile_in2 tile_in3 places_ready t_done x_hi_done x_split up_done gelu_done down_done
            y_step y_stored0 y_stored1 y_stored2 y_stored3
            back_in0 back_in1 part_done mix_done out_stored0 out_stored1""".split()
        S = {n: sem(n) for n in names}

        def wait(e, name, value):
            if isinstance(value, int) and value <= 0:
                return
            e.wait_ge(S[name], value)

        counted = {}

        def alone(e, name, value):
            if isinstance(value, int):
                wait(e, name, value)
            else:
                if e not in counted:
                    counted[e] = e.alloc_register("awaited")
                e.reg_mov(counted[e], value)
                e.wait_ge(S["consts_ready"], 1)
                e.wait_ge(S[name], counted[e])

        def iterations(e, body):
            def live(n):
                return [0 <= n + d < NB for d in (2, 1, 0, -1, -2, -3, -4, -5)]
            for n in range(-2, 6):
                body(n // 2, n % 2, live(n))
            with e.Fori(3, NB // 2 - 1) as half:
                for parity in range(2):
                    body(half, parity, [True] * 8)
            for n in range(NB - 2, NB + 5):
                body(n // 2, n % 2, live(n))

        (TOP_L0, TOP_L1, LESS_TOP, E_SUM, E_REC, SCORE, TOP_S0, TOP_S1, TOP_I0, TOP_I1, TOP_F, GAP, ONE_HOT, CHOSEN,
         COUNT_A, COUNT_B, W_DEN, W_FIRST, W_SECOND, TO_0, TO_1, PLACE_E, PLACE_K, PLACE_F, PLACE_I) = range(1, 26)
        STEPS = PLACE_I

        def sc_wait(e, half, parity, b):
            if not isinstance(b, int) or b >= 2:
                e.wait_ge(S[f"scattered{parity}"], 16 * TT * K * (half - 2))

        def cap(v, most):
            return min(v, most) if isinstance(v, int) else v

        block = attention.enter_context(nc.Block())

        @block.sync
        def _(sp):
            sp.dma_start(c_sb[:, :], c).then_inc(S["c_in"], 16)
            sp.dma_start(wmod_sb[:, :], wmod).then_inc(S["c_in"], 16)
            sp.dma_start(x_all[:, 0:TT, :], x[0].rearrange("(t p) m -> p t m", p=P)).then_inc(S["x_in0"], 16)
            sp.dma_start(x_all[:, TT:2 * TT, :], x[1].rearrange("(t p) m -> p t m", p=P)).then_inc(S["x_in1"], 16)
            sp.dma_start(roped[0][:, 2, :], wv.rearrange("m h d -> m (h d)")).then_inc(S["wv_in"], 16)
            sp.dma_start(roped[0][:, 3, :].rearrange("p (h m) -> p h m", h=H),
                         wo.rearrange("h d m -> d h m")).then_inc(S["wv_in"], 16)
            sp.dma_start(roped[0][:, 0, :], wq.rearrange("m h d -> m (h d)")).then_inc(S["w_in"], 16)
            sp.dma_start(roped[0][:, 1, :], wk.rearrange("m h d -> m (h d)")).then_inc(S["w_in"], 16)
            sp.dma_start(cos_sb[:, :, :], rope_cos.rearrange("(t p) d -> p t d", p=P)).then_inc(S["const_in"], 16)
            sp.dma_start(sin_sb[:, :, :], rope_sin.rearrange("(t p) d -> p t d", p=P)).then_inc(S["const_in"], 16)
            xv = x.rearrange("b (t p) m -> p (b t) m", p=P)
            with sp.Fori(1, NB // 2) as half:
                for parity in range(2):
                    sp.wait_ge(S[f"x_in{parity}"], 16 * half)
                    sp.dma_start(x_all[:, bass.ds(half * (2 * TT) + parity * TT, TT), :],
                                 xv[:, bass.ds(half * (2 * TT) + parity * TT, TT), :])\
                        .then_inc(S[f"x_in{parity}"], 16)
            sp.dma_start(wr_sb[:, :], wr).then_inc(S["router_in"], 16)
            sp.dma_start(br_b[:, :], br.rearrange("(o e) -> o e", o=1).broadcast_to([P, E]))\
                .then_inc(S["router_in"], 16)
            sp.wait_ge(S["iota_done"], 11)
            for k in range(SPARE):
                r0 = E * REGION + k * TILE
                sp.dma_start(x_rows[r0:r0 + TILE, :].rearrange("(p s) c -> p s c", p=P), filler[:, :, :])\
                    .then_inc(S["filled"], 16)
            sp.wait_ge(S["guard_done"], 5)
            sp.dma_start(mod_dram, mod_rows[:, :]).then_inc(S["mod_stored"], 16)
            sp.wait_ge(S["mod_stored"], 16)
            for parity in range(2):
                sp.dma_start(ga_b[parity][:, :], mod_dram[parity:parity + 1, 0:M].broadcast_to([P, M]))\
                    .then_inc(S[f"ga_in{parity}"], 16)
                sp.dma_start(sbcb_b[parity][:, :], mod_dram[parity:parity + 1, M:3 * M].broadcast_to([P, 2 * M]))\
                    .then_inc(S[f"sbcb_in{parity}"], 16)
            with sp.Fori(1, NB // 2) as half:
                for parity in range(2):
                    row = bass.ds(half * 2 + parity, 1)
                    alone(sp, "x2_done", 4 * half + 2 * parity - 2)
                    sp.wait_ge(S[f"ga_in{parity}"], 16 * half)
                    sp.dma_start(ga_b[parity][:, :], mod_dram[row, 0:M].broadcast_to([P, M]))\
                        .then_inc(S[f"ga_in{parity}"], 16)
                    sp.wait_ge(S["h2_ready"], 2 * half + parity - 1)
                    sp.wait_ge(S[f"sbcb_in{parity}"], 16 * half)
                    sp.dma_start(sbcb_b[parity][:, :], mod_dram[row, M:3 * M].broadcast_to([P, 2 * M]))\
                        .then_inc(S[f"sbcb_in{parity}"], 16)
            sp.wait_ge(S["table_step"], 1)
            sp.wait_ge(S["filled"], 16 * SPARE)
            for e in range(E):
                end = sp.value_load(counts_i[0:1, e:e + 1], min_val=0, max_val=NTOK)
                sp.dma_start(x_rows[bass.ds(end + e * REGION, TILE), :].rearrange("(p s) c -> p s c", p=P),
                             filler[:, :, :]).then_inc(S["tail_filled"], 16)
            sp.wait_ge(S["tail_filled"], 16 * E)

        @block.gpsimd
        def _(pool):
            pool.memset(ident[:, :], 0.0).then_inc(S["consts_ready"], 1)
            pool.memset(ident_bf[:, :], 0.0).then_inc(S["consts_ready"], 1)
            pool.memset(causal_bf[:, :], 0.0).then_inc(S["consts_ready"], 1)
            pool.wait_ge(S["consts_ready"], 3)
            for tile in (ident, ident_bf):
                pool.affine_select(out=tile[:, :], in_=tile[:, :], compare_op=ALU.not_equal, fill=1.0,
                                   base=0, pattern=[[-1, P]], channel_multiplier=1).then_inc(S["consts_ready"], 1)
            pool.affine_select(out=causal_bf[:, :], in_=causal_bf[:, :], compare_op=ALU.is_ge, fill=MASKED,
                               base=0, pattern=[[1, P]], channel_multiplier=-1).then_inc(S["consts_ready"], 1)
            pool.memset(before_bf[:, :], 0.0).then_inc(S["iota_done"], 1)
            pool.memset(filler[:, :, :], 0.0).then_inc(S["iota_done"], 1)
            pool.iota(token_at[:, :, :], pattern=[[P, NTT], [NTOK, K]], base=0, channel_multiplier=1,
                      allow_small_or_imprecise_dtypes=True).then_inc(S["iota_done"], 1)
            pool.iota(iota_e[:, :], pattern=[[1, E]], base=0, channel_multiplier=0,
                      allow_small_or_imprecise_dtypes=True).then_inc(S["iota_done"], 1)
            pool.wait_ge(S["iota_done"], 2)
            pool.affine_select(out=before_bf[:, :], in_=before_bf[:, :], compare_op=ALU.is_ge, fill=1.0,
                               base=0, pattern=[[-1, P]], channel_multiplier=1).then_inc(S["iota_done"], 1)
            pool.memset(filler[:, :, M:RW], SKIP).then_inc(S["iota_done"], 1)
            pool.iota(base_e[:, :], pattern=[[REGION, E]], base=0, channel_multiplier=0,
                      allow_small_or_imprecise_dtypes=True).then_inc(S["iota_done"], 1)
            pool.memset(ones_e[:, :], 1.0).then_inc(S["iota_done"], 1)
            pool.iota(iota_t[:, :], pattern=[[1, NTILES]], base=0, channel_multiplier=0,
                      allow_small_or_imprecise_dtypes=True).then_inc(S["iota_done"], 1)
            pool.memset(ones_bf[:, :], 1.0).then_inc(S["iota_done"], 1)
            pool.memset(counts[0][:, :], 0.0).then_inc(S["iota_done"], 1)
            for k in range(2):
                pool.memset(mv2[k][:, :, :], 1.0).then_inc(S["ones_ready"], 1)
                pool.memset(vals[k][:, :, :, D:VW], 1.0).then_inc(S["ones_ready"], 1)
                pool.memset(ssq[k][:, :], 1.0).then_inc(S["ones_ready"], 1)
                pool.memset(mv[k][:, :, :], 1.0).then_inc(S["ones_ready"], 1)

            def body(half, parity, live):
                n = 2 * half + parity
                _, _, A, B, _, _, _, RT = live
                if B:
                    b = n - 1
                    wait(pool, "rr_done", n + 2)
                    wait(pool, "add_done", NU * b + TT)
                    for t in range(TT):
                        v = roped[1 - parity][:, t, :].rearrange("p (h d) -> p h d", h=H)
                        r = rr[1 - parity][:, t * H:(t + 1) * H].rearrange("p (h o) -> p h o", o=1)\
                            .to_broadcast([P, H, D])
                        pool.tensor_tensor(out=v, in0=v, in1=r, op=ALU.mult).then_inc(S["qs_done"], 1)
                if A:
                    for u in range(NU):
                        wait(pool, "rope_done", NU * n + u + 1)
                        pool.tensor_tensor(out=roped[parity][:, u, :], in0=roped[parity][:, u, :],
                                           in1=rope_b[:, u % 2, :], op=ALU.add).then_inc(S["add_done"], 1)
                if RT:
                    b = n - 5
                    alone(pool, "route_step", STEPS * (b + 1))
                    wait(pool, "rows_copied", b + 1)
                    for t in range(TT):
                        for j in range(K):
                            at = place[1 - parity][:, t * K + j:t * K + j + 1]
                            pool.indirect_dma_start(
                                out=x_rows, out_offset=bass.IndirectOffsetOnAxis(ap=at, axis=0),
                                in_=rows[j][1 - parity][:, t, :], in_offset=None)\
                                .then_inc(S[f"scattered{1 - parity}"], 16)
            iterations(pool, body)
            for k in range(2):
                pool.wait_ge(S[f"scattered{k}"], 16 * TT * K * NB // 2)

        @block.scalar
        def _(act):
            act.wait_ge(S["c_in"], 32)
            nc.scalar.activation(silu_c[:, :], c_sb[:, :], ACT.Silu).then_inc(S["silu_done"], 1)
            act.wait_ge(S["w_in"], 32)
            for k in range(2):
                nc.scalar.activation(wqk_hi[:, k * HD:(k + 1) * HD], roped[0][:, k, :], ACT.Copy, scale=WS)\
                    .then_inc(S["hi_done"], 1)
            act.wait_ge(S["wvt_done"], 1)
            nc.scalar.activation(roped[1][:, 0, :], UN[0][:, :], ACT.Copy).then_inc(S["wvt_ready"], 1)
            act.wait_ge(S["wvo_done"], 1)
            nc.scalar.activation(roped[1][:, 1, :], UN[1][:, :], ACT.Copy, scale=WS).then_inc(S["wvo_scaled"], 1)
            act.wait_ge(S["wvo_scaled"], 1)
            nc.scalar.activation(wvo_hi[:, :], roped[1][:, 1, :], ACT.Copy).then_inc(S["wvo_hi_done"], 1)
            act.wait_ge(S["ones_ready"], 8)
            act.wait_ge(S["mod_copied"], 2)

            def body(half, parity, live):
                n = 2 * half + parity
                _, X, A, B, C, _, N2, RT = live
                for h in range(H):
                    if C:
                        b = n - 2
                        g = H * b + h
                        if h == 0:
                            wait(act, "rr_done", b + 3)
                        wait(act, "s_done", g + 1)
                        wait(act, "o_done", g - NPR + 1)
                        wait(act, "exp_done", 2 * (g - NPR + 1))
                        r = rr[parity]
                        kc = TT * H + h
                        nc.scalar.activation(probs[:, h % NPR, 0:T], SC[h % 2][:, 0:T], ACT.Exp,
                                             scale=r[:, kc:kc + 1]).then_inc(S["exp_done"], 1)
                        nc.scalar.activation(probs[:, h % NPR, T:T + P], SC[h % 2][:, T:T + P], ACT.Exp,
                                             scale=r[:, kc + H:kc + H + 1]).then_inc(S["exp_done"], 1)
                    if N2 and h == 2:
                        b = n - 4
                        wait(act, "h2_ready", b + 1)
                        sc_wait(act, half, parity, b)
                        nc.scalar.activation(rows[1][parity][:, :, 0:M], rows[0][parity][:, :, 0:M], ACT.Copy)\
                            .then_inc(S["rows_copied"], 1)
                    if A and h % 2 == 0:
                        u = h // 2
                        wait(act, "p_done", NU * n + u + 1)
                        wait(act, "ssq_done", NU * n + u - 1)
                        wait(act, "sq_done", NU * n + u - 1)
                        nc.scalar.activation(squares[:, u % 2, :], UN[0][:, :], ACT.Square)\
                            .then_inc(S["sq_done"], 1)
                    if B and h < NU:
                        b = n - 1
                        t = h % TT
                        dst = (k_t if h < TT else q_t)[1 - parity]
                        wait(act, "tr_done", NU * b + h + 1)
                        wait(act, "s_done", H * (b - 1))
                        nc.scalar.activation(dst[:, :, t * P:(t + 1) * P],
                                             UN[1][:, :].rearrange("p (h c) -> p h c", h=H), ACT.Copy)\
                            .then_inc(S["tr_copied"], 1)
                    if B and NU <= h < NU + TT:
                        b, t = n - 1, h - NU
                        wait(act, "vw_done", TT * b + t + 1)
                        wait(act, "o_done", H * (b - 1))
                        nc.scalar.activation(vals[1 - parity][:, t, :, 0:D],
                                             UN[1][:, :].rearrange("p (h c) -> p h c", h=H), ACT.Copy,
                                             scale=1.0 / WS).then_inc(S["vals_ready"], 1)
                    if X and h == NU + TT:
                        b = n + 1
                        wait(act, "tx_done", b + 1)
                        wait(act, "h_ready", b)
                        nc.scalar.activation(h_t[:, :], UN[1][:, 0:T], ACT.Identity,
                                             scale=mod_t[:, 1, bass.ds(b, 1)],
                                             bias=mod_t[:, 0, bass.ds(b, 1)]).then_inc(S["ht32_done"], 1)
                        wait(act, "ht32_done", b + 1)
                        wait(act, "vw_done", TT * (b - 1))
                        nc.scalar.activation(h_hi[1 - parity][:, :], h_t[:, :], ACT.Copy)\
                            .then_inc(S["hhi_done"], 1)
                    if RT and h in (1, 5):
                        b = n - 5
                        src, dst, after = ((lg_m, e_lg, LESS_TOP) if h == 1 else (gap, e_gap, GAP))
                        wait(act, "route_step", STEPS * b + after)
                        nc.scalar.activation(dst[:], src[:], ACT.Exp).then_inc(S["route_exp"], 1)
                    if N2 and h == H - 1:
                        b = n - 4
                        wait(act, "h2t_done", b + 1)
                        wait(act, "rt_done", b)
                        nc.scalar.activation(h2_t[:, :], UN[1][:, 0:T], ACT.Copy).then_inc(S["h2t_copied"], 1)
            iterations(act, body)

        @block.vector
        def _(dve):
            dve.wait_ge(S["ct_done"], 1)
            nc.vector.tensor_copy(silu_ct[:, :], OP[0][:, 0:NB]).then_inc(S["ct_ready"], 1)
            dve.wait_ge(S["mod_done"], 1)
            nc.vector.tensor_copy(mod_t[:, 0, :], SC[0][:, 0:NB]).then_inc(S["mod_copied"], 1)
            nc.vector.tensor_scalar(mod_t[:, 1, :], SC[0][:, NB:2 * NB], 1.0, None, ALU.add).then_inc(S["mod_copied"], 1)
            nc.vector.tensor_copy(mod_rows[:, :], SC[1][0:NB, :]).then_inc(S["mod_copied"], 1)
            dve.wait_ge(S["mod_copied"], 3)
            gates = mod_rows[:, :].rearrange("b (j m) -> b j m", j=4)[:, 0:4:3, :]
            ga3 = guard_a[:, :].rearrange("b (j m) -> b j m", j=2)
            gb3 = guard_b[:, :].rearrange("b (j m) -> b j m", j=2)
            nc.vector.tensor_scalar(ga3, gates, 0.0, 2.0, ALU.is_ge, ALU.mult).then_inc(S["guard_done"], 1)
            nc.vector.scalar_tensor_tensor(out=gb3, in0=gates, scalar=-1.0, in1=gates, op0=ALU.mult, op1=ALU.max)\
                .then_inc(S["guard_done"], 1)
            nc.vector.tensor_scalar(mod_rows[:, 2 * M:3 * M], mod_rows[:, 2 * M:3 * M], 1.0, None, ALU.add)\
                .then_inc(S["guard_done"], 1)
            dve.wait_ge(S["guard_done"], 3)
            nc.vector.tensor_scalar(ga3, ga3, 1.0, None, ALU.subtract).then_inc(S["guard_done"], 1)
            dve.wait_ge(S["guard_done"], 4)
            nc.vector.scalar_tensor_tensor(out=gates, in0=gb3, scalar=0.25, in1=ga3, op0=ALU.max, op1=ALU.mult)\
                .then_inc(S["guard_done"], 1)
            dve.wait_ge(S["hi_done"], 2)
            for k in range(2):
                nc.vector.scalar_tensor_tensor(out=wqk_lo[:, k * HD:(k + 1) * HD], in0=roped[0][:, k, :], scalar=WS,
                                               in1=wqk_hi[:, k * HD:(k + 1) * HD], op0=ALU.mult, op1=ALU.subtract)\
                    .then_inc(S["split_done"], 1)
            dve.wait_ge(S["wvo_hi_done"], 1)
            nc.vector.tensor_tensor(out=wvo_lo[:, :], in0=roped[1][:, 1, :], in1=wvo_hi[:, :], op=ALU.subtract)\
                .then_inc(S["split_done"], 1)
            dve.wait_ge(S["ones_ready"], 8)
            dve.wait_ge(S["const_in"], 32)
            dve.wait_ge(S["split_done"], 3)
            dve.wait_ge(S["iota_done"], 11)
            dve.wait_ge(S["router_in"], 32)

            FIRST_PART = {0: (TOP_L0, TOP_L1), 1: (E_SUM,), 2: (SCORE,), 3: (TOP_I0, TOP_I1), 4: (ONE_HOT,),
                          5: (COUNT_A,), 6: (W_DEN,), 7: (W_SECOND, TO_0)}
            LAST_PART = {0: (LESS_TOP,), 1: (E_REC,), 2: (TOP_S0, TOP_S1), 3: (TOP_F, GAP), 4: (CHOSEN,),
                         5: (COUNT_B,), 6: (W_FIRST,), 7: (TO_1, PLACE_E)}
            CH = 14

            def body(half, parity, live):
                n = 2 * half + parity
                L, X, A, _, C, R, N2, RT = live
                other = 1 - parity
                chain = X or A or live[3] or C or R or N2
                if chain:
                    base = CH * (n + 1)
                    r = rr[other]
                    wait(dve, "ssq_done", cap(NU * n, NU * NB))
                    wait(dve, "mv2_done", TT * (n - 3))
                    wait(dve, "mv_done", cap(TT * (n + 2), TT * NB))
                    wait(dve, "chain_done", base)
                    s = WS * WS * RMS_EPS
                    nc.vector.tensor_scalar(vx[:, 0:TT * H], ssq[other][:, 0:TT * H], 1.0 / D, s, ALU.mult, ALU.add)\
                        .then_inc(S["chain_done"], 1)
                    nc.vector.tensor_scalar(vx[:, TT * H:NU * H], ssq[other][:, TT * H:NU * H], float(D), s * D * D,
                                            ALU.mult, ALU.add).then_inc(S["chain_done"], 1)
                    for k, m in ((0, mv[other]), (1, mv2[parity])):
                        c0 = NU * H + k * TT
                        nc.vector.tensor_scalar(vx[:, c0:c0 + TT], m[:, :, 1:2].rearrange("p t o -> p (t o)"),
                                                LN_EPS, None, ALU.add).then_inc(S["chain_done"], 1)
                if R:
                    b = n - 3
                    wait(dve, "acc_done", H * TT * (b + 1))
                    hb = half + (parity - 3) // 2
                    dve.wait_ge(S[f"ga_in{other}"], 16 * (hb + 1))
                    nc.vector.tensor_tensor(
                        out=acc[:, :, :], in0=acc[:, :, :],
                        in1=ga_b[other][:, :].rearrange("p (o m) -> p o m", o=1).to_broadcast([P, TT, M]),
                        op=ALU.mult).then_inc(S["x2_done"], 1)
                if chain:
                    wait(dve, "chain_done", base + 4)
                    nc.vector.tensor_scalar(half_bits[:, :], vx[:, :].bitcast(I32), 1, None, ALU.logical_shift_right)\
                        .then_inc(S["chain_done"], 1)
                if R:
                    xs = x_all[:, bass.ds(TT * b, TT), :]
                    wait(dve, "x2_done", 2 * b + 1)
                    nc.vector.tensor_tensor(out=xs, in0=xs, in1=acc[:, :, :], op=ALU.add).then_inc(S["x2_done"], 1)
                if chain:
                    wait(dve, "chain_done", base + 5)
                    nc.vector.tensor_scalar(y_a[:, :].bitcast(I32), half_bits[:, :], -1.0, float(MAGIC), ALU.mult,
                                            ALU.add).then_inc(S["chain_done"], 1)
                    for k in range(3):
                        if L and k < TT:
                            b = n + 2
                            if k == 0:
                                alone(dve, f"x_in{parity}", 16 * (half + 2))
                                wait(dve, "mv_done", TT * b)
                            nc.vector.bn_stats(bst[:, k, :], x_all[:, bass.ds(TT * b + k, 1), :]
                                               .rearrange("p o m -> p (o m)")).then_inc(S["stat_done"], 1)
                        wait(dve, "chain_done", base + 6 + 3 * k)
                        nc.vector.scalar_tensor_tensor(out=y_t[:, :], in0=y_a[:, :], scalar=-0.5, in1=y_a[:, :],
                                                       op0=ALU.mult, op1=ALU.mult).then_inc(S["chain_done"], 1)
                        if L and k < TT:
                            alone(dve, "stat_done", TT * (n + 2) + k + 1)
                            nc.vector.bn_aggr(mv[parity][:, k, :], bst[:, k, :]).then_inc(S["mv_done"], 1)
                        wait(dve, "chain_done", base + 7 + 3 * k)
                        nc.vector.tensor_tensor(out=y_t[:, :], in0=y_t[:, :], in1=vx[:, :], op=ALU.mult)\
                            .then_inc(S["chain_done"], 1)
                        wait(dve, "chain_done", base + 8 + 3 * k)
                        if k == 2:
                            wait(dve, "exp_done", cap(2 * H * (n - 2), 2 * H * NB))
                        dst = r if k == 2 else y_a
                        ins = nc.vector.scalar_tensor_tensor(out=dst[:, :], in0=y_t[:, :], scalar=1.5, in1=y_a[:, :],
                                                             op0=ALU.add, op1=ALU.mult)
                        ins.then_inc(S["rr_done" if k == 2 else "chain_done"], 1)
                elif L:
                    b = n + 2
                    dve.wait_ge(S[f"x_in{parity}"], 16 * (half + 2))
                    for k in range(TT):
                        nc.vector.bn_stats(bst[:, k, :], x_all[:, TT * b + k, :]).then_inc(S["stat_done"], 1)
                    for k in range(TT):
                        wait(dve, "stat_done", TT * b + k + 1)
                        nc.vector.bn_aggr(mv[parity][:, k, :], bst[:, k, :]).then_inc(S["mv_done"], 1)
                if X:
                    b = n + 1
                    wait(dve, "rr_done", b + 1)
                    wait(dve, "tx_done", b)
                    for t in range(TT):
                        nc.vector.tensor_scalar(xn[:, t, :], x_all[:, bass.ds(TT * b + t, 1), :]
                                                .rearrange("p o m -> p (o m)"), mv[other][:, t, 0:1],
                                                r[:, NU * H + t:NU * H + t + 1], ALU.subtract, ALU.mult)\
                            .then_inc(S["xn_ready"], 1)

                if N2:
                    for t in range(TT):
                        wait(dve, "rr_done", n + 2) if t == 0 else None
                        c0 = NU * H + TT + t
                        nc.vector.tensor_scalar(xn2[:, t, :], x_all[:, bass.ds(TT * (n - 4) + t, 1), :]
                                                .rearrange("p o m -> p (o m)"), mv2[parity][:, t, 0:1],
                                                r[:, c0:c0 + 1], ALU.subtract, ALU.mult).then_inc(S["xn2_done"], 1)

                def modulate(b, step):
                    row = sbcb_b[parity][:, (1 - step) * M:(2 - step) * M].rearrange("p (o m) -> p o m", o=1)\
                        .to_broadcast([P, TT, M])
                    if step == 0:
                        wait(dve, "xn2_done", 3 * b + 2)
                        dve.wait_ge(S[f"sbcb_in{parity}"], 16 * (half - 1))
                        nc.vector.tensor_tensor(out=xn2[:, :, :], in0=xn2[:, :, :], in1=row, op=ALU.mult)\
                            .then_inc(S["xn2_done"], 1)
                    else:
                        wait(dve, "xn2_done", 3 * b + 3)
                        sc_wait(dve, half, parity, b)
                        nc.vector.tensor_tensor(out=rows[0][parity][:, :, 0:M], in0=xn2[:, :, :], in1=row,
                                                op=ALU.add).then_inc(S["h2_ready"], 1)

                def route(b, step):
                    at = STEPS * b

                    def after(k):
                        own = alone if step in (TOP_S0, TOP_S1, TOP_I0, TOP_I1) else wait
                        own(dve, "route_step", at + k)

                    def each_t(v):
                        return v.rearrange("p (t o) -> p t o", o=1)
                    if step in (TOP_L0, TOP_L1):
                        t = step - TOP_L0
                        if t == 0:
                            alone(dve, "lg_ready", b + 1)
                        ins = nc.vector.max(top_l[:, t, :], lg[other][:, t, :])
                    elif step == LESS_TOP:
                        after(TOP_L1)
                        wait(dve, "route_exp", 2 * b)
                        ins = nc.vector.tensor_tensor(out=lg_m[:, :, :], in0=lg[other][:, :, :],
                                                      in1=top_l[:, :, 0:1].to_broadcast([P, TT, E]), op=ALU.subtract)
                    elif step == E_SUM:
                        wait(dve, "route_exp", 2 * b + 1)
                        ins = nc.vector.tensor_reduce(out=e_sum[:, :], in_=e_lg[:, :, :], op=ALU.add, axis=AX.X)
                    elif step == E_REC:
                        after(E_SUM)
                        ins = nc.vector.reciprocal(e_rec[:, :], e_sum[:, :])
                    elif step == SCORE:
                        after(E_REC)
                        ins = nc.vector.tensor_tensor(out=score[:, :, :], in0=e_lg[:, :, :],
                                                      in1=each_t(e_rec[:, :]).to_broadcast([P, TT, E]), op=ALU.mult)
                    elif step in (TOP_S0, TOP_S1):
                        t = step - TOP_S0
                        after(SCORE)
                        ins = nc.vector.max(top_s[:, t, :], score[:, t, :])
                    elif step in (TOP_I0, TOP_I1):
                        t = step - TOP_I0
                        after(TOP_S0 + t)
                        ins = nc.vector.max_index(top_i[:, t, :], top_s[:, t, :], score[:, t, :])
                    elif step == TOP_F:
                        after(TOP_I1)
                        ins = nc.vector.tensor_copy(top_f[:, :, :], top_i[:, :, 0:K])
                    elif step == GAP:
                        after(TOP_S1)
                        ins = nc.vector.tensor_tensor(out=each_t(gap[:, :]), in0=top_s[:, :, 1:2],
                                                      in1=top_s[:, :, 0:1], op=ALU.subtract)
                    elif step == ONE_HOT:
                        after(TOP_F)
                        ins = nc.vector.tensor_tensor(
                            out=one_hot[:, :, :],
                            in0=iota_e[:, :].rearrange("p (o e) -> p o e", o=1).to_broadcast([P, TT * K, E]),
                            in1=top_f[:, :, :].rearrange("p t (j o) -> p (t j) o", o=1)
                                .to_broadcast([P, TT * K, E]), op=ALU.is_equal)
                    elif step == CHOSEN:
                        after(ONE_HOT)
                        wait(dve, "px_done", b)
                        oh = one_hot[:, :, :].rearrange("p (t j) e -> p t j e", j=K)
                        ins = nc.vector.tensor_tensor(out=chosen[:, :, :], in0=oh[:, :, 0, :], in1=oh[:, :, 1, :],
                                                      op=ALU.add)
                    elif step == COUNT_A:
                        after(CHOSEN)
                        ins = nc.vector.tensor_tensor(out=counts[parity][:, :], in0=counts[other][:, :],
                                                      in1=chosen[:, 0, :], op=ALU.add)
                    elif step == COUNT_B:
                        after(COUNT_A)
                        ins = nc.vector.tensor_tensor(out=counts[parity][:, :], in0=counts[parity][:, :],
                                                      in1=chosen[:, 1, :], op=ALU.add)
                    elif step == W_DEN:
                        wait(dve, "route_exp", 2 * b + 2)
                        ins = nc.vector.tensor_scalar(w_den[:, :], e_gap[:, :], 1.0, None, ALU.add)
                    elif step == W_FIRST:
                        after(W_DEN)
                        ins = nc.vector.reciprocal(weights[:, bass.ds(TT * b, TT), 0:1], each_t(w_den[:, :]))
                    elif step == W_SECOND:
                        after(W_FIRST)
                        ins = nc.vector.tensor_tensor(out=weights[:, bass.ds(TT * b, TT), 1:2],
                                                      in0=weights[:, bass.ds(TT * b, TT), 0:1],
                                                      in1=each_t(e_gap[:, :]), op=ALU.mult)
                    elif step in (TO_0, TO_1):
                        j = step - TO_0
                        ins = nc.vector.tensor_copy(rows[j][other][:, :, M:RW],
                                                    token_at[:, bass.ds(TT * b, TT), j:j + 1])
                    elif step == PLACE_E:
                        wait(dve, "px_done", b + 1)
                        ins = nc.vector.tensor_tensor(
                            out=place_e[:, :, :], in0=UN[1][:, 512:512 + TT * E].rearrange("p (t e) -> p t e", t=TT),
                            in1=base_e[:, :].rearrange("p (o e) -> p o e", o=1).to_broadcast([P, TT, E]), op=ALU.add)
                    elif step == PLACE_K:
                        after(PLACE_E)
                        pe3 = place_e[:, :, :].rearrange("p t (o e) -> p t o e", o=1).to_broadcast([P, TT, K, E])
                        ins = nc.vector.tensor_tensor(
                            out=place_k[:, :, :].rearrange("p (t j) e -> p t j e", j=K),
                            in0=one_hot[:, :, :].rearrange("p (t j) e -> p t j e", j=K), in1=pe3, op=ALU.mult)
                    elif step == PLACE_F:
                        after(PLACE_K)
                        ins = nc.vector.tensor_reduce(out=place_f[:, :], in_=place_k[:, :, :], op=ALU.add, axis=AX.X)
                    elif step == PLACE_I:
                        after(PLACE_F)
                        ins = nc.vector.tensor_copy(place[other][:, :], place_f[:, :])
                    ins.then_inc(S["route_step"], 1)

                def add_head(b, h):
                    g = H * b + h
                    o = OP[h % 2][:, :].rearrange("p (t c) -> p t c", t=TT)
                    wait(dve, "o_done", g + 1)
                    nc.vector.reciprocal(den[:, h % 2, :], o[:, :, D:D + 1].rearrange("p t o -> p (t o)"))\
                        .then_inc(S["den_done"], 1)
                    wait(dve, "den_done", g + 1)
                    for t in range(TT):
                        if h == 0:
                            if t == 0:
                                wait(dve, "x2_done", 2 * b)
                            ins = nc.vector.tensor_scalar(acc[:, t, :], o[:, t, 0:M], den[:, h % 2, t:t + 1], None,
                                                          ALU.mult)
                        else:
                            wait(dve, "acc_done", TT * (g - 1) + t + 1)
                            ins = nc.vector.scalar_tensor_tensor(out=acc[:, t, :], in0=o[:, t, 0:M],
                                                                 scalar=den[:, h % 2, t:t + 1], in1=acc[:, t, :],
                                                                 op0=ALU.mult, op1=ALU.add)
                        ins.then_inc(S["acc_done"], 1)

                for h in range(H):
                    u = h // 2
                    w = NU * n + u
                    if C and h >= 1:
                        add_head(n - 2, h - 1)
                    if RT:
                        for k in FIRST_PART[h]:
                            route(n - 5, k)
                    if A and h % 2 == 0:
                        t = u % TT
                        wait(dve, "sq_done", w + 1)
                        wait(dve, "tr_done", NU * (n - 1))
                        nc.vector.tensor_tensor(
                            out=roped[parity][:, u, :].rearrange("p (g c) -> p g c", c=D // 2),
                            in0=UN[0][:, :].rearrange("p (g c) -> p g c", c=D // 2),
                            in1=cos_sb[:, t:t + 1, :].to_broadcast([P, 2 * H, D // 2]),
                            op=ALU.mult).then_inc(S["ropea_done"], 1)
                    if N2 and h in (0, 1):
                        modulate(n - 4, h)
                    if A and h % 2 == 0:
                        wait(dve, "add_done", w - 1)
                        nc.vector.tensor_tensor(
                            out=rope_b[:, u % 2, :].rearrange("p (h s c) -> p h s c", h=H, s=2),
                            in0=UN[0][:, :].rearrange("p (h s c) -> p h s c", h=H, s=2)[:, :, ::-1, :],
                            in1=sin_sb[:, t, :].rearrange("p (o s c) -> p o s c", o=1, s=2)
                                .to_broadcast([P, H, 2, D // 2]),
                            op=ALU.mult).then_inc(S["rope_done"], 1)
                    if A and h % 2 == 1:
                        wait(dve, "ssq_done", w - NU)
                        nc.vector.tensor_reduce(out=ssq[parity][:, u * H:(u + 1) * H],
                                                in_=squares[:, u % 2, :].rearrange("p (h d) -> p h d", h=H),
                                                op=ALU.add, axis=AX.X).then_inc(S["ssq_done"], 1)
                    if R and h in (1, 2):
                        b = n - 3
                        for t in range(TT):
                            if h == 1:
                                alone(dve, "x2_done", 2 * b + 2)
                                nc.vector.bn_stats(bst2[:, t, :], x_all[:, bass.ds(TT * b + t, 1), :]
                                                   .rearrange("p o m -> p (o m)")).then_inc(S["stat2_done"], 1)
                            else:
                                alone(dve, "stat2_done", TT * b + t + 1)
                                nc.vector.bn_aggr(mv2[other][:, t, :], bst2[:, t, :]).then_inc(S["mv2_done"], 1)
                    if RT:
                        for k in LAST_PART[h]:
                            route(n - 5, k)
                if RT:
                    route(n - 5, PLACE_K)
                if X:
                    b = n + 1
                    wait(dve, "hhi_done", b + 1)
                    wait(dve, "vw_done", TT * (b - 1))
                    nc.vector.tensor_tensor(out=h_lo[other][:, :], in0=h_t[:, :], in1=h_hi[other][:, :],
                                            op=ALU.subtract).then_inc(S["h_ready"], 1)
                if RT:
                    route(n - 5, PLACE_F)
                if C:
                    add_head(n - 2, H - 1)
                if RT:
                    route(n - 5, PLACE_I)
                if N2:
                    b = n - 4
                    wait(dve, "rt_done", b + 1)
                    nc.vector.tensor_tensor(
                        out=lg[parity][:, :, :], in0=UN[1][:, 512:512 + TT * E].rearrange("p (t e) -> p t e", t=TT),
                        in1=br_b[:, :].rearrange("p (o e) -> p o e", o=1).to_broadcast([P, TT, E]),
                        op=ALU.add).then_inc(S["lg_ready"], 1)
            iterations(dve, body)

            dve.wait_ge(S["count_done"], 1)
            steps = [0]

            def link(ins):
                steps[0] += 1
                ins.then_inc(S["table_step"], 1)
                dve.wait_ge(S["table_step"], steps[0])
            link(nc.vector.tensor_copy(counts_i[:, :], UN[1][:, 0:E]))
            link(nc.vector.tensor_scalar(tiles_i[:, :], UN[1][:, 0:E], float(TILE - 1), None, ALU.add))
            link(nc.vector.tensor_scalar(tiles_i[:, :], tiles_i[:, :], TILE.bit_length() - 1, None,
                                         ALU.logical_shift_right))
            link(nc.vector.tensor_copy(tiles_f[:, :], tiles_i[:, :]))
            link(nc.vector.tensor_tensor_scan(out=tiles_to[:, :], data0=ones_e[:, :], data1=tiles_f[:, :],
                                              initial=0.0, op0=ALU.mult, op1=ALU.add))

            def by_tile(v):
                return v.rearrange("p (o e) -> p o e", o=1).to_broadcast([P, NTILES, E])
            link(nc.vector.tensor_tensor(out=behind[:, :, :],
                                         in0=iota_t[:, :].rearrange("p (i o) -> p i o", o=1)
                                             .to_broadcast([P, NTILES, E]),
                                         in1=by_tile(tiles_to[:, :]), op=ALU.is_ge))
            link(nc.vector.tensor_reduce(out=tile_e[:, :], in_=behind[:, :, :], op=ALU.add, axis=AX.X))
            link(nc.vector.tensor_tensor(out=behind[:, :, :], in0=behind[:, :, :], in1=by_tile(tiles_f[:, :]),
                                         op=ALU.mult))
            link(nc.vector.tensor_reduce(out=tile_r[:, :], in_=behind[:, :, :], op=ALU.add, axis=AX.X))
            link(nc.vector.tensor_tensor(out=tile_r[:, :], in0=iota_t[:, :], in1=tile_r[:, :], op=ALU.subtract))
            link(nc.vector.tensor_scalar(tile_r[:, :], tile_r[:, :], float(TILE), None, ALU.mult))
            link(nc.vector.scalar_tensor_tensor(out=table[:, 1, :], in0=tile_e[:, :], scalar=float(REGION),
                                                in1=tile_r[:, :], op0=ALU.mult, op1=ALU.add))
            link(nc.vector.tensor_scalar(table[:, 0, :], tile_e[:, :], float(E - 1), None, ALU.min))

        @block.tensor
        def _(pe):
            pe.wait_ge(S["silu_done"], 1)
            pe.wait_ge(S["consts_ready"], 6)
            nc.tensor.transpose(OP[0][:, 0:NB], silu_c[:, :], ident[0:NB, 0:NB]).then_inc(S["ct_done"], 1)
            pe.wait_ge(S["ct_ready"], 1)
            for j in range(2):
                nc.tensor.matmul(SC[0][:, j * NB:(j + 1) * NB], wmod_sb[:, j * M:(j + 1) * M], silu_ct[:, :],
                                 start=True, stop=True)
            nc.tensor.matmul(SC[1][0:NB, :], silu_ct[:, :], wmod_sb[:, 2 * M:6 * M], start=True, stop=True)\
                .then_inc(S["mod_done"], 1)
            pe.wait_ge(S["wv_in"], 32)
            for h in range(H):
                ins = nc.tensor.transpose(UN[0][:, h * P:(h + 1) * P], roped[0][:, 2, h * D:(h + 1) * D], ident[:, :])
            ins.then_inc(S["wvt_done"], 1)
            pe.wait_ge(S["wvt_ready"], 1)
            for h in range(H):
                ins = nc.tensor.matmul(UN[1][:, h * M:(h + 1) * M], roped[1][:, 0, h * M:(h + 1) * M],
                                       roped[0][:, 3, h * M:(h + 1) * M], start=True, stop=True)
            ins.then_inc(S["wvo_done"], 1)
            pe.wait_ge(S["wvo_scaled"], 1)
            pe.wait_ge(S["split_done"], 3)
            pe.wait_ge(S["ones_ready"], 8)
            pe.wait_ge(S["iota_done"], 11)
            pe.wait_ge(S["router_in"], 32)
            pe.wait_ge(S["mod_copied"], 3)

            def split_product(dst, hi, lo, w_hi, w_lo):
                for k in range(0, HD, 512):
                    for m, (a, w) in enumerate(((hi, w_hi), (hi, w_lo), (lo, w_hi))):
                        ins = nc.tensor.matmul(dst[:, k:k + 512], a, w[:, k:k + 512], start=(m == 0), stop=(m == 2))
                return ins

            def body(half, parity, live):
                n = 2 * half + parity
                _, X, A, B, C, _, N2, RT = live
                other = 1 - parity
                freed = ("lg_ready", n - 4) if not isinstance(n, int) or n > 4 else ("ht32_done", n + 1)

                def values_times_probs(b, h):
                    g = H * b + h
                    if h == 0:
                        wait(pe, "vals_ready", TT * (b + 1))
                    wait(pe, "exp_done", 2 * (g + 1))
                    wait(pe, "acc_done", TT * (g - 1))
                    o, pr, v = OP[h % 2], probs[:, h % NPR, :], vals[parity]
                    nc.tensor.matmul(o[:, 0:D + 1], pr[:, 0:P], v[:, 0, h, 0:D + 1], start=True, stop=True)
                    nc.tensor.matmul(o[:, 256:256 + D + 1], pr[:, P:2 * P], v[:, 0, h, 0:D + 1],
                                     start=True, stop=False)
                    nc.tensor.matmul(o[:, 256:256 + D + 1], pr[:, 2 * P:3 * P], v[:, 1, h, 0:D + 1],
                                     start=False, stop=True).then_inc(S["o_done"], 1)

                for h in range(H):
                    if C:
                        b = n - 2
                        g = H * b + h
                        if h == 0:
                            wait(pe, "tr_copied", NU * (b + 1))
                        wait(pe, "exp_done", 2 * (g - 1))
                        s, q, k = SC[h % 2], q_t[parity], k_t[parity]
                        nc.tensor.matmul(s[:, 0:T], k[:, h, 0:P], q[:, h, 0:T], start=True, stop=False)
                        nc.tensor.matmul(s[:, 0:P], ident_bf[:, :], causal_bf[:, :], start=False, stop=True)
                        nc.tensor.matmul(s[:, T:T + P], k[:, h, P:T], q[:, h, P:T], start=True, stop=False)
                        nc.tensor.matmul(s[:, T:T + P], ident_bf[:, :], causal_bf[:, :], start=False, stop=True)\
                            .then_inc(S["s_done"], 1)
                    if A and h % 2 == 0:
                        u = h // 2
                        t, kind = u % TT, u // TT
                        if u == 0:
                            wait(pe, "h_ready", n + 1)
                        wait(pe, "rope_done", NU * n + u)
                        toks = slice(t * P, (t + 1) * P)
                        cols = slice(kind * HD, (kind + 1) * HD)
                        split_product(UN[0], h_hi[parity][:, toks], h_lo[parity][:, toks],
                                      wqk_hi[:, cols], wqk_lo[:, cols]).then_inc(S["p_done"], 1)
                    if B and h < NU:
                        b = n - 1
                        u = (h + TT) % NU
                        wait(pe, *freed)
                        freed = ("tr_copied", NU * b + h + 1)
                        if u >= TT:
                            wait(pe, "add_done", NU * b + u + 1)
                        else:
                            wait(pe, "qs_done", TT * b + u + 1)
                        for j in range(H):
                            ins = nc.tensor.transpose(UN[1][:, j * P:(j + 1) * P],
                                                      roped[other][:, u, j * D:(j + 1) * D], ident[:, :])
                        ins.then_inc(S["tr_done"], 1)
                    if B and NU <= h < NU + TT:
                        b, t = n - 1, h - NU
                        wait(pe, *freed)
                        freed = ("vals_ready", TT * b + t + 1)
                        toks = slice(t * P, (t + 1) * P)
                        split_product(UN[1], h_hi[other][:, toks], h_lo[other][:, toks],
                                      wvo_hi[:, :], wvo_lo[:, :]).then_inc(S["vw_done"], 1)
                    if X and h == NU + TT:
                        b = n + 1
                        wait(pe, *freed)
                        freed = ("ht32_done", b + 1)
                        wait(pe, "xn_ready", TT * (b + 1))
                        for t in range(TT):
                            ins = nc.tensor.transpose(UN[1][:, t * P:(t + 1) * P], xn[:, t, :], ident[:, :])
                        ins.then_inc(S["tx_done"], 1)
                    if RT and h == NU + TT:
                        b = n - 5
                        wait(pe, "vals_ready", cap(TT * n, TT * NB))
                        wait(pe, "route_step", STEPS * b + CHOSEN)
                        for t in range(TT):
                            dst = UN[1][:, 512 + t * E:512 + (t + 1) * E]
                            nc.tensor.matmul(dst, before_bf[:, :], chosen[:, t, :], start=True, stop=False)
                            for k in range(t):
                                nc.tensor.matmul(dst, ones_bf[:, :], chosen[:, k, :], start=False, stop=False)
                            ins = nc.tensor.matmul(dst, ones_bf[:, :], counts[other][:, :], start=False, stop=True)
                        ins.then_inc(S["px_done"], 1)
                    if N2 and h == H - 1:
                        b = n - 4
                        wait(pe, *freed)
                        wait(pe, "h2_ready", b + 1)
                        for t in range(TT):
                            ins = nc.tensor.transpose(UN[1][:, t * P:(t + 1) * P], rows[0][parity][:, t, 0:M],
                                                      ident[:, :])
                        ins.then_inc(S["h2t_done"], 1)
                    if C and h >= 1:
                        values_times_probs(n - 2, h - 1)
                if C:
                    values_times_probs(n - 2, H - 1)
                if N2:
                    b = n - 4
                    wait(pe, "h2t_copied", b + 1)
                    if RT:
                        wait(pe, "route_step", STEPS * (n - 5) + PLACE_E)
                    for t in range(TT):
                        ins = nc.tensor.matmul(UN[1][:, 512 + t * E:512 + (t + 1) * E], h2_t[:, t * P:(t + 1) * P],
                                               wr_sb[:, :], start=True, stop=True)
                    ins.then_inc(S["rt_done"], 1)
            iterations(pe, body)
            wait(pe, "lg_ready", NB)
            wait(pe, "route_step", STEPS * NB)
            nc.tensor.matmul(UN[1][:, 0:E], ones_bf[:, :], counts[0][:, :], start=True, stop=True)\
                .then_inc(S["count_done"], 1)

        attention.close()

        phase[0] = experts = ExitStack()
        SLOTS = 4
        w1_hi = sb("w1_hi", [P, E * F], F16)
        w1_lo = sb("w1_lo", [P, E * F], F16)
        w1_sb = sb("w1_sb", [P, E * F])
        w2_sb = sb("w2_sb", [P, E * FC * M])
        b1_rows = sb("b1_rows", [E * FC, P])
        b1_t = sb("b1_t", [P, E * FC])
        b2_b = sb("b2_b", [P, E * M])
        tile_x = [sb(f"tile_x{k}", [P, TILE // P, RW]) for k in range(SLOTS)]
        place_y = [sb(f"place_y{k}", [P, TILE // P], I32) for k in range(SLOTS)]
        id_x = sb("id_x", [P, P])
        x_hi = [sb(f"x_hi{k}", [P, TILE], F16) for k in range(2)]
        x_lo = [sb(f"x_lo{k}", [P, TILE], F16) for k in range(2)]
        hidden = [sb(f"hidden{k}", [P, FC, TILE]) for k in range(2)]
        y_sum = sb("y_sum", [P, TILE // P, M])
        y_pos = sb("y_pos", [P, TILE // P, M])
        y_out = [sb(f"y_out{k}", [P, TILE // P, M]) for k in range(SLOTS)]
        XT = [ps(f"xt{k}", [P, 512]) for k in range(1)]
        UP = [ps(f"up{k}", [P, 1024]) for k in range(2)]
        DN = [ps(f"down{k}", [P, 512]) for k in range(2)]
        TS = TILE // P

        def tiles(e, body):
            def live(n):
                return [0 <= n + d < NTILES for d in (SLOTS - 1, 1, 0, -1)]
            rounds = (NTILES - SLOTS + 1) // SLOTS
            for n in range(1 - SLOTS, SLOTS):
                body(n // SLOTS, n % SLOTS, live(n))
            with e.Fori(1, rounds) as turn:
                for slot in range(SLOTS):
                    body(turn, slot, [True] * 4)
            for n in range(rounds * SLOTS, NTILES + 1):
                body(n // SLOTS, n % SLOTS, live(n))

        def round_of(turn, slot, d):
            return turn + (slot + d) // SLOTS, (slot + d) % SLOTS

        def entry(e, k, n, most):
            return e.value_load(table[0:1, k, bass.ds(n, 1)], min_val=0, max_val=most)

        block = experts.enter_context(nc.Block())

        @block.sync
        def _(sp):
            sp.dma_start(w1_sb[:, :].rearrange("c (e f) -> c e f", e=E), w1.rearrange("e c f -> c e f"))\
                .then_inc(S["w1_in"], 16)
            sp.dma_start(b1_rows[:, :], b1.rearrange("e (k p) -> (e k) p", p=P)).then_inc(S["b_in"], 16)
            sp.dma_start(b2_b[:, :], b2.rearrange("(o e) m -> o (e m)", o=1).broadcast_to([P, E * M]))\
                .then_inc(S["b_in"], 16)
            sp.dma_start(w2_sb[:, :].rearrange("p (g m) -> p g m", m=M), w2.rearrange("e (k p) m -> p (e k) m", p=P))\
                .then_inc(S["w2_in"], 16)

            def body(turn, slot, live):
                LOAD, _, _, _ = live
                if LOAD:
                    i = SLOTS * turn + slot + SLOTS - 1
                    before, at = round_of(turn, slot, SLOTS - 1)
                    row = entry(sp, 1, i, E * REGION + (SPARE - 1) * TILE)
                    alone(sp, "t_done", i - SLOTS + 1)
                    alone(sp, "places_ready", i - SLOTS + 1)
                    wait(sp, f"tile_in{at}", 16 * before)
                    sp.dma_start(tile_x[at][:, :, :], x_rows[bass.ds(row, TILE), :]
                                 .rearrange("(p s) c -> p s c", p=P)).then_inc(S[f"tile_in{at}"], 16)
            tiles(sp, body)

        @block.gpsimd
        def _(pool):
            pool.memset(id_x[:, :], 0.0).then_inc(S["consts_ready"], 1)
            pool.wait_ge(S["consts_ready"], 7)
            pool.affine_select(out=id_x[:, :], in_=id_x[:, :], compare_op=ALU.not_equal, fill=1.0,
                               base=0, pattern=[[-1, P]], channel_multiplier=1).then_inc(S["consts_ready"], 1)

            def body(turn, slot, live):
                _, _, _, DOWN = live
                if DOWN:
                    i = SLOTS * turn + slot - 1
                    at = (slot - 1) % SLOTS
                    alone(pool, "y_step", 3 * (i + 1))
                    for s in range(TS):
                        pool.indirect_dma_start(
                            out=y_rows, out_offset=bass.IndirectOffsetOnAxis(ap=place_y[at][:, s:s + 1], axis=0),
                            in_=y_out[at][:, s, :], in_offset=None, bounds_check=K * NTOK - 1, oob_is_err=False)\
                            .then_inc(S[f"y_stored{at}"], 16)
            tiles(pool, body)
            for k in range(SLOTS):
                pool.wait_ge(S[f"y_stored{k}"], 16 * TS * ((NTILES - k + SLOTS - 1) // SLOTS))

        @block.scalar
        def _(act):
            act.wait_ge(S["w1_in"], 16)
            for e in range(E):
                nc.scalar.activation(w1_hi[:, e * F:(e + 1) * F], w1_sb[:, e * F:(e + 1) * F], ACT.Copy, scale=WS)\
                    .then_inc(S["w1_hi_done"], 1)
            act.wait_ge(S["b1_ready"], 1)

            def body(turn, slot, live):
                n = SLOTS * turn + slot
                _, T1, UPW, _ = live
                parity, other = slot % 2, 1 - slot % 2
                if T1:
                    i = n + 1
                    wait(act, "t_done", i + 1)
                    wait(act, "up_done", FC * (i - 1))
                    nc.scalar.activation(x_hi[other][:, :], XT[0][:, 0:TILE], ACT.Copy).then_inc(S["x_hi_done"], 1)
                if UPW:
                    expert = entry(act, 0, n, E - 1)
                    for k in range(FC):
                        wait(act, "up_done", FC * n + k + 1)
                        wait(act, "down_done", n - 1)
                        nc.scalar.activation(hidden[parity][:, k, :], UP[k // 2][:, (k % 2) * 512:(k % 2) * 512 + TILE],
                                             ACT.Gelu, bias=b1_t[:, bass.ds(expert * FC + k, 1)], scale=1.0 / WS)\
                            .then_inc(S["gelu_done"], 1)
            tiles(act, body)

        @block.vector
        def _(dve):
            for e in range(E):
                dve.wait_ge(S["w1_hi_done"], e + 1)
                cols = slice(e * F, (e + 1) * F)
                nc.vector.scalar_tensor_tensor(out=w1_lo[:, cols], in0=w1_sb[:, cols], scalar=WS, in1=w1_hi[:, cols],
                                               op0=ALU.mult, op1=ALU.subtract).then_inc(S["w1_split"], 1)
            dve.wait_ge(S["b_in"], 32)
            dve.wait_ge(S["b1_turned"], 1)
            nc.vector.tensor_copy(b1_t[:, :], XT[0][:, 0:E * FC]).then_inc(S["b1_ready"], 1)

            def body(turn, slot, live):
                n = SLOTS * turn + slot
                _, T1, _, DOWN = live
                parity, other = slot % 2, 1 - slot % 2
                if T1:
                    i = n + 1
                    wait(dve, "x_hi_done", i + 1)
                    wait(dve, "up_done", FC * (i - 1))
                    nc.vector.tensor_tensor(out=x_lo[other][:, :], in0=XT[0][:, 0:TILE], in1=x_hi[other][:, :],
                                            op=ALU.subtract).then_inc(S["x_split"], 1)
                    before, at = round_of(turn, slot, 1)
                    wait(dve, f"y_stored{at}", 16 * TS * before)
                    nc.vector.tensor_copy(place_y[at][:, :], tile_x[at][:, :, M:RW]
                                          .rearrange("p s o -> p (s o)")).then_inc(S["places_ready"], 1)
                if DOWN:
                    i = n - 1
                    at = (slot - 1) % SLOTS
                    expert = entry(dve, 0, i, E - 1)
                    wait(dve, "down_done", i + 1)
                    wait(dve, "y_step", 3 * i)
                    nc.vector.tensor_tensor(
                        out=y_sum[:, :, :], in0=DN[other][:, 0:TILE].rearrange("p (s m) -> p s m", s=TS),
                        in1=b2_b[:, bass.ds(expert * M, M)].rearrange("p (o m) -> p o m", o=1)
                            .to_broadcast([P, TS, M]), op=ALU.add).then_inc(S["y_step"], 1)
                    wait(dve, "y_step", 3 * i + 1)
                    nc.vector.tensor_scalar(y_pos[:, :, :], y_sum[:, :, :], 0.0, None, ALU.max)\
                        .then_inc(S["y_step"], 1)
                    wait(dve, "y_step", 3 * i + 2)
                    nc.vector.scalar_tensor_tensor(out=y_out[at][:, :, :], in0=y_sum[:, :, :], scalar=0.0,
                                                   in1=y_pos[:, :, :], op0=ALU.min, op1=ALU.add)\
                        .then_inc(S["y_step"], 1)
            tiles(dve, body)

        @block.tensor
        def _(pe):
            pe.wait_ge(S["w1_split"], E)
            pe.wait_ge(S["w2_in"], 16)
            pe.wait_ge(S["consts_ready"], 8)
            pe.wait_ge(S["b_in"], 32)
            nc.tensor.transpose(XT[0][:, 0:E * FC], b1_rows[:, :], id_x[0:E * FC, 0:E * FC])\
                .then_inc(S["b1_turned"], 1)
            pe.wait_ge(S["b1_ready"], 1)

            def body(turn, slot, live):
                n = SLOTS * turn + slot
                _, T1, UPW, DOWN = live
                parity, other = slot % 2, 1 - slot % 2
                if T1:
                    i = n + 1
                    before, at = round_of(turn, slot, 1)
                    wait(pe, f"tile_in{at}", 16 * (before + 1))
                    wait(pe, "x_split", i)
                    for s in range(TS):
                        ins = nc.tensor.transpose(XT[0][:, s * P:(s + 1) * P], tile_x[at][:, s, 0:M], id_x[:, :])
                    ins.then_inc(S["t_done"], 1)
                if UPW:
                    expert = entry(pe, 0, n, E - 1)
                    wait(pe, "x_split", n + 1)
                    for k in range(FC):
                        wait(pe, "gelu_done", FC * (n - 1) + k + 1)
                        dst = UP[k // 2][:, (k % 2) * 512:(k % 2) * 512 + TILE]
                        cols = bass.ds(expert * F + k * P, P)
                        nc.tensor.matmul(dst, w1_hi[:, cols], x_hi[parity][:, :], start=True, stop=False)
                        nc.tensor.matmul(dst, w1_hi[:, cols], x_lo[parity][:, :], start=False, stop=False)
                        nc.tensor.matmul(dst, w1_lo[:, cols], x_hi[parity][:, :], start=False, stop=True)\
                            .then_inc(S["up_done"], 1)
                if DOWN:
                    i = n - 1
                    expert = entry(pe, 0, i, E - 1)
                    wait(pe, "y_step", 3 * (i - 2) + 1)
                    for s in range(TS):
                        for k in range(FC):
                            wait(pe, "gelu_done", FC * i + k + 1)
                            ins = nc.tensor.matmul(DN[other][:, s * M:(s + 1) * M],
                                                   hidden[other][:, k, s * P:(s + 1) * P],
                                                   w2_sb[:, bass.ds((expert * FC + k) * M, M)],
                                                   start=(k == 0), stop=(k == FC - 1))
                    ins.then_inc(S["down_done"], 1)
            tiles(pe, body)

        experts.close()

        phase[0] = last = ExitStack()
        back = [[sb(f"back{j}{k}", [P, TT, M]) for k in range(2)] for j in range(K)]
        gb_b = [sb(f"gb_b{k}", [P, M]) for k in range(2)]
        part = sb("part", [P, TT, M])
        mixed = sb("mixed", [P, TT, M])
        sums = [sb(f"sums{k}", [P, TT, M]) for k in range(2)]
        block = last.enter_context(nc.Block())
        MIX = 2 * TT + 2

        def batches(e, body):
            for n in range(2):
                body(0, n)
            with e.Fori(1, NB // 2) as half:
                for parity in range(2):
                    body(half, parity)

        @block.sync
        def _(sp):
            yv = y_rows.rearrange("(j g p) m -> j p g m", j=K, p=P)

            def body(half, parity):
                n = 2 * half + parity
                alone(sp, "mix_done", MIX * (n - 1))
                wait(sp, f"back_in{parity}", 16 * (K + 1) * half)
                for j in range(K):
                    sp.dma_start(back[j][parity][:, :, :], yv[j, :, bass.ds(n * TT, TT), :])\
                        .then_inc(S[f"back_in{parity}"], 16)
                sp.dma_start(gb_b[parity][:, :], mod_dram[bass.ds(n, 1), 3 * M:4 * M].broadcast_to([P, M]))\
                    .then_inc(S[f"back_in{parity}"], 16)
            batches(sp, body)

        @block.vector
        def _(dve):
            def body(half, parity):
                n = 2 * half + parity
                at = MIX * n
                dve.wait_ge(S[f"back_in{parity}"], 16 * (K + 1) * (half + 1))
                for t in range(TT):
                    w = weights[:, bass.ds(TT * n + t, 1), :].rearrange("p o k -> p (o k)")
                    nc.vector.tensor_scalar(part[:, t, :], back[0][parity][:, t, :], w[:, 0:1], None, ALU.mult)\
                        .then_inc(S["mix_done"], 1)
                for t in range(TT):
                    w = weights[:, bass.ds(TT * n + t, 1), :].rearrange("p o k -> p (o k)")
                    wait(dve, "mix_done", at + t + 1)
                    nc.vector.scalar_tensor_tensor(out=mixed[:, t, :], in0=back[1][parity][:, t, :], scalar=w[:, 1:2],
                                                   in1=part[:, t, :], op0=ALU.mult, op1=ALU.add)\
                        .then_inc(S["mix_done"], 1)
                wait(dve, "mix_done", at + 2 * TT)
                nc.vector.tensor_tensor(out=mixed[:, :, :], in0=mixed[:, :, :],
                                        in1=gb_b[parity][:, :].rearrange("p (o m) -> p o m", o=1)
                                            .to_broadcast([P, TT, M]), op=ALU.mult).then_inc(S["mix_done"], 1)
                wait(dve, "mix_done", at + 2 * TT + 1)
                wait(dve, f"out_stored{parity}", 16 * half)
                nc.vector.tensor_tensor(out=sums[parity][:, :, :], in0=mixed[:, :, :],
                                        in1=x_all[:, bass.ds(TT * n, TT), :], op=ALU.add).then_inc(S["mix_done"], 1)
            batches(dve, body)

        @block.scalar
        def _(act):
            ov = out.rearrange("b (t p) m -> p (b t) m", p=P)

            def body(half, parity):
                n = 2 * half + parity
                wait(act, "mix_done", MIX * (n + 1))
                act.dma_start(ov[:, bass.ds(TT * n, TT), :], sums[parity][:, :, :])\
                    .then_inc(S[f"out_stored{parity}"], 16)
            batches(act, body)
            for k in range(2):
                act.wait_ge(S[f"out_stored{k}"], 16 * NB // 2)
        last.close()


_INS = ["L0_attn_x", "L0_attn_wq", "L0_attn_wk", "L0_attn_wv", "L0_attn_wo", "L0_ffn_Wr", "L0_ffn_br",
        "L0_ffn_W1", "L0_ffn_b1", "L0_ffn_W2", "L0_ffn_b2", "L0_c", "L0_wmod"]


def rope_tables(length, width, base=1250.0):
    half = width // 2
    pos = np.arange(length, dtype=np.float32)[:, None]
    freqs = np.power(np.float32(base), -np.arange(half, dtype=np.float32) / np.float32(half)).astype(np.float32)
    rad = (pos * freqs[None, :]).astype(np.float32)
    cos, sin = np.cos(rad).astype(np.float32), np.sin(rad).astype(np.float32)
    return cos, np.concatenate([-sin, sin], axis=1)


def kernel(**inputs):
    import concourse.bacc as bacc
    from concourse.bass_utils import run_bass_kernel_spmd

    nc = bacc.Bacc("TRN2", target_bir_lowering=False, num_devices=1)
    arrays, args = {}, []
    given = [(name, np.ascontiguousarray(inputs[name])) for name in _INS]
    cos, sin = rope_tables(given[0][1].shape[1], given[1][1].shape[2])
    for name, a in [*given, ("rope_cos", cos), ("rope_sin", sin)]:
        arrays[f"in_{name}"] = a
        args.append(nc.dram_tensor(f"in_{name}", a.shape, mybir.dt.from_np(a.dtype), kind="ExternalInput").ap())
    args.append(nc.dram_tensor("out_x", given[0][1].shape, F32, kind="ExternalOutput").ap())
    adaln_block(nc, *args)
    r = run_bass_kernel_spmd(nc, [arrays], core_ids=[0])
    return r.results[0]["out_x"]
```

```python
import math
from contextlib import ExitStack

import numpy as np

import concourse.bass as bass
from concourse import mybir

F32 = mybir.dt.float32
F16 = mybir.dt.float16
BF16 = mybir.dt.bfloat16
I32 = mybir.dt.int32
U32 = mybir.dt.uint32
ALU = mybir.AluOpType
ACT = mybir.ActivationFunctionType
AX = mybir.AxisListType


def adaln_block(nc, x, wq, wk, wv, wo, wr, br, w1, b1, w2, b2, c, wmod, rope_cos, rope_sin, out,
                debug=None, stop_after=None):
    NB, T, M = x.shape
    H, D = wq.shape[1], wq.shape[2]
    P = 128
    TT = T // P
    HD = H * D
    NU = 2 * TT
    LN_EPS, RMS_EPS = 1e-5, 1e-6
    WS = 64.0
    MASKED = -1e30
    MAGIC = 0x5F3759DF
    NCH = NU * H + 2 * TT
    E = wr.shape[1]
    K = 2
    F = w1.shape[2]
    FC = F // P
    NTOK = NB * T
    NTT = NB * TT
    TILE = 2 * P
    NTILES = (K * NTOK + E * (TILE - 1)) // TILE
    SPARE = NTILES - K * NTOK // TILE
    REGION = NTOK + TILE
    RW = M + 1
    SKIP = float(1 << 20)

    ctx = ExitStack()
    with ctx:
        phase = [ctx]

        def sb(name, shape, dt=F32):
            return phase[0].enter_context(nc.sbuf_tensor(name, shape, dt))

        def ps(name, shape, dt=F32):
            return phase[0].enter_context(nc.psum_tensor(name, shape, dt))

        def sem(name):
            return ctx.enter_context(nc.semaphore(name))

        x_all = sb("x_all", [P, NB * TT, M])
        weights = sb("weights", [P, NTT, K])
        token_at = sb("token_at", [P, NTT, K])
        table = sb("table", [P, 2, NTILES], I32)
        counts_i = sb("counts_i", [P, E], I32)
        x_rows = nc.dram_tensor("x_rows", [(E * REGION + SPARE * TILE), RW], F32).ap()
        y_rows = nc.dram_tensor("y_rows", [K * NTOK, M], F32).ap()
        mod_dram = nc.dram_tensor("mod_dram", [NB, 4 * M], F32).ap()

        phase[0] = attention = ExitStack()
        wqk_hi = sb("wqk_hi", [P, 2 * HD], F16)
        wqk_lo = sb("wqk_lo", [P, 2 * HD], F16)
        wvo_hi = sb("wvo_hi", [P, HD], F16)
        wvo_lo = sb("wvo_lo", [P, HD], F16)
        ident = sb("ident", [P, P])
        ident_bf = sb("ident_bf", [P, P], BF16)
        causal_bf = sb("causal_bf", [P, P], BF16)
        cos_sb = sb("cos_sb", [P, TT, D // 2])
        sin_sb = sb("sin_sb", [P, TT, D])
        mod_t = sb("mod_t", [P, 2, NB])
        mod_rows = sb("mod_rows", [NB, 4 * M])
        silu_c = sb("silu_c", [NB, M])
        c_sb = sb("c_sb", [NB, M])
        silu_ct = sb("silu_ct", [P, NB])
        wmod_sb = sb("wmod_sb", [P, 6 * M])
        guard_a = sb("guard_a", [NB, 2 * M])
        guard_b = sb("guard_b", [NB, 2 * M])
        roped = [sb(f"roped{k}", [P, NU, HD]) for k in range(2)]
        rope_b = sb("rope_b", [P, 2, HD])
        squares = sb("squares", [P, HD])
        q_t = [sb(f"q_t{k}", [P, H, T]) for k in range(2)]
        k_t = [sb(f"k_t{k}", [P, H, T]) for k in range(2)]
        VW = D + 2
        vals = [sb(f"vals{k}", [P, TT, H, VW]) for k in range(2)]
        NPR = 4
        probs = sb("probs", [P, NPR, T + P])
        h_t = sb("h_t", [P, T])
        h_hi = [sb(f"h_hi{k}", [P, T], F16) for k in range(2)]
        h_lo = [sb(f"h_lo{k}", [P, T], F16) for k in range(2)]
        xn = sb("xn", [P, TT, M])
        acc = sb("acc", [P, TT, M])
        den = sb("den", [P, 2, TT])
        ssq = [sb(f"ssq{k}", [P, NU * H]) for k in range(2)]
        bst = sb("bst", [P, TT, 6])
        mv = [sb(f"mv{k}", [P, TT, 2]) for k in range(2)]
        vx = sb("vx", [P, NCH])
        half_bits = sb("half_bits", [P, NCH], I32)
        y_a = sb("y_a", [P, NCH])
        y_t = sb("y_t", [P, NCH])
        rr = [sb(f"rr{k}", [P, NCH]) for k in range(2)]
        ga_b = [sb(f"ga_b{k}", [P, M]) for k in range(2)]
        sbcb_b = [sb(f"sbcb_b{k}", [P, 2 * M]) for k in range(2)]
        mv2 = [sb(f"mv2{k}", [P, TT, 2]) for k in range(2)]
        bst2 = sb("bst2", [P, TT, 6])
        xn2 = sb("xn2", [P, TT, M])
        rows = [[sb(f"rows{j}{k}", [P, TT, RW]) for k in range(2)] for j in range(K)]
        h2_t = sb("h2_t", [P, T])
        wr_sb = sb("wr_sb", [P, E])
        br_sb = sb("br_sb", [1, E])
        ones_row = sb("ones_row", [1, P])
        ahead = sb("ahead", [P, TT * E])
        lg = [sb(f"lg{k}", [P, TT, E]) for k in range(2)]
        top_l = sb("top_l", [P, TT, 8])
        lg_m = sb("lg_m", [P, TT, E])
        e_lg = sb("e_lg", [P, TT, E])
        e_sum = sb("e_sum", [P, TT])
        e_rec = sb("e_rec", [P, TT])
        score = sb("score", [P, TT, E])
        top_s = sb("top_s", [P, TT, 8])
        top_i = sb("top_i", [P, TT, 8], U32)
        top_f = sb("top_f", [P, TT, K])
        gap = sb("gap", [P, TT])
        e_gap = sb("e_gap", [P, TT])
        w_den = sb("w_den", [P, TT])
        iota_e = sb("iota_e", [P, E])
        base_e = sb("base_e", [P, E])
        one_hot = sb("one_hot", [P, TT * K, E])
        chosen = sb("chosen", [P, TT, E], BF16)
        counts = [sb(f"counts{k}", [P, E], BF16) for k in range(2)]
        before_bf = sb("before_bf", [P, P], BF16)
        ones_bf = sb("ones_bf", [P, P], BF16)
        place_e = sb("place_e", [P, TT, E])
        place_k = sb("place_k", [P, TT * K, E])
        place_f = sb("place_f", [P, TT * K])
        place = [sb(f"place{k}", [P, TT * K], I32) for k in range(2)]
        ones_e = sb("ones_e", [P, E])
        iota_t = sb("iota_t", [P, NTILES])
        tiles_i = sb("tiles_i", [P, E], I32)
        tiles_f = sb("tiles_f", [P, E])
        tiles_to = sb("tiles_to", [P, E])
        behind = squares[:, 0:NTILES * E].rearrange("p (i e) -> p i e", e=E)
        tile_e = sb("tile_e", [P, NTILES])
        tile_r = sb("tile_r", [P, NTILES])
        filler = sb("filler", [P, TILE // P, RW])
        UN = [ps(f"unit{k}", [P, 2 * 512]) for k in range(2)]
        SC = [ps(f"scores{k}", [P, 512]) for k in range(2)]
        OP = [ps(f"pv{k}", [P, 512]) for k in range(2)]

        names = """w_in c_in wv_in const_in x_in0 x_in1 ga_in0 ga_in1 consts_ready ones_ready silu_done ct_done
            ct_ready mod_done mod_copied guard_done mod_stored wvt_done wvt_ready wvo_done wvo_ready
            hi_done split_done wvo_scaled wvo_hi_done
            tx_done p_done tr_done vw_done s_done o_done
            ht32_done hhi_done h_ready sq_done ssq_done ropea_done rope_done add_done qs_done
            tr_copied vals_ready exp_done den_done acc_done x2_done stat_done mv_done chain_done rr_done xn_ready
            out_done router_in sbcb_in0 sbcb_in1 iota_done scattered0 scattered1 filled
            mv2_done stat2_done xn2_done h2_ready rows_copied h2t_done h2t_copied rt_done lg_ready
            route_step route_exp px_done count_done table_step ahead_copied tail_filled
            b1_turned b1_ready w1_in w2_in w1_hi_done w1_split b_in tile_in0 tile_in1 tile_in2 tile_in3 places_ready t_done x_hi_done x_split up_done gelu_done down_done
            y_step y_stored0 y_stored1 y_stored2 y_stored3
            back_in0 back_in1 part_done mix_done out_stored0 out_stored1""".split()
        S = {n: sem(n) for n in names}

        def wait(e, name, value):
            if isinstance(value, int) and value <= 0:
                return
            e.wait_ge(S[name], value)

        counted = {}

        def alone(e, name, value):
            if isinstance(value, int):
                wait(e, name, value)
            else:
                if e not in counted:
                    counted[e] = e.alloc_register("awaited")
                e.reg_mov(counted[e], value)
                e.wait_ge(S["consts_ready"], 1)
                e.wait_ge(S[name], counted[e])

        def iterations(e, body):
            def live(n):
                return [0 <= n + d < NB for d in (2, 1, 0, -1, -2, -3, -4, -5, -6)]
            for n in range(-2, 6):
                body(n // 2, n % 2, live(n))
            with e.Fori(3, NB // 2 - 1) as half:
                for parity in range(2):
                    body(half, parity, [True] * 9)
            for n in range(NB - 2, NB + 6):
                body(n // 2, n % 2, live(n))

        (TOP_L0, TOP_L1, LESS_TOP, E_SUM, E_REC, SCORE, TOP_S0, TOP_S1, TOP_I0, TOP_I1, TOP_F, GAP, ONE_HOT, CHOSEN,
         COUNT_A, COUNT_B, W_DEN, W_FIRST, W_SECOND, TO_0, TO_1, PLACE_E, PLACE_K, PLACE_F, PLACE_I) = range(1, 26)
        STEPS = PLACE_I

        (VX_Q, VX_K, VX_X, VX_H, HALF_BITS, GUESS) = range(1, 7)
        CH = GUESS + 9
        TURNED = {0: 2, 1: 3, 5: 0, 6: 1}
        VALUES = {2: 0, 3: 1}
        H_AT, Q_AT, H2_AT = 4, 5, 7
        BESIDE = 3 * P
        HH = H // 2

        def sc_wait(e, half, parity, b):
            if not isinstance(b, int) or b >= 2:
                e.wait_ge(S[f"scattered{parity}"], 16 * TT * K * (half - 2))

        def cap(v, most):
            return min(v, most) if isinstance(v, int) else v

        block = attention.enter_context(nc.Block())

        @block.sync
        def _(sp):
            sp.dma_start(c_sb[:, :], c).then_inc(S["c_in"], 16)
            sp.dma_start(wmod_sb[:, :], wmod).then_inc(S["c_in"], 16)
            sp.dma_start(x_all[:, 0:TT, :], x[0].rearrange("(t p) m -> p t m", p=P)).then_inc(S["x_in0"], 16)
            sp.dma_start(x_all[:, TT:2 * TT, :], x[1].rearrange("(t p) m -> p t m", p=P)).then_inc(S["x_in1"], 16)
            sp.dma_start(roped[0][:, 2, :], wv.rearrange("m h d -> m (h d)")).then_inc(S["wv_in"], 16)
            sp.dma_start(roped[0][:, 3, :].rearrange("p (h m) -> p h m", h=H),
                         wo.rearrange("h d m -> d h m")).then_inc(S["wv_in"], 16)
            sp.dma_start(roped[0][:, 0, :], wq.rearrange("m h d -> m (h d)")).then_inc(S["w_in"], 16)
            sp.dma_start(roped[0][:, 1, :], wk.rearrange("m h d -> m (h d)")).then_inc(S["w_in"], 16)
            sp.dma_start(cos_sb[:, :, :], rope_cos.rearrange("(t p) d -> p t d", p=P)).then_inc(S["const_in"], 16)
            sp.dma_start(sin_sb[:, :, :], rope_sin.rearrange("(t p) d -> p t d", p=P)).then_inc(S["const_in"], 16)
            sp.dma_start(wr_sb[:, :], wr).then_inc(S["router_in"], 16)
            sp.dma_start(br_sb[:, :], br.rearrange("(o e) -> o e", o=1))\
                .then_inc(S["router_in"], 16)
            sp.wait_ge(S["iota_done"], 12)
            for k in range(SPARE):
                r0 = E * REGION + k * TILE
                sp.dma_start(x_rows[r0:r0 + TILE, :].rearrange("(p s) c -> p s c", p=P), filler[:, :, :])\
                    .then_inc(S["filled"], 16)
            sp.wait_ge(S["guard_done"], 5)
            sp.dma_start(mod_dram, mod_rows[:, :]).then_inc(S["mod_stored"], 16)
            sp.wait_ge(S["mod_stored"], 16)
            for parity in range(2):
                sp.dma_start(ga_b[parity][:, :], mod_dram[parity:parity + 1, 0:M].broadcast_to([P, M]))\
                    .then_inc(S[f"ga_in{parity}"], 16)
                sp.dma_start(sbcb_b[parity][:, :], mod_dram[parity:parity + 1, M:3 * M].broadcast_to([P, 2 * M]))\
                    .then_inc(S[f"sbcb_in{parity}"], 16)
            xv = x.rearrange("b (t p) m -> p (b t) m", p=P)
            with sp.Fori(1, NB // 2) as half:
                for parity in range(2):
                    sp.wait_ge(S[f"x_in{parity}"], 16 * half)
                    sp.dma_start(x_all[:, bass.ds(half * (2 * TT) + parity * TT, TT), :],
                                 xv[:, bass.ds(half * (2 * TT) + parity * TT, TT), :])\
                        .then_inc(S[f"x_in{parity}"], 16)
            with sp.Fori(1, NB // 2) as half:
                for parity in range(2):
                    row = bass.ds(half * 2 + parity, 1)
                    alone(sp, "x2_done", 4 * half + 2 * parity - 2)
                    sp.wait_ge(S[f"ga_in{parity}"], 16 * half)
                    sp.dma_start(ga_b[parity][:, :], mod_dram[row, 0:M].broadcast_to([P, M]))\
                        .then_inc(S[f"ga_in{parity}"], 16)
                    sp.wait_ge(S["h2_ready"], 2 * half + parity - 1)
                    sp.wait_ge(S[f"sbcb_in{parity}"], 16 * half)
                    sp.dma_start(sbcb_b[parity][:, :], mod_dram[row, M:3 * M].broadcast_to([P, 2 * M]))\
                        .then_inc(S[f"sbcb_in{parity}"], 16)
            sp.wait_ge(S["table_step"], 1)
            sp.wait_ge(S["filled"], 16 * SPARE)
            for e in range(E):
                end = sp.value_load(counts_i[0:1, e:e + 1], min_val=0, max_val=NTOK)
                sp.dma_start(x_rows[bass.ds(end + e * REGION, TILE), :].rearrange("(p s) c -> p s c", p=P),
                             filler[:, :, :]).then_inc(S["tail_filled"], 16)
            sp.wait_ge(S["tail_filled"], 16 * E)

        @block.gpsimd
        def _(pool):
            pool.memset(ident[:, :], 0.0).then_inc(S["consts_ready"], 1)
            pool.memset(ident_bf[:, :], 0.0).then_inc(S["consts_ready"], 1)
            pool.memset(causal_bf[:, :], 0.0).then_inc(S["consts_ready"], 1)
            pool.wait_ge(S["consts_ready"], 3)
            for tile in (ident, ident_bf):
                pool.affine_select(out=tile[:, :], in_=tile[:, :], compare_op=ALU.not_equal, fill=1.0,
                                   base=0, pattern=[[-1, P]], channel_multiplier=1).then_inc(S["consts_ready"], 1)
            pool.affine_select(out=causal_bf[:, :], in_=causal_bf[:, :], compare_op=ALU.is_ge, fill=MASKED,
                               base=0, pattern=[[1, P]], channel_multiplier=-1).then_inc(S["consts_ready"], 1)
            pool.memset(before_bf[:, :], 0.0).then_inc(S["iota_done"], 1)
            pool.memset(filler[:, :, :], 0.0).then_inc(S["iota_done"], 1)
            pool.iota(token_at[:, :, :], pattern=[[P, NTT], [NTOK, K]], base=0, channel_multiplier=1,
                      allow_small_or_imprecise_dtypes=True).then_inc(S["iota_done"], 1)
            pool.iota(iota_e[:, :], pattern=[[1, E]], base=0, channel_multiplier=0,
                      allow_small_or_imprecise_dtypes=True).then_inc(S["iota_done"], 1)
            pool.wait_ge(S["iota_done"], 2)
            pool.affine_select(out=before_bf[:, :], in_=before_bf[:, :], compare_op=ALU.is_ge, fill=1.0,
                               base=0, pattern=[[-1, P]], channel_multiplier=1).then_inc(S["iota_done"], 1)
            pool.memset(filler[:, :, M:RW], SKIP).then_inc(S["iota_done"], 1)
            pool.iota(base_e[:, :], pattern=[[REGION, E]], base=0, channel_multiplier=0,
                      allow_small_or_imprecise_dtypes=True).then_inc(S["iota_done"], 1)
            pool.memset(ones_e[:, :], 1.0).then_inc(S["iota_done"], 1)
            pool.iota(iota_t[:, :], pattern=[[1, NTILES]], base=0, channel_multiplier=0,
                      allow_small_or_imprecise_dtypes=True).then_inc(S["iota_done"], 1)
            pool.memset(ones_bf[:, :], 1.0).then_inc(S["iota_done"], 1)
            pool.memset(ones_row[:, :], 1.0).then_inc(S["iota_done"], 1)
            pool.memset(counts[0][:, :], 0.0).then_inc(S["iota_done"], 1)
            for k in range(2):
                pool.memset(mv2[k][:, :, :], 1.0).then_inc(S["ones_ready"], 1)
                pool.memset(vals[k][:, :, :, D:VW], 1.0).then_inc(S["ones_ready"], 1)
                pool.memset(ssq[k][:, :], 1.0).then_inc(S["ones_ready"], 1)
                pool.memset(mv[k][:, :, :], 1.0).then_inc(S["ones_ready"], 1)

            def body(half, parity, live):
                n = 2 * half + parity
                _, _, A, B, _, _, _, _, ST = live

                def add(u):
                    wait(pool, "rope_done", 2 * (NU * n + u + 1))
                    pool.tensor_tensor(out=roped[parity][:, u, :], in0=roped[parity][:, u, :],
                                       in1=rope_b[:, u % 2, :], op=ALU.add).then_inc(S["add_done"], 1)
                if A:
                    add(0)
                if ST:
                    b = n - 6
                    alone(pool, "route_step", STEPS * (b + 1))
                    wait(pool, "rows_copied", b + 1)
                    for t in range(TT):
                        for j in range(K):
                            at = place[parity][:, t * K + j:t * K + j + 1]
                            pool.indirect_dma_start(
                                out=x_rows, out_offset=bass.IndirectOffsetOnAxis(ap=at, axis=0),
                                in_=rows[j][parity][:, t, :], in_offset=None)\
                                .then_inc(S[f"scattered{parity}"], 16)
                if B:
                    b = n - 1
                    wait(pool, "rr_done", n + 2)
                    wait(pool, "add_done", cap(NU * n + 1, NU * NB))
                    for t in range(TT):
                        v = roped[1 - parity][:, t, :].rearrange("p (h d) -> p h d", h=H)
                        r = rr[1 - parity][:, t * H:(t + 1) * H].rearrange("p (h o) -> p h o", o=1)\
                            .to_broadcast([P, H, D])
                        pool.tensor_tensor(out=v, in0=v, in1=r, op=ALU.mult).then_inc(S["qs_done"], 1)
                if A:
                    for u in range(1, NU):
                        add(u)
            iterations(pool, body)
            for k in range(2):
                pool.wait_ge(S[f"scattered{k}"], 16 * TT * K * NB // 2)

        @block.scalar
        def _(act):
            act.wait_ge(S["c_in"], 32)
            nc.scalar.activation(silu_c[:, :], c_sb[:, :], ACT.Silu).then_inc(S["silu_done"], 1)
            act.wait_ge(S["w_in"], 32)
            for k in range(2):
                nc.scalar.activation(wqk_hi[:, k * HD:(k + 1) * HD], roped[0][:, k, :], ACT.Copy, scale=WS)\
                    .then_inc(S["hi_done"], 1)
            act.wait_ge(S["wvt_done"], 1)
            nc.scalar.activation(roped[1][:, 0, :], UN[0][:, :], ACT.Copy).then_inc(S["wvt_ready"], 1)
            act.wait_ge(S["wvo_done"], 1)
            nc.scalar.activation(roped[1][:, 1, :], UN[1][:, :], ACT.Copy, scale=WS).then_inc(S["wvo_scaled"], 1)
            act.wait_ge(S["wvo_scaled"], 1)
            nc.scalar.activation(wvo_hi[:, :], roped[1][:, 1, :], ACT.Copy).then_inc(S["wvo_hi_done"], 1)
            act.wait_ge(S["ones_ready"], 8)
            act.wait_ge(S["mod_copied"], 2)

            def body(half, parity, live):
                n = 2 * half + parity
                _, X, A, B, C, _, N2, RT, ST = live
                for h in range(H):
                    if C:
                        b = n - 2
                        g = H * b + h
                        if h == 0:
                            wait(act, "rr_done", b + 3)
                        wait(act, "s_done", g + 1)
                        wait(act, "o_done", g - NPR + 1)
                        wait(act, "exp_done", 2 * (g - NPR + 1))
                        r = rr[parity]
                        kc = TT * H + h
                        nc.scalar.activation(probs[:, h % NPR, 0:T], SC[h % 2][:, 0:T], ACT.Exp,
                                             scale=r[:, kc:kc + 1]).then_inc(S["exp_done"], 1)
                        nc.scalar.activation(probs[:, h % NPR, T:T + P], SC[h % 2][:, T:T + P], ACT.Exp,
                                             scale=r[:, kc + H:kc + H + 1]).then_inc(S["exp_done"], 1)
                    if ST and h == 0:
                        wait(act, "px_done", n - 5)
                        nc.scalar.activation(ahead[:, :], SC[0][:, BESIDE:BESIDE + TT * E], ACT.Copy)\
                            .then_inc(S["ahead_copied"], 1)
                    if RT and h == 1:
                        b = n - 5
                        wait(act, "rt_done", b + 1)
                        nc.scalar.activation(lg[1 - parity][:, :, :].rearrange("p t e -> p (t e)"),
                                             SC[1][:, BESIDE:BESIDE + TT * E], ACT.Copy).then_inc(S["lg_ready"], 1)
                    if A:
                        w, u = 2 * NU * n + h, h // 2
                        wait(act, "p_done", w + 1)
                        wait(act, "sq_done", HH * (w - 1))
                        if h == 0:
                            wait(act, "chain_done", (CH - 1) * n + 2)
                        for j in range(HH):
                            c = HH * (h % 2) + j
                            nc.scalar.activation(squares[:, c * D:(c + 1) * D], UN[0][:, c * D:(c + 1) * D],
                                                 ACT.Square, accum_out=ssq[parity][:, u * H + c:u * H + c + 1])\
                                .then_inc(S["sq_done"], 1)
                    if B and h in TURNED:
                        b = n - 1
                        u = TURNED[h]
                        t = u % TT
                        dst = (q_t if u < TT else k_t)[1 - parity]
                        wait(act, "tr_done", NU * b + list(TURNED).index(h) + 1)
                        wait(act, "s_done", H * (b - 1))
                        nc.scalar.activation(dst[:, :, t * P:(t + 1) * P],
                                             UN[1][:, :].rearrange("p (h c) -> p h c", h=H), ACT.Copy)\
                            .then_inc(S["tr_copied"], 1)
                    if B and h in VALUES:
                        b, t = n - 1, VALUES[h]
                        wait(act, "vw_done", TT * b + t + 1)
                        wait(act, "o_done", H * (b - 1))
                        nc.scalar.activation(vals[1 - parity][:, t, :, 0:D],
                                             UN[1][:, :].rearrange("p (h c) -> p h c", h=H), ACT.Copy,
                                             scale=1.0 / WS).then_inc(S["vals_ready"], 1)
                    if X and h == H_AT:
                        b = n + 1
                        wait(act, "tx_done", b + 1)
                        wait(act, "h_ready", b)
                        nc.scalar.activation(h_t[:, :], UN[1][:, 0:T], ACT.Identity,
                                             scale=mod_t[:, 1, bass.ds(b, 1)],
                                             bias=mod_t[:, 0, bass.ds(b, 1)]).then_inc(S["ht32_done"], 1)
                        wait(act, "ht32_done", b + 1)
                        wait(act, "vw_done", TT * (b - 1))
                        nc.scalar.activation(h_hi[1 - parity][:, :], h_t[:, :], ACT.Copy)\
                            .then_inc(S["hhi_done"], 1)
                    if RT and h in (3, 6):
                        b = n - 5
                        src, dst, after = ((lg_m, e_lg, LESS_TOP) if h == 3 else (gap, e_gap, GAP))
                        wait(act, "route_step", STEPS * b + after)
                        nc.scalar.activation(dst[:], src[:], ACT.Exp).then_inc(S["route_exp"], 1)
                    if N2 and h == H2_AT:
                        b = n - 4
                        wait(act, "h2t_done", b + 1)
                        wait(act, "rt_done", b)
                        nc.scalar.activation(h2_t[:, :], UN[1][:, 0:T], ACT.Copy).then_inc(S["h2t_copied"], 1)
                        sc_wait(act, half, parity, b)
                        nc.scalar.activation(rows[1][parity][:, :, 0:M], rows[0][parity][:, :, 0:M], ACT.Copy)\
                            .then_inc(S["rows_copied"], 1)
            iterations(act, body)

        @block.vector
        def _(dve):
            dve.wait_ge(S["ct_done"], 1)
            nc.vector.tensor_copy(silu_ct[:, :], OP[0][:, 0:NB]).then_inc(S["ct_ready"], 1)
            dve.wait_ge(S["mod_done"], 1)
            nc.vector.tensor_copy(mod_t[:, 0, :], SC[0][:, 0:NB]).then_inc(S["mod_copied"], 1)
            nc.vector.tensor_scalar(mod_t[:, 1, :], SC[0][:, NB:2 * NB], 1.0, None, ALU.add).then_inc(S["mod_copied"], 1)
            nc.vector.tensor_copy(mod_rows[:, :], SC[1][0:NB, :]).then_inc(S["mod_copied"], 1)
            dve.wait_ge(S["mod_copied"], 3)
            gates = mod_rows[:, :].rearrange("b (j m) -> b j m", j=4)[:, 0:4:3, :]
            ga3 = guard_a[:, :].rearrange("b (j m) -> b j m", j=2)
            gb3 = guard_b[:, :].rearrange("b (j m) -> b j m", j=2)
            nc.vector.tensor_scalar(ga3, gates, 0.0, 2.0, ALU.is_ge, ALU.mult).then_inc(S["guard_done"], 1)
            nc.vector.scalar_tensor_tensor(out=gb3, in0=gates, scalar=-1.0, in1=gates, op0=ALU.mult, op1=ALU.max)\
                .then_inc(S["guard_done"], 1)
            nc.vector.tensor_scalar(mod_rows[:, 2 * M:3 * M], mod_rows[:, 2 * M:3 * M], 1.0, None, ALU.add)\
                .then_inc(S["guard_done"], 1)
            dve.wait_ge(S["guard_done"], 3)
            nc.vector.tensor_scalar(ga3, ga3, 1.0, None, ALU.subtract).then_inc(S["guard_done"], 1)
            dve.wait_ge(S["guard_done"], 4)
            nc.vector.scalar_tensor_tensor(out=gates, in0=gb3, scalar=0.25, in1=ga3, op0=ALU.max, op1=ALU.mult)\
                .then_inc(S["guard_done"], 1)
            dve.wait_ge(S["hi_done"], 2)
            for k in range(2):
                nc.vector.scalar_tensor_tensor(out=wqk_lo[:, k * HD:(k + 1) * HD], in0=roped[0][:, k, :], scalar=WS,
                                               in1=wqk_hi[:, k * HD:(k + 1) * HD], op0=ALU.mult, op1=ALU.subtract)\
                    .then_inc(S["split_done"], 1)
            dve.wait_ge(S["wvo_hi_done"], 1)
            nc.vector.tensor_tensor(out=wvo_lo[:, :], in0=roped[1][:, 1, :], in1=wvo_hi[:, :], op=ALU.subtract)\
                .then_inc(S["split_done"], 1)
            dve.wait_ge(S["ones_ready"], 8)
            dve.wait_ge(S["const_in"], 32)
            dve.wait_ge(S["split_done"], 3)
            dve.wait_ge(S["iota_done"], 12)
            dve.wait_ge(S["router_in"], 32)

            NEWTON = range(GUESS + 1, CH + 1)
            SMALL = {
                (0, 0): (VX_Q, VX_K, VX_X, VX_H),
                (0, 1): (HALF_BITS,), (0, 2): (GUESS,), (0, 3): NEWTON[0:1], (0, 4): NEWTON[1:2],
                (1, 0): NEWTON[2:3], (1, 1): NEWTON[3:4], (1, 2): NEWTON[4:5], (1, 3): NEWTON[5:6],
                (1, 4): NEWTON[6:7], (2, 0): NEWTON[7:8], (2, 1): NEWTON[8:9]}
            ROUTE = {
                (3, 0): (TOP_L0, TOP_L1), (3, 1): (LESS_TOP,),
                (4, 0): (E_SUM,), (4, 1): (E_REC,), (4, 2): (SCORE,), (4, 3): (TOP_S0, TOP_S1),
                (5, 0): (TOP_I0, TOP_I1), (5, 1): (TOP_F, GAP), (5, 2): (ONE_HOT,), (5, 3): (CHOSEN,),
                (5, 4): (COUNT_A,), (6, 0): (COUNT_B,), (7, 0): (W_DEN,), (7, 1): (W_FIRST,),
                (7, 2): (W_SECOND,), (7, 3): (TO_0, TO_1)}
            STORE = {(1, 0): (PLACE_E,), (1, 1): (PLACE_K,), (1, 2): (PLACE_F,), (1, 3): (PLACE_I,)}

            def body(half, parity, live):
                n = 2 * half + parity
                L, X, A, _, C, R, N2, RT, ST = live
                other = 1 - parity
                chain = X or A or live[3] or C or R or N2
                r = rr[other]

                def root(k):
                    base = (CH - 1) * (n + 1)
                    s = WS * WS * RMS_EPS
                    if k == VX_Q:
                        wait(dve, "sq_done", cap(NU * H * n, NU * H * NB))
                        wait(dve, "mv2_done", TT * (n - 3))
                        wait(dve, "mv_done", cap(TT * (n + 2), TT * NB))
                        wait(dve, "chain_done", base)
                        ins = nc.vector.tensor_scalar(vx[:, 0:TT * H], ssq[other][:, 0:TT * H], 1.0 / D, s,
                                                      ALU.mult, ALU.add)
                    elif k == VX_K:
                        ins = nc.vector.tensor_scalar(vx[:, TT * H:NU * H], ssq[other][:, TT * H:NU * H], float(D),
                                                      s * D * D, ALU.mult, ALU.add)
                    elif k in (VX_X, VX_H):
                        m = mv[other] if k == VX_X else mv2[parity]
                        c0 = NU * H + (k - VX_X) * TT
                        ins = nc.vector.tensor_scalar(vx[:, c0:c0 + TT], m[:, :, 1:2].rearrange("p t o -> p (t o)"),
                                                      LN_EPS, None, ALU.add)
                    elif k == HALF_BITS:
                        wait(dve, "chain_done", base + VX_H)
                        ins = nc.vector.tensor_scalar(half_bits[:, :], vx[:, :].bitcast(I32), 1, None,
                                                      ALU.logical_shift_right)
                    elif k == GUESS:
                        wait(dve, "chain_done", base + HALF_BITS)
                        ins = nc.vector.tensor_scalar(y_a[:, :].bitcast(I32), half_bits[:, :], -1.0, float(MAGIC),
                                                      ALU.mult, ALU.add)
                    else:
                        wait(dve, "chain_done", base + k - 1)
                        part_of_step = (k - NEWTON[0]) % 3
                        if part_of_step == 0:
                            ins = nc.vector.scalar_tensor_tensor(out=y_t[:, :], in0=y_a[:, :], scalar=-0.5,
                                                                 in1=y_a[:, :], op0=ALU.mult, op1=ALU.mult)
                        elif part_of_step == 1:
                            ins = nc.vector.tensor_tensor(out=y_t[:, :], in0=y_t[:, :], in1=vx[:, :], op=ALU.mult)
                        else:
                            if k == CH:
                                wait(dve, "exp_done", cap(2 * H * (n - 2), 2 * H * NB))
                            dst = r if k == CH else y_a
                            ins = nc.vector.scalar_tensor_tensor(out=dst[:, :], in0=y_t[:, :], scalar=1.5,
                                                                 in1=y_a[:, :], op0=ALU.add, op1=ALU.mult)
                            if k == CH:
                                ins.then_inc(S["rr_done"], 1)
                                return
                    ins.then_inc(S["chain_done"], 1)

                def normalise():
                    if X:
                        b = n + 1
                        wait(dve, "rr_done", b + 1)
                        wait(dve, "tx_done", b)
                        for t in range(TT):
                            nc.vector.tensor_scalar(xn[:, t, :], x_all[:, bass.ds(TT * b + t, 1), :]
                                                    .rearrange("p o m -> p (o m)"), mv[other][:, t, 0:1],
                                                    r[:, NU * H + t:NU * H + t + 1], ALU.subtract, ALU.mult)\
                                .then_inc(S["xn_ready"], 1)

                def normalise2():
                    if N2:
                        wait(dve, "rr_done", n + 2)
                        for t in range(TT):
                            c0 = NU * H + TT + t
                            nc.vector.tensor_scalar(xn2[:, t, :], x_all[:, bass.ds(TT * (n - 4) + t, 1), :]
                                                    .rearrange("p o m -> p (o m)"), mv2[parity][:, t, 0:1],
                                                    r[:, c0:c0 + 1], ALU.subtract, ALU.mult)\
                                .then_inc(S["xn2_done"], 1)

                def modulate(b, step):
                    row = sbcb_b[parity][:, (1 - step) * M:(2 - step) * M].rearrange("p (o m) -> p o m", o=1)\
                        .to_broadcast([P, TT, M])
                    if step == 0:
                        wait(dve, "xn2_done", 3 * b + 2)
                        dve.wait_ge(S[f"sbcb_in{parity}"], 16 * (half - 1))
                        nc.vector.tensor_tensor(out=xn2[:, :, :], in0=xn2[:, :, :], in1=row, op=ALU.mult)\
                            .then_inc(S["xn2_done"], 1)
                    else:
                        wait(dve, "xn2_done", 3 * b + 3)
                        sc_wait(dve, half, parity, b)
                        nc.vector.tensor_tensor(out=rows[0][parity][:, :, 0:M], in0=xn2[:, :, :], in1=row,
                                                op=ALU.add).then_inc(S["h2_ready"], 1)

                def route(b, step):
                    at = STEPS * b

                    def after(k):
                        own = alone if step in (TOP_S0, TOP_S1, TOP_I0, TOP_I1) else wait
                        own(dve, "route_step", at + k)

                    def each_t(v):
                        return v.rearrange("p (t o) -> p t o", o=1)
                    if step in (TOP_L0, TOP_L1):
                        t = step - TOP_L0
                        if t == 0:
                            alone(dve, "lg_ready", b + 1)
                        ins = nc.vector.max(top_l[:, t, :], lg[other][:, t, :])
                    elif step == LESS_TOP:
                        after(TOP_L1)
                        wait(dve, "route_exp", 2 * b)
                        ins = nc.vector.tensor_tensor(out=lg_m[:, :, :], in0=lg[other][:, :, :],
                                                      in1=top_l[:, :, 0:1].to_broadcast([P, TT, E]), op=ALU.subtract)
                    elif step == E_SUM:
                        wait(dve, "route_exp", 2 * b + 1)
                        ins = nc.vector.tensor_reduce(out=e_sum[:, :], in_=e_lg[:, :, :], op=ALU.add, axis=AX.X)
                    elif step == E_REC:
                        after(E_SUM)
                        ins = nc.vector.reciprocal(e_rec[:, :], e_sum[:, :])
                    elif step == SCORE:
                        after(E_REC)
                        ins = nc.vector.tensor_tensor(out=score[:, :, :], in0=e_lg[:, :, :],
                                                      in1=each_t(e_rec[:, :]).to_broadcast([P, TT, E]), op=ALU.mult)
                    elif step in (TOP_S0, TOP_S1):
                        t = step - TOP_S0
                        after(SCORE)
                        ins = nc.vector.max(top_s[:, t, :], score[:, t, :])
                    elif step in (TOP_I0, TOP_I1):
                        t = step - TOP_I0
                        after(TOP_S0 + t)
                        ins = nc.vector.max_index(top_i[:, t, :], top_s[:, t, :], score[:, t, :])
                    elif step == TOP_F:
                        after(TOP_I1)
                        ins = nc.vector.tensor_copy(top_f[:, :, :], top_i[:, :, 0:K])
                    elif step == GAP:
                        after(TOP_S1)
                        ins = nc.vector.tensor_tensor(out=each_t(gap[:, :]), in0=top_s[:, :, 1:2],
                                                      in1=top_s[:, :, 0:1], op=ALU.subtract)
                    elif step == ONE_HOT:
                        after(TOP_F)
                        ins = nc.vector.tensor_tensor(
                            out=one_hot[:, :, :],
                            in0=iota_e[:, :].rearrange("p (o e) -> p o e", o=1).to_broadcast([P, TT * K, E]),
                            in1=top_f[:, :, :].rearrange("p t (j o) -> p (t j) o", o=1)
                                .to_broadcast([P, TT * K, E]), op=ALU.is_equal)
                    elif step == CHOSEN:
                        after(ONE_HOT)
                        wait(dve, "px_done", b)
                        oh = one_hot[:, :, :].rearrange("p (t j) e -> p t j e", j=K)
                        ins = nc.vector.tensor_tensor(out=chosen[:, :, :], in0=oh[:, :, 0, :], in1=oh[:, :, 1, :],
                                                      op=ALU.add)
                    elif step == COUNT_A:
                        after(CHOSEN)
                        ins = nc.vector.tensor_tensor(out=counts[parity][:, :], in0=counts[other][:, :],
                                                      in1=chosen[:, 0, :], op=ALU.add)
                    elif step == COUNT_B:
                        after(COUNT_A)
                        ins = nc.vector.tensor_tensor(out=counts[parity][:, :], in0=counts[parity][:, :],
                                                      in1=chosen[:, 1, :], op=ALU.add)
                    elif step == W_DEN:
                        wait(dve, "route_exp", 2 * b + 2)
                        ins = nc.vector.tensor_scalar(w_den[:, :], e_gap[:, :], 1.0, None, ALU.add)
                    elif step == W_FIRST:
                        after(W_DEN)
                        ins = nc.vector.reciprocal(weights[:, bass.ds(TT * b, TT), 0:1], each_t(w_den[:, :]))
                    elif step == W_SECOND:
                        after(W_FIRST)
                        ins = nc.vector.tensor_tensor(out=weights[:, bass.ds(TT * b, TT), 1:2],
                                                      in0=weights[:, bass.ds(TT * b, TT), 0:1],
                                                      in1=each_t(e_gap[:, :]), op=ALU.mult)
                    elif step in (TO_0, TO_1):
                        j = step - TO_0
                        ins = nc.vector.tensor_copy(rows[j][other][:, :, M:RW],
                                                    token_at[:, bass.ds(TT * b, TT), j:j + 1])
                    elif step == PLACE_E:
                        wait(dve, "ahead_copied", b + 1)
                        ins = nc.vector.tensor_tensor(
                            out=place_e[:, :, :], in0=ahead[:, :].rearrange("p (t e) -> p t e", t=TT),
                            in1=base_e[:, :].rearrange("p (o e) -> p o e", o=1).to_broadcast([P, TT, E]), op=ALU.add)
                    elif step == PLACE_K:
                        after(PLACE_E)
                        pe3 = place_e[:, :, :].rearrange("p t (o e) -> p t o e", o=1).to_broadcast([P, TT, K, E])
                        ins = nc.vector.tensor_tensor(
                            out=place_k[:, :, :].rearrange("p (t j) e -> p t j e", j=K),
                            in0=one_hot[:, :, :].rearrange("p (t j) e -> p t j e", j=K), in1=pe3, op=ALU.mult)
                    elif step == PLACE_F:
                        after(PLACE_K)
                        ins = nc.vector.tensor_reduce(out=place_f[:, :], in_=place_k[:, :, :], op=ALU.add, axis=AX.X)
                    elif step == PLACE_I:
                        after(PLACE_F)
                        ins = nc.vector.tensor_copy(place[parity][:, :], place_f[:, :])
                    ins.then_inc(S["route_step"], 1)

                def denominators(b, h):
                    wait(dve, "o_done", H * b + h + 1)
                    o = OP[h % 2][:, :].rearrange("p (t c) -> p t c", t=TT)
                    nc.vector.reciprocal(den[:, h % 2, :], o[:, :, D:D + 1].rearrange("p t o -> p (t o)"))\
                        .then_inc(S["den_done"], 1)

                def add_head(b, h, t):
                    g = H * b + h
                    o = OP[h % 2][:, :].rearrange("p (t c) -> p t c", t=TT)
                    wait(dve, "den_done", g + 1)
                    if h == 0:
                        if t == 0:
                            wait(dve, "x2_done", 2 * b)
                        ins = nc.vector.tensor_scalar(acc[:, t, :], o[:, t, 0:M], den[:, h % 2, t:t + 1], None,
                                                      ALU.mult)
                    else:
                        wait(dve, "acc_done", TT * (g - 1) + t + 1)
                        ins = nc.vector.scalar_tensor_tensor(out=acc[:, t, :], in0=o[:, t, 0:M],
                                                             scalar=den[:, h % 2, t:t + 1], in1=acc[:, t, :],
                                                             op0=ALU.mult, op1=ALU.add)
                    ins.then_inc(S["acc_done"], 1)

                def small(h, slot):
                    for k in SMALL.get((h, slot), ()):
                        if chain:
                            root(k)
                    for k in STORE.get((h, slot), ()):
                        if ST:
                            route(n - 6, k)
                    for k in ROUTE.get((h, slot), ()):
                        if RT:
                            route(n - 5, k)

                for h in range(H):
                    w, u, bank = 2 * NU * n + h, h // 2, h % 2
                    t = u % TT
                    heads = slice(bank * HH * D, (bank + 1) * HH * D)
                    adds, ended = (C, (n - 2, h - 1)) if h else (R, (n - 3, H - 1))
                    if adds:
                        denominators(*ended)
                    small(h, 0)
                    if R and h == 1:
                        b = n - 3
                        xs = x_all[:, bass.ds(TT * b, TT), :]
                        wait(dve, "x2_done", 2 * b + 1)
                        nc.vector.tensor_tensor(out=xs, in0=xs, in1=acc[:, :, :], op=ALU.add)\
                            .then_inc(S["x2_done"], 1)
                    if A:
                        wait(dve, "sq_done", HH * (w + 1))
                        wait(dve, "tr_done", NU * (n - 1))
                        nc.vector.tensor_tensor(
                            out=roped[parity][:, u, heads].rearrange("p (g c) -> p g c", c=D // 2),
                            in0=UN[0][:, heads].rearrange("p (g c) -> p g c", c=D // 2),
                            in1=cos_sb[:, t:t + 1, :].to_broadcast([P, 2 * HH, D // 2]),
                            op=ALU.mult).then_inc(S["ropea_done"], 1)
                    small(h, 1)
                    if adds:
                        add_head(*ended, 0)
                    small(h, 2)
                    if adds:
                        add_head(*ended, 1)
                    small(h, 3)
                    if A:
                        wait(dve, "add_done", NU * n + u - 1)
                        nc.vector.tensor_tensor(
                            out=rope_b[:, u % 2, heads].rearrange("p (h s c) -> p h s c", h=HH, s=2),
                            in0=UN[0][:, heads].rearrange("p (h s c) -> p h s c", h=HH, s=2)[:, :, ::-1, :],
                            in1=sin_sb[:, t, :].rearrange("p (o s c) -> p o s c", o=1, s=2)
                                .to_broadcast([P, HH, 2, D // 2]),
                            op=ALU.mult).then_inc(S["rope_done"], 1)
                    small(h, 4)
                    if R and h == 0:
                        b = n - 3
                        wait(dve, "acc_done", H * TT * (b + 1))
                        dve.wait_ge(S[f"ga_in{other}"], 16 * (half + (parity - 3) // 2 + 1))
                        nc.vector.tensor_tensor(
                            out=acc[:, :, :], in0=acc[:, :, :],
                            in1=ga_b[other][:, :].rearrange("p (o m) -> p o m", o=1).to_broadcast([P, TT, M]),
                            op=ALU.mult).then_inc(S["x2_done"], 1)
                    if h == 2:
                        normalise()
                    if h == 3:
                        normalise2()
                    if R and h in (2, 3):
                        b = n - 3
                        for t in range(TT):
                            if h == 2:
                                alone(dve, "x2_done", 2 * b + 2)
                                nc.vector.bn_stats(bst2[:, t, :], x_all[:, bass.ds(TT * b + t, 1), :]
                                                   .rearrange("p o m -> p (o m)")).then_inc(S["stat2_done"], 1)
                            else:
                                alone(dve, "stat2_done", TT * b + t + 1)
                                nc.vector.bn_aggr(mv2[other][:, t, :], bst2[:, t, :]).then_inc(S["mv2_done"], 1)
                    if N2 and h in (4, 5):
                        modulate(n - 4, h - 4)
                    if L and h == 6:
                        b = n + 2
                        alone(dve, f"x_in{parity}", 16 * (half + 2))
                        wait(dve, "mv_done", TT * b)
                        for k in range(TT):
                            nc.vector.bn_stats(bst[:, k, :], x_all[:, bass.ds(TT * b + k, 1), :]
                                               .rearrange("p o m -> p (o m)")).then_inc(S["stat_done"], 1)
                    if X and h == 6:
                        b = n + 1
                        wait(dve, "hhi_done", b + 1)
                        wait(dve, "vw_done", TT * (b - 1))
                        nc.vector.tensor_tensor(out=h_lo[other][:, :], in0=h_t[:, :], in1=h_hi[other][:, :],
                                                op=ALU.subtract).then_inc(S["h_ready"], 1)
                    if L and h == 7:
                        for k in range(TT):
                            alone(dve, "stat_done", TT * (n + 2) + k + 1)
                            nc.vector.bn_aggr(mv[parity][:, k, :], bst[:, k, :]).then_inc(S["mv_done"], 1)
            iterations(dve, body)

            dve.wait_ge(S["count_done"], 1)
            steps = [0]

            def link(ins):
                steps[0] += 1
                ins.then_inc(S["table_step"], 1)
                dve.wait_ge(S["table_step"], steps[0])
            link(nc.vector.tensor_copy(counts_i[:, :], UN[1][:, 0:E]))
            link(nc.vector.tensor_scalar(tiles_i[:, :], UN[1][:, 0:E], float(TILE - 1), None, ALU.add))
            link(nc.vector.tensor_scalar(tiles_i[:, :], tiles_i[:, :], TILE.bit_length() - 1, None,
                                         ALU.logical_shift_right))
            link(nc.vector.tensor_copy(tiles_f[:, :], tiles_i[:, :]))
            link(nc.vector.tensor_tensor_scan(out=tiles_to[:, :], data0=ones_e[:, :], data1=tiles_f[:, :],
                                              initial=0.0, op0=ALU.mult, op1=ALU.add))

            def by_tile(v):
                return v.rearrange("p (o e) -> p o e", o=1).to_broadcast([P, NTILES, E])
            link(nc.vector.tensor_tensor(out=behind,
                                         in0=iota_t[:, :].rearrange("p (i o) -> p i o", o=1)
                                             .to_broadcast([P, NTILES, E]),
                                         in1=by_tile(tiles_to[:, :]), op=ALU.is_ge))
            link(nc.vector.tensor_reduce(out=tile_e[:, :], in_=behind, op=ALU.add, axis=AX.X))
            link(nc.vector.tensor_tensor(out=behind, in0=behind, in1=by_tile(tiles_f[:, :]),
                                         op=ALU.mult))
            link(nc.vector.tensor_reduce(out=tile_r[:, :], in_=behind, op=ALU.add, axis=AX.X))
            link(nc.vector.tensor_tensor(out=tile_r[:, :], in0=iota_t[:, :], in1=tile_r[:, :], op=ALU.subtract))
            link(nc.vector.tensor_scalar(tile_r[:, :], tile_r[:, :], float(TILE), None, ALU.mult))
            link(nc.vector.scalar_tensor_tensor(out=table[:, 1, :], in0=tile_e[:, :], scalar=float(REGION),
                                                in1=tile_r[:, :], op0=ALU.mult, op1=ALU.add))
            link(nc.vector.tensor_scalar(table[:, 0, :], tile_e[:, :], float(E - 1), None, ALU.min))

        @block.tensor
        def _(pe):
            pe.wait_ge(S["silu_done"], 1)
            pe.wait_ge(S["consts_ready"], 6)
            nc.tensor.transpose(OP[0][:, 0:NB], silu_c[:, :], ident[0:NB, 0:NB]).then_inc(S["ct_done"], 1)
            pe.wait_ge(S["ct_ready"], 1)
            for j in range(2):
                nc.tensor.matmul(SC[0][:, j * NB:(j + 1) * NB], wmod_sb[:, j * M:(j + 1) * M], silu_ct[:, :],
                                 start=True, stop=True)
            nc.tensor.matmul(SC[1][0:NB, :], silu_ct[:, :], wmod_sb[:, 2 * M:6 * M], start=True, stop=True)\
                .then_inc(S["mod_done"], 1)
            pe.wait_ge(S["wv_in"], 32)
            for h in range(H):
                ins = nc.tensor.transpose(UN[0][:, h * P:(h + 1) * P], roped[0][:, 2, h * D:(h + 1) * D], ident[:, :])
            ins.then_inc(S["wvt_done"], 1)
            pe.wait_ge(S["wvt_ready"], 1)
            for h in range(H):
                ins = nc.tensor.matmul(UN[1][:, h * M:(h + 1) * M], roped[1][:, 0, h * M:(h + 1) * M],
                                       roped[0][:, 3, h * M:(h + 1) * M], start=True, stop=True)
            ins.then_inc(S["wvo_done"], 1)
            pe.wait_ge(S["wvo_scaled"], 1)
            pe.wait_ge(S["split_done"], 3)
            pe.wait_ge(S["ones_ready"], 8)
            pe.wait_ge(S["iota_done"], 12)
            pe.wait_ge(S["router_in"], 32)
            pe.wait_ge(S["mod_copied"], 3)

            def split_product(dst, hi, lo, w_hi, w_lo):
                for k in range(0, w_hi.shape[1], 512):
                    for m, (a, w) in enumerate(((hi, w_hi), (hi, w_lo), (lo, w_hi))):
                        ins = nc.tensor.matmul(dst[:, k:k + 512], a, w[:, k:k + 512], start=(m == 0), stop=(m == 2))
                return ins

            def body(half, parity, live):
                n = 2 * half + parity
                _, X, A, B, C, _, N2, RT, ST = live
                other = 1 - parity

                def values_times_probs(b, h):
                    g = H * b + h
                    if h == 0:
                        wait(pe, "vals_ready", TT * (b + 1))
                    wait(pe, "exp_done", 2 * (g + 1))
                    wait(pe, "acc_done", TT * (g - 1))
                    o, pr, v = OP[h % 2], probs[:, h % NPR, :], vals[parity]
                    nc.tensor.matmul(o[:, 0:D + 1], pr[:, 0:P], v[:, 0, h, 0:D + 1], start=True, stop=True)
                    nc.tensor.matmul(o[:, 256:256 + D + 1], pr[:, P:2 * P], v[:, 0, h, 0:D + 1],
                                     start=True, stop=False)
                    nc.tensor.matmul(o[:, 256:256 + D + 1], pr[:, 2 * P:3 * P], v[:, 1, h, 0:D + 1],
                                     start=False, stop=True).then_inc(S["o_done"], 1)

                for h in range(H):
                    g = H * (n - 2) + h
                    if C or ST and h == 0 or RT and h == 1:
                        wait(pe, "exp_done", cap(2 * (g - 1), 2 * H * NB))
                        if h == 2 or not C:
                            wait(pe, "ahead_copied", n - 5 if h == 2 else n - 6)
                        if h == 3 or not C:
                            wait(pe, "lg_ready", cap(n - 4 if h == 3 else n - 5, NB))
                    if ST and h == 0:
                        b = n - 6
                        wait(pe, "route_step", STEPS * b + CHOSEN)
                        for t in range(TT):
                            dst = SC[0][:, BESIDE + t * E:BESIDE + (t + 1) * E]
                            nc.tensor.matmul(dst, before_bf[:, :], chosen[:, t, :], start=True, stop=False)
                            for k in range(t):
                                nc.tensor.matmul(dst, ones_bf[:, :], chosen[:, k, :], start=False, stop=False)
                            ins = nc.tensor.matmul(dst, ones_bf[:, :], counts[parity][:, :], start=False, stop=True)
                        ins.then_inc(S["px_done"], 1)
                    if RT and h == 1:
                        b = n - 5
                        wait(pe, "h2t_copied", b + 1)
                        for t in range(TT):
                            dst = SC[1][:, BESIDE + t * E:BESIDE + (t + 1) * E]
                            nc.tensor.matmul(dst, h2_t[:, t * P:(t + 1) * P], wr_sb[:, :], start=True, stop=False)
                            ins = nc.tensor.matmul(dst, ones_row[:, :], br_sb[:, :], start=False, stop=True)
                        ins.then_inc(S["rt_done"], 1)
                    if C:
                        if h == 0:
                            wait(pe, "tr_copied", NU * (n - 1))
                        s, q, k = SC[h % 2], q_t[parity], k_t[parity]
                        nc.tensor.matmul(s[:, 0:T], k[:, h, 0:P], q[:, h, 0:T], start=True, stop=False)
                        nc.tensor.matmul(s[:, 0:P], ident_bf[:, :], causal_bf[:, :], start=False, stop=True)
                        nc.tensor.matmul(s[:, T:T + P], k[:, h, P:T], q[:, h, P:T], start=True, stop=False)
                        nc.tensor.matmul(s[:, T:T + P], ident_bf[:, :], causal_bf[:, :], start=False, stop=True)\
                            .then_inc(S["s_done"], 1)
                    if A:
                        w, u = 2 * NU * n + h, h // 2
                        t, kind = u % TT, u // TT
                        if h == 0:
                            wait(pe, "h_ready", n + 1)
                        wait(pe, "rope_done", w - 1)
                        toks = slice(t * P, (t + 1) * P)
                        c0 = kind * HD + (h % 2) * HH * D
                        split_product(UN[0][:, (h % 2) * HH * D:(h % 2 + 1) * HH * D], h_hi[parity][:, toks],
                                      h_lo[parity][:, toks], wqk_hi[:, c0:c0 + HH * D], wqk_lo[:, c0:c0 + HH * D])\
                            .then_inc(S["p_done"], 1)
                    if (h == 0 and B) or (h == H_AT and X and not B) or (h == H2_AT and N2 and not B):
                        wait(pe, "h2t_copied", cap(n - 4, NB))
                        wait(pe, "ht32_done", cap(n + 1, NB))
                    if B and h in TURNED:
                        b, u = n - 1, TURNED[h]
                        if h == 1:
                            wait(pe, "tr_copied", NU * b + 1)
                        elif h == Q_AT:
                            if X:
                                wait(pe, "ht32_done", n + 2)
                            else:
                                wait(pe, "vals_ready", TT * n)
                        elif h == Q_AT + 1:
                            wait(pe, "tr_copied", NU * b + TT + 1)
                        if u >= TT:
                            wait(pe, "add_done", NU * b + u + 1)
                        else:
                            wait(pe, "qs_done", TT * b + u + 1)
                        for j in range(H):
                            ins = nc.tensor.transpose(UN[1][:, j * P:(j + 1) * P],
                                                      roped[other][:, u, j * D:(j + 1) * D], ident[:, :])
                        ins.then_inc(S["tr_done"], 1)
                    if B and h in VALUES:
                        b, t = n - 1, VALUES[h]
                        if t == 0:
                            wait(pe, "tr_copied", NU * b + TT)
                        else:
                            wait(pe, "vals_ready", TT * b + t)
                        toks = slice(t * P, (t + 1) * P)
                        split_product(UN[1], h_hi[other][:, toks], h_lo[other][:, toks],
                                      wvo_hi[:, :], wvo_lo[:, :]).then_inc(S["vw_done"], 1)
                    if X and h == H_AT:
                        b = n + 1
                        if B:
                            wait(pe, "vals_ready", TT * n)
                        wait(pe, "xn_ready", TT * (b + 1))
                        for t in range(TT):
                            ins = nc.tensor.transpose(UN[1][:, t * P:(t + 1) * P], xn[:, t, :], ident[:, :])
                        ins.then_inc(S["tx_done"], 1)
                    if N2 and h == H2_AT:
                        b = n - 4
                        if B:
                            wait(pe, "tr_copied", NU * n)
                        wait(pe, "h2_ready", b + 1)
                        for t in range(TT):
                            ins = nc.tensor.transpose(UN[1][:, t * P:(t + 1) * P], rows[0][parity][:, t, 0:M],
                                                      ident[:, :])
                        ins.then_inc(S["h2t_done"], 1)
                    if C and h >= 1:
                        values_times_probs(n - 2, h - 1)
                if C:
                    values_times_probs(n - 2, H - 1)
            iterations(pe, body)
            wait(pe, "lg_ready", NB)
            wait(pe, "route_step", STEPS * NB)
            nc.tensor.matmul(UN[1][:, 0:E], ones_bf[:, :], counts[0][:, :], start=True, stop=True)\
                .then_inc(S["count_done"], 1)

        attention.close()

        phase[0] = experts = ExitStack()
        SLOTS = 4
        w1_hi = sb("w1_hi", [P, E * F], F16)
        w1_lo = sb("w1_lo", [P, E * F], F16)
        w1_sb = sb("w1_sb", [P, E * F])
        w2_sb = sb("w2_sb", [P, E * FC * M])
        b1_rows = sb("b1_rows", [E * FC, P])
        b1_t = sb("b1_t", [P, E * FC])
        b2_b = sb("b2_b", [P, E * M])
        tile_x = [sb(f"tile_x{k}", [P, TILE // P, RW]) for k in range(SLOTS)]
        place_y = [sb(f"place_y{k}", [P, TILE // P], I32) for k in range(SLOTS)]
        id_x = sb("id_x", [P, P])
        x_hi = [sb(f"x_hi{k}", [P, TILE], F16) for k in range(2)]
        x_lo = [sb(f"x_lo{k}", [P, TILE], F16) for k in range(2)]
        hidden = [sb(f"hidden{k}", [P, FC, TILE]) for k in range(2)]
        y_sum = sb("y_sum", [P, TILE // P, M])
        y_pos = sb("y_pos", [P, TILE // P, M])
        y_out = [sb(f"y_out{k}", [P, TILE // P, M]) for k in range(SLOTS)]
        XT = [ps(f"xt{k}", [P, 512]) for k in range(1)]
        UP = [ps(f"up{k}", [P, 1024]) for k in range(2)]
        DN = [ps(f"down{k}", [P, 512]) for k in range(2)]
        TS = TILE // P

        def tiles(e, body):
            def live(n):
                return [0 <= n + d < NTILES for d in (SLOTS - 1, 1, 0, -1)]
            rounds = (NTILES - SLOTS + 1) // SLOTS
            for n in range(1 - SLOTS, SLOTS):
                body(n // SLOTS, n % SLOTS, live(n))
            with e.Fori(1, rounds) as turn:
                for slot in range(SLOTS):
                    body(turn, slot, [True] * 4)
            for n in range(rounds * SLOTS, NTILES + 1):
                body(n // SLOTS, n % SLOTS, live(n))

        def round_of(turn, slot, d):
            return turn + (slot + d) // SLOTS, (slot + d) % SLOTS

        def entry(e, k, n, most):
            return e.value_load(table[0:1, k, bass.ds(n, 1)], min_val=0, max_val=most)

        block = experts.enter_context(nc.Block())

        @block.sync
        def _(sp):
            sp.dma_start(w1_sb[:, :].rearrange("c (e f) -> c e f", e=E), w1.rearrange("e c f -> c e f"))\
                .then_inc(S["w1_in"], 16)
            sp.dma_start(b1_rows[:, :], b1.rearrange("e (k p) -> (e k) p", p=P)).then_inc(S["b_in"], 16)
            sp.dma_start(b2_b[:, :], b2.rearrange("(o e) m -> o (e m)", o=1).broadcast_to([P, E * M]))\
                .then_inc(S["b_in"], 16)
            sp.dma_start(w2_sb[:, :].rearrange("p (g m) -> p g m", m=M), w2.rearrange("e (k p) m -> p (e k) m", p=P))\
                .then_inc(S["w2_in"], 16)

            def body(turn, slot, live):
                LOAD, _, _, _ = live
                if LOAD:
                    i = SLOTS * turn + slot + SLOTS - 1
                    before, at = round_of(turn, slot, SLOTS - 1)
                    row = entry(sp, 1, i, E * REGION + (SPARE - 1) * TILE)
                    alone(sp, "t_done", i - SLOTS + 1)
                    alone(sp, "places_ready", i - SLOTS + 1)
                    wait(sp, f"tile_in{at}", 16 * before)
                    sp.dma_start(tile_x[at][:, :, :], x_rows[bass.ds(row, TILE), :]
                                 .rearrange("(p s) c -> p s c", p=P)).then_inc(S[f"tile_in{at}"], 16)
            tiles(sp, body)

        @block.gpsimd
        def _(pool):
            pool.memset(id_x[:, :], 0.0).then_inc(S["consts_ready"], 1)
            pool.wait_ge(S["consts_ready"], 7)
            pool.affine_select(out=id_x[:, :], in_=id_x[:, :], compare_op=ALU.not_equal, fill=1.0,
                               base=0, pattern=[[-1, P]], channel_multiplier=1).then_inc(S["consts_ready"], 1)

            def body(turn, slot, live):
                _, _, _, DOWN = live
                if DOWN:
                    i = SLOTS * turn + slot - 1
                    at = (slot - 1) % SLOTS
                    alone(pool, "y_step", 3 * (i + 1))
                    for s in range(TS):
                        pool.indirect_dma_start(
                            out=y_rows, out_offset=bass.IndirectOffsetOnAxis(ap=place_y[at][:, s:s + 1], axis=0),
                            in_=y_out[at][:, s, :], in_offset=None, bounds_check=K * NTOK - 1, oob_is_err=False)\
                            .then_inc(S[f"y_stored{at}"], 16)
            tiles(pool, body)
            for k in range(SLOTS):
                pool.wait_ge(S[f"y_stored{k}"], 16 * TS * ((NTILES - k + SLOTS - 1) // SLOTS))

        @block.scalar
        def _(act):
            act.wait_ge(S["w1_in"], 16)
            for e in range(E):
                nc.scalar.activation(w1_hi[:, e * F:(e + 1) * F], w1_sb[:, e * F:(e + 1) * F], ACT.Copy, scale=WS)\
                    .then_inc(S["w1_hi_done"], 1)
            act.wait_ge(S["b1_ready"], 1)

            def body(turn, slot, live):
                n = SLOTS * turn + slot
                _, T1, UPW, _ = live
                parity, other = slot % 2, 1 - slot % 2
                if T1:
                    i = n + 1
                    wait(act, "t_done", i + 1)
                    wait(act, "up_done", FC * (i - 1))
                    nc.scalar.activation(x_hi[other][:, :], XT[0][:, 0:TILE], ACT.Copy).then_inc(S["x_hi_done"], 1)
                if UPW:
                    expert = entry(act, 0, n, E - 1)
                    for k in range(FC):
                        wait(act, "up_done", FC * n + k + 1)
                        wait(act, "down_done", n - 1)
                        nc.scalar.activation(hidden[parity][:, k, :], UP[k // 2][:, (k % 2) * 512:(k % 2) * 512 + TILE],
                                             ACT.Gelu, bias=b1_t[:, bass.ds(expert * FC + k, 1)], scale=1.0 / WS)\
                            .then_inc(S["gelu_done"], 1)
            tiles(act, body)

        @block.vector
        def _(dve):
            for e in range(E):
                dve.wait_ge(S["w1_hi_done"], e + 1)
                cols = slice(e * F, (e + 1) * F)
                nc.vector.scalar_tensor_tensor(out=w1_lo[:, cols], in0=w1_sb[:, cols], scalar=WS, in1=w1_hi[:, cols],
                                               op0=ALU.mult, op1=ALU.subtract).then_inc(S["w1_split"], 1)
            dve.wait_ge(S["b_in"], 32)
            dve.wait_ge(S["b1_turned"], 1)
            nc.vector.tensor_copy(b1_t[:, :], XT[0][:, 0:E * FC]).then_inc(S["b1_ready"], 1)

            def body(turn, slot, live):
                n = SLOTS * turn + slot
                _, T1, _, DOWN = live
                parity, other = slot % 2, 1 - slot % 2
                if T1:
                    i = n + 1
                    wait(dve, "x_hi_done", i + 1)
                    wait(dve, "up_done", FC * (i - 1))
                    nc.vector.tensor_tensor(out=x_lo[other][:, :], in0=XT[0][:, 0:TILE], in1=x_hi[other][:, :],
                                            op=ALU.subtract).then_inc(S["x_split"], 1)
                    before, at = round_of(turn, slot, 1)
                    wait(dve, f"y_stored{at}", 16 * TS * before)
                    nc.vector.tensor_copy(place_y[at][:, :], tile_x[at][:, :, M:RW]
                                          .rearrange("p s o -> p (s o)")).then_inc(S["places_ready"], 1)
                if DOWN:
                    i = n - 1
                    at = (slot - 1) % SLOTS
                    expert = entry(dve, 0, i, E - 1)
                    wait(dve, "down_done", i + 1)
                    wait(dve, "y_step", 3 * i)
                    nc.vector.tensor_tensor(
                        out=y_sum[:, :, :], in0=DN[other][:, 0:TILE].rearrange("p (s m) -> p s m", s=TS),
                        in1=b2_b[:, bass.ds(expert * M, M)].rearrange("p (o m) -> p o m", o=1)
                            .to_broadcast([P, TS, M]), op=ALU.add).then_inc(S["y_step"], 1)
                    wait(dve, "y_step", 3 * i + 1)
                    nc.vector.tensor_scalar(y_pos[:, :, :], y_sum[:, :, :], 0.0, None, ALU.max)\
                        .then_inc(S["y_step"], 1)
                    wait(dve, "y_step", 3 * i + 2)
                    nc.vector.scalar_tensor_tensor(out=y_out[at][:, :, :], in0=y_sum[:, :, :], scalar=0.0,
                                                   in1=y_pos[:, :, :], op0=ALU.min, op1=ALU.add)\
                        .then_inc(S["y_step"], 1)
            tiles(dve, body)

        @block.tensor
        def _(pe):
            pe.wait_ge(S["w1_split"], E)
            pe.wait_ge(S["w2_in"], 16)
            pe.wait_ge(S["consts_ready"], 8)
            pe.wait_ge(S["b_in"], 32)
            nc.tensor.transpose(XT[0][:, 0:E * FC], b1_rows[:, :], id_x[0:E * FC, 0:E * FC])\
                .then_inc(S["b1_turned"], 1)
            pe.wait_ge(S["b1_ready"], 1)

            def body(turn, slot, live):
                n = SLOTS * turn + slot
                _, T1, UPW, DOWN = live
                parity, other = slot % 2, 1 - slot % 2
                if T1:
                    i = n + 1
                    before, at = round_of(turn, slot, 1)
                    wait(pe, f"tile_in{at}", 16 * (before + 1))
                    wait(pe, "x_split", i)
                    for s in range(TS):
                        ins = nc.tensor.transpose(XT[0][:, s * P:(s + 1) * P], tile_x[at][:, s, 0:M], id_x[:, :])
                    ins.then_inc(S["t_done"], 1)
                if UPW:
                    expert = entry(pe, 0, n, E - 1)
                    wait(pe, "x_split", n + 1)
                    for k in range(FC):
                        wait(pe, "gelu_done", FC * (n - 1) + k + 1)
                        dst = UP[k // 2][:, (k % 2) * 512:(k % 2) * 512 + TILE]
                        cols = bass.ds(expert * F + k * P, P)
                        nc.tensor.matmul(dst, w1_hi[:, cols], x_hi[parity][:, :], start=True, stop=False)
                        nc.tensor.matmul(dst, w1_hi[:, cols], x_lo[parity][:, :], start=False, stop=False)
                        nc.tensor.matmul(dst, w1_lo[:, cols], x_hi[parity][:, :], start=False, stop=True)\
                            .then_inc(S["up_done"], 1)
                if DOWN:
                    i = n - 1
                    expert = entry(pe, 0, i, E - 1)
                    wait(pe, "y_step", 3 * (i - 2) + 1)
                    for s in range(TS):
                        for k in range(FC):
                            wait(pe, "gelu_done", FC * i + k + 1)
                            ins = nc.tensor.matmul(DN[other][:, s * M:(s + 1) * M],
                                                   hidden[other][:, k, s * P:(s + 1) * P],
                                                   w2_sb[:, bass.ds((expert * FC + k) * M, M)],
                                                   start=(k == 0), stop=(k == FC - 1))
                    ins.then_inc(S["down_done"], 1)
            tiles(pe, body)

        experts.close()

        phase[0] = last = ExitStack()
        back = [[sb(f"back{j}{k}", [P, TT, M]) for k in range(2)] for j in range(K)]
        gb_b = [sb(f"gb_b{k}", [P, M]) for k in range(2)]
        part = sb("part", [P, TT, M])
        mixed = sb("mixed", [P, TT, M])
        sums = [sb(f"sums{k}", [P, TT, M]) for k in range(2)]
        block = last.enter_context(nc.Block())
        MIX = 2 * TT + 2

        def batches(e, body):
            for n in range(2):
                body(0, n)
            with e.Fori(1, NB // 2) as half:
                for parity in range(2):
                    body(half, parity)

        @block.sync
        def _(sp):
            yv = y_rows.rearrange("(j g p) m -> j p g m", j=K, p=P)

            def body(half, parity):
                n = 2 * half + parity
                alone(sp, "mix_done", MIX * (n - 1))
                wait(sp, f"back_in{parity}", 16 * (K + 1) * half)
                for j in range(K):
                    sp.dma_start(back[j][parity][:, :, :], yv[j, :, bass.ds(n * TT, TT), :])\
                        .then_inc(S[f"back_in{parity}"], 16)
                sp.dma_start(gb_b[parity][:, :], mod_dram[bass.ds(n, 1), 3 * M:4 * M].broadcast_to([P, M]))\
                    .then_inc(S[f"back_in{parity}"], 16)
            batches(sp, body)

        @block.vector
        def _(dve):
            def body(half, parity):
                n = 2 * half + parity
                at = MIX * n
                dve.wait_ge(S[f"back_in{parity}"], 16 * (K + 1) * (half + 1))
                for t in range(TT):
                    w = weights[:, bass.ds(TT * n + t, 1), :].rearrange("p o k -> p (o k)")
                    nc.vector.tensor_scalar(part[:, t, :], back[0][parity][:, t, :], w[:, 0:1], None, ALU.mult)\
                        .then_inc(S["mix_done"], 1)
                for t in range(TT):
                    w = weights[:, bass.ds(TT * n + t, 1), :].rearrange("p o k -> p (o k)")
                    wait(dve, "mix_done", at + t + 1)
                    nc.vector.scalar_tensor_tensor(out=mixed[:, t, :], in0=back[1][parity][:, t, :], scalar=w[:, 1:2],
                                                   in1=part[:, t, :], op0=ALU.mult, op1=ALU.add)\
                        .then_inc(S["mix_done"], 1)
                wait(dve, "mix_done", at + 2 * TT)
                nc.vector.tensor_tensor(out=mixed[:, :, :], in0=mixed[:, :, :],
                                        in1=gb_b[parity][:, :].rearrange("p (o m) -> p o m", o=1)
                                            .to_broadcast([P, TT, M]), op=ALU.mult).then_inc(S["mix_done"], 1)
                wait(dve, "mix_done", at + 2 * TT + 1)
                wait(dve, f"out_stored{parity}", 16 * half)
                nc.vector.tensor_tensor(out=sums[parity][:, :, :], in0=mixed[:, :, :],
                                        in1=x_all[:, bass.ds(TT * n, TT), :], op=ALU.add).then_inc(S["mix_done"], 1)
            batches(dve, body)

        @block.scalar
        def _(act):
            ov = out.rearrange("b (t p) m -> p (b t) m", p=P)

            def body(half, parity):
                n = 2 * half + parity
                wait(act, "mix_done", MIX * (n + 1))
                act.dma_start(ov[:, bass.ds(TT * n, TT), :], sums[parity][:, :, :])\
                    .then_inc(S[f"out_stored{parity}"], 16)
            batches(act, body)
            for k in range(2):
                act.wait_ge(S[f"out_stored{k}"], 16 * NB // 2)
        last.close()


_INS = ["L0_attn_x", "L0_attn_wq", "L0_attn_wk", "L0_attn_wv", "L0_attn_wo", "L0_ffn_Wr", "L0_ffn_br",
        "L0_ffn_W1", "L0_ffn_b1", "L0_ffn_W2", "L0_ffn_b2", "L0_c", "L0_wmod"]


def rope_tables(length, width, base=1250.0):
    half = width // 2
    pos = np.arange(length, dtype=np.float32)[:, None]
    freqs = np.power(np.float32(base), -np.arange(half, dtype=np.float32) / np.float32(half)).astype(np.float32)
    rad = (pos * freqs[None, :]).astype(np.float32)
    cos, sin = np.cos(rad).astype(np.float32), np.sin(rad).astype(np.float32)
    return cos, np.concatenate([-sin, sin], axis=1)


def kernel(**inputs):
    import concourse.bacc as bacc
    from concourse.bass_utils import run_bass_kernel_spmd

    nc = bacc.Bacc("TRN2", target_bir_lowering=False, num_devices=1)
    arrays, args = {}, []
    given = [(name, np.ascontiguousarray(inputs[name])) for name in _INS]
    cos, sin = rope_tables(given[0][1].shape[1], given[1][1].shape[2])
    for name, a in [*given, ("rope_cos", cos), ("rope_sin", sin)]:
        arrays[f"in_{name}"] = a
        args.append(nc.dram_tensor(f"in_{name}", a.shape, mybir.dt.from_np(a.dtype), kind="ExternalInput").ap())
    args.append(nc.dram_tensor("out_x", given[0][1].shape, F32, kind="ExternalOutput").ap())
    adaln_block(nc, *args)
    r = run_bass_kernel_spmd(nc, [arrays], core_ids=[0])
    return r.results[0]["out_x"]
```

```python
import math
from contextlib import ExitStack

import numpy as np

import concourse.bass as bass
from concourse import mybir

F32 = mybir.dt.float32
F16 = mybir.dt.float16
BF16 = mybir.dt.bfloat16
I32 = mybir.dt.int32
U32 = mybir.dt.uint32
ALU = mybir.AluOpType
ACT = mybir.ActivationFunctionType
AX = mybir.AxisListType


def adaln_block(nc, x, wq, wk, wv, wo, wr, br, w1, b1, w2, b2, c, wmod, rope_cos, rope_sin, out):
    NB, T, M = x.shape
    H, D = wq.shape[1], wq.shape[2]
    P = 128
    TT = T // P
    HD = H * D
    NU = 2 * TT
    LN_EPS, RMS_EPS = 1e-5, 1e-6
    WS = 64.0
    MASKED = -1e30
    MAGIC = 0x5F3759DF
    NCH = NU * H + 2 * TT
    E = wr.shape[1]
    K = 2
    F = w1.shape[2]
    FC = F // P
    NTOK = NB * T
    NTT = NB * TT
    TILE = 2 * P
    NTILES = (K * NTOK + E * (TILE - 1)) // TILE
    ENTRIES = NTILES + 1
    SPARE = NTILES - K * NTOK // TILE
    REGION = NTOK + TILE
    RW = M + 1
    SKIP = float(1 << 20)

    ctx = ExitStack()
    with ctx:
        phase = [ctx]

        def sb(name, shape, dt=F32):
            return phase[0].enter_context(nc.sbuf_tensor(name, shape, dt))

        def ps(name, shape, dt=F32):
            return phase[0].enter_context(nc.psum_tensor(name, shape, dt))

        def sem(name):
            return ctx.enter_context(nc.semaphore(name))

        x_all = sb("x_all", [P, NB * TT, M])
        weights = sb("weights", [P, NTT, K])
        token_at = sb("token_at", [P, NTT, K])
        table = sb("table", [P, 3, ENTRIES], I32)
        counts_i = sb("counts_i", [P, E], I32)
        w1_hi = sb("w1_hi", [P, E * F], F16)
        w1_lo = sb("w1_lo", [P, E * F], F16)
        w2_hi = sb("w2_hi", [P, E * FC * M], F16)
        w2_lo = sb("w2_lo", [P, E * FC * M], F16)
        b1_t = sb("b1_t", [P, E * FC])
        b2_b = sb("b2_b", [P, E * M])
        ident = sb("ident", [P, P])
        x_rows = nc.dram_tensor("x_rows", [(E * REGION + SPARE * TILE), RW], F32).ap()
        y_rows = nc.dram_tensor("y_rows", [K * NTOK, M], F32).ap()
        mod_dram = nc.dram_tensor("mod_dram", [NB, 4 * M], F32).ap()

        phase[0] = attention = ExitStack()
        wqk_hi = sb("wqk_hi", [P, 2 * HD], F16)
        wqk_lo = sb("wqk_lo", [P, 2 * HD], F16)
        wvo_hi = sb("wvo_hi", [P, HD], F16)
        wvo_lo = sb("wvo_lo", [P, HD], F16)
        ident_bf = sb("ident_bf", [P, P], BF16)
        causal_bf = sb("causal_bf", [P, P], BF16)
        cos_sb = sb("cos_sb", [P, TT, D // 2])
        sin_sb = sb("sin_sb", [P, TT, D])
        mod_t = sb("mod_t", [P, 2, NB])
        mod_rows = sb("mod_rows", [NB, 4 * M])
        roped = [sb(f"roped{k}", [P, NU, HD]) for k in range(2)]
        wmod_sb = roped[1][:, 2, 0:6 * M]
        start = roped[1][:, 3, :]
        guard_a, guard_b = start[0:NB, 0:2 * M], start[0:NB, 2 * M:4 * M]
        c_sb, silu_c, silu_ct = start[0:NB, 4 * M:5 * M], start[0:NB, 5 * M:6 * M], start[:, 6 * M:6 * M + NB]
        b1_rows = start[0:E * FC, 6 * M + NB:7 * M + NB]
        rope_b = sb("rope_b", [P, 2, HD])
        squares = sb("squares", [P, HD])
        q_t = [sb(f"q_t{k}", [P, H, T]) for k in range(2)]
        k_t = [sb(f"k_t{k}", [P, H, T]) for k in range(2)]
        VW = D + 2
        vals = [sb(f"vals{k}", [P, TT, H, VW]) for k in range(2)]
        NPR = 4
        probs = sb("probs", [P, NPR, T + P])
        h_t = sb("h_t", [P, T])
        h_hi = [sb(f"h_hi{k}", [P, T], F16) for k in range(2)]
        h_lo = [sb(f"h_lo{k}", [P, T], F16) for k in range(2)]
        xn = sb("xn", [P, TT, M])
        acc = sb("acc", [P, TT, M])
        den = sb("den", [P, 2, TT])
        ssq = [sb(f"ssq{k}", [P, NU * H]) for k in range(2)]
        bst = sb("bst", [P, TT, 6])
        mv = [sb(f"mv{k}", [P, TT, 2]) for k in range(2)]
        vx = sb("vx", [P, NCH])
        half_bits = sb("half_bits", [P, NCH], I32)
        y_a = sb("y_a", [P, NCH])
        y_t = sb("y_t", [P, NCH])
        rr = [sb(f"rr{k}", [P, NCH]) for k in range(2)]
        ga_b = [sb(f"ga_b{k}", [P, M]) for k in range(2)]
        sbcb_b = [sb(f"sbcb_b{k}", [P, 2 * M]) for k in range(2)]
        mv2 = [sb(f"mv2{k}", [P, TT, 2]) for k in range(2)]
        bst2 = sb("bst2", [P, TT, 6])
        xn2 = sb("xn2", [P, TT, M])
        rows = [[sb(f"rows{j}{k}", [P, TT, RW]) for k in range(2)] for j in range(K)]
        h2_rows = sb("h2_rows", [P, TT, M])
        h2_t = sb("h2_t", [P, T])
        wr_sb = sb("wr_sb", [P, E])
        br_sb = sb("br_sb", [1, TT * E])
        ones_row = sb("ones_row", [1, P])
        ahead = sb("ahead", [P, TT * E])
        lg = [sb(f"lg{k}", [P, TT, E]) for k in range(2)]
        top_l = sb("top_l", [P, TT, 8])
        lg_m = sb("lg_m", [P, TT, E])
        e_lg = sb("e_lg", [P, TT, E])
        e_sum = sb("e_sum", [P, TT])
        e_rec = sb("e_rec", [P, TT])
        score = sb("score", [P, TT, E])
        top_s = sb("top_s", [P, TT, 8])
        top_i = sb("top_i", [P, TT, 8], U32)
        top_f = sb("top_f", [P, TT, K])
        gap = sb("gap", [P, TT])
        e_gap = sb("e_gap", [P, TT])
        w_den = sb("w_den", [P, TT])
        iota_e = sb("iota_e", [P, E])
        base_e = sb("base_e", [P, E])
        one_hot = sb("one_hot", [P, TT * K, E])
        chosen = sb("chosen", [P, TT, E], BF16)
        counts = [sb(f"counts{k}", [P, E], BF16) for k in range(2)]
        before_bf = sb("before_bf", [P, P], BF16)
        ones_bf = sb("ones_bf", [P, P], BF16)
        place_e = sb("place_e", [P, TT, E])
        place_k = sb("place_k", [P, TT * K, E])
        place_f = sb("place_f", [P, TT * K])
        place = [sb(f"place{k}", [P, TT * K], I32) for k in range(2)]
        ones_e = sb("ones_e", [P, E])
        iota_t = sb("iota_t", [P, ENTRIES])
        tiles_i = sb("tiles_i", [P, E], I32)
        tiles_f = sb("tiles_f", [P, E])
        tiles_to = sb("tiles_to", [P, E])
        behind = squares[:, 0:ENTRIES * E].rearrange("p (i e) -> p i e", e=E)
        tile_e = sb("tile_e", [P, ENTRIES])
        tile_r = sb("tile_r", [P, ENTRIES])
        filler = sb("filler", [P, TILE // P, RW])
        UN = [ps(f"unit{k}", [P, 2 * 512]) for k in range(2)]
        SC = [ps(f"scores{k}", [P, 512]) for k in range(2)]
        OP = [ps(f"pv{k}", [P, 512]) for k in range(2)]

        names = """w_in c_in wv_in const_in x_in0 x_in1 ga_in0 ga_in1 consts_ready ones_ready silu_done ct_done
            ct_ready mod_done mod_copied guard_done mod_stored wvt_done wvt_ready wvo_done hi_done
            split_done wvo_scaled wvo_hi_done tx_done p_done tr_done vw_done s_done o_done ht32_done
            hhi_done h_ready sq_done ropea_done rope_done add_done qs_done tr_copied vals_ready exp_done
            den_done acc_done x2_done stat_done mv_done chain_done rr_done xn_ready router_in sbcb_in0
            sbcb_in1 iota_done scattered0 scattered1 filled mv2_done stat2_done xn2_done h2_ready
            rows_copied h2t_done h2t_copied rt_done lg_ready route_step route_exp px_done count_done
            table_step ahead_copied tail_filled0 tail_filled1 gates_in b1_turned b1_ready w_ex_in0 w_ex_in1
            ex_hi_done ex_split b_in tile_in0 tile_in1 tile_in2 tile_in3 tile_in4 tile_in5 tile_in6 tile_in7
            places_ready t_done x_hi_done x_split up_done gelu_done hid_hi_done hid_split down_done y_step
            y_stored0 y_stored1 y_stored2 y_stored3 y_stored4 y_stored5 y_stored6 y_stored7 back_in0
            back_in1 back_in2 back_in3 first_done mix_done gated sum_done out_stored0 out_stored1
            out_stored2 out_stored3""".split()
        S = {n: sem(n) for n in names}

        def wait(e, name, value):
            if isinstance(value, int) and value <= 0:
                return
            e.wait_ge(S[name], value)

        counted = {}

        def alone(e, name, value):
            if isinstance(value, int):
                wait(e, name, value)
            else:
                if e not in counted:
                    counted[e] = e.alloc_register("awaited")
                e.reg_mov(counted[e], value)
                e.wait_ge(S["consts_ready"], 1)
                e.wait_ge(S[name], counted[e])

        def iterations(e, body):
            def live(n):
                return [0 <= n + d < NB for d in (2, 1, 0, -1, -2, -3, -4, -5, -6)]
            for n in range(-2, 8):
                body(n // 2, n % 2, live(n))
            with e.Fori(4, NB // 2 - 1) as half:
                for parity in range(2):
                    body(half, parity, [True] * 9)
            for n in range(NB - 2, NB + 6):
                body(n // 2, n % 2, live(n))

        (TOP_L0, TOP_L1, LESS_TOP, E_SUM, E_REC, SCORE, TOP_S0, TOP_S1, TOP_I0, TOP_I1, TOP_F, GAP, ONE_HOT, CHOSEN,
         COUNT_A, COUNT_B, W_DEN, W_FIRST, W_SECOND, TO_0, TO_1, PLACE_E, PLACE_K, PLACE_F, PLACE_I) = range(1, 26)
        STEPS = PLACE_I

        (VX_Q, VX_K, VX_X, VX_H, HALF_BITS, GUESS) = range(1, 7)
        CH = GUESS + 9
        TURNED = {0: 2, 1: 3, 5: 0, 6: 1}
        VALUES = {2: 0, 3: 1}
        H_AT, Q_AT, H2_AT = 4, 5, 7
        BESIDE = 3 * P
        HH = H // 2

        def expert_weights(n, h):
            e = n * E // 2 + h // 2
            staged, hi, lo = (k_t, w1_hi, w1_lo) if h % 2 == 0 else (q_t, w2_hi, w2_lo)
            flat = staged[n][:, :, :].rearrange("c h t -> c (h t)")
            return flat[:, (h // 2) * F:(h // 2 + 1) * F], hi[:, e * F:(e + 1) * F], lo[:, e * F:(e + 1) * F]

        def cap(v, most):
            return min(v, most) if isinstance(v, int) else v

        block = attention.enter_context(nc.Block())

        def fill_tails(e, k):
            e.wait_ge(S["table_step"], 1)
            e.wait_ge(S["filled"], 16 * SPARE)
            for expert in range(k, E, 2):
                end = e.value_load(counts_i[0:1, expert:expert + 1], min_val=0, max_val=NTOK)
                e.dma_start(x_rows[bass.ds(end + expert * REGION, TILE), :].rearrange("(p s) c -> p s c", p=P),
                            filler[:, :, :]).then_inc(S[f"tail_filled{k}"], 16)
            e.wait_ge(S[f"tail_filled{k}"], 16 * E // 2)

        @block.sync
        def _(sp):
            sp.dma_start(c_sb, c).then_inc(S["c_in"], 16)
            sp.dma_start(wmod_sb, wmod).then_inc(S["c_in"], 16)
            sp.dma_start(x_all[:, 0:TT, :], x[0].rearrange("(t p) m -> p t m", p=P)).then_inc(S["x_in0"], 16)
            sp.dma_start(x_all[:, TT:2 * TT, :], x[1].rearrange("(t p) m -> p t m", p=P)).then_inc(S["x_in1"], 16)
            sp.dma_start(roped[0][:, 2, :], wv.rearrange("m h d -> m (h d)")).then_inc(S["wv_in"], 16)
            sp.dma_start(roped[0][:, 3, :].rearrange("p (h m) -> p h m", h=H),
                         wo.rearrange("h d m -> d h m")).then_inc(S["wv_in"], 16)
            sp.dma_start(roped[0][:, 0, :], wq.rearrange("m h d -> m (h d)")).then_inc(S["w_in"], 16)
            sp.dma_start(roped[0][:, 1, :], wk.rearrange("m h d -> m (h d)")).then_inc(S["w_in"], 16)
            sp.dma_start(cos_sb[:, :, :], rope_cos.rearrange("(t p) d -> p t d", p=P)).then_inc(S["const_in"], 16)
            sp.dma_start(sin_sb[:, :, :], rope_sin.rearrange("(t p) d -> p t d", p=P)).then_inc(S["const_in"], 16)
            sp.dma_start(wr_sb[:, :], wr).then_inc(S["router_in"], 16)
            for t in range(TT):
                sp.dma_start(br_sb[:, t * E:(t + 1) * E], br.rearrange("(o e) -> o e", o=1))\
                    .then_inc(S["router_in"], 16)
            sp.dma_start(b1_rows, b1.rearrange("e (k p) -> (e k) p", p=P)).then_inc(S["b_in"], 16)
            sp.dma_start(b2_b[:, :], b2.rearrange("(o e) m -> o (e m)", o=1).broadcast_to([P, E * M]))\
                .then_inc(S["b_in"], 16)
            for k in range(2):
                mine = slice(k * E // 2, (k + 1) * E // 2)
                sp.dma_start(k_t[k][:, :, :].rearrange("c h t -> c (h t)").rearrange("c (e f) -> c e f", f=F),
                             w1[mine].rearrange("e c f -> c e f")).then_inc(S[f"w_ex_in{k}"], 16)
                sp.dma_start(q_t[k][:, :, :].rearrange("c h t -> c (h t)").rearrange("c (g m) -> c g m", m=M),
                             w2[mine].rearrange("e (j p) m -> p (e j) m", p=P)).then_inc(S[f"w_ex_in{k}"], 16)
            sp.wait_ge(S["iota_done"], 12)
            for k in range(SPARE):
                r0 = E * REGION + k * TILE
                sp.dma_start(x_rows[r0:r0 + TILE, :].rearrange("(p s) c -> p s c", p=P), filler[:, :, :])\
                    .then_inc(S["filled"], 16)
            sp.wait_ge(S["guard_done"], 5)
            sp.dma_start(mod_dram, mod_rows[:, :]).then_inc(S["mod_stored"], 16)
            sp.wait_ge(S["mod_stored"], 16)
            for parity in range(2):
                sp.dma_start(ga_b[parity][:, :], mod_dram[parity:parity + 1, 0:M].broadcast_to([P, M]))\
                    .then_inc(S[f"ga_in{parity}"], 16)
                sp.dma_start(sbcb_b[parity][:, :], mod_dram[parity:parity + 1, M:3 * M].broadcast_to([P, 2 * M]))\
                    .then_inc(S[f"sbcb_in{parity}"], 16)
            xv = x.rearrange("b (t p) m -> p (b t) m", p=P)
            with sp.Fori(1, NB // 2) as half:
                for parity in range(2):
                    sp.wait_ge(S[f"x_in{parity}"], 16 * half)
                    sp.dma_start(x_all[:, bass.ds(half * (2 * TT) + parity * TT, TT), :],
                                 xv[:, bass.ds(half * (2 * TT) + parity * TT, TT), :])\
                        .then_inc(S[f"x_in{parity}"], 16)
            with sp.Fori(1, NB // 2) as half:
                for parity in range(2):
                    row = bass.ds(half * 2 + parity, 1)
                    alone(sp, "x2_done", 4 * half + 2 * parity - 2)
                    sp.wait_ge(S[f"ga_in{parity}"], 16 * half)
                    sp.dma_start(ga_b[parity][:, :], mod_dram[row, 0:M].broadcast_to([P, M]))\
                        .then_inc(S[f"ga_in{parity}"], 16)
                    sp.wait_ge(S["h2_ready"], 2 * half + parity - 1)
                    sp.wait_ge(S[f"sbcb_in{parity}"], 16 * half)
                    sp.dma_start(sbcb_b[parity][:, :], mod_dram[row, M:3 * M].broadcast_to([P, 2 * M]))\
                        .then_inc(S[f"sbcb_in{parity}"], 16)
            fill_tails(sp, 0)

        @block.gpsimd
        def _(pool):
            pool.memset(ident[:, :], 0.0).then_inc(S["consts_ready"], 1)
            pool.memset(ident_bf[:, :], 0.0).then_inc(S["consts_ready"], 1)
            pool.memset(causal_bf[:, :], 0.0).then_inc(S["consts_ready"], 1)
            pool.wait_ge(S["consts_ready"], 3)
            for tile in (ident, ident_bf):
                pool.affine_select(out=tile[:, :], in_=tile[:, :], compare_op=ALU.not_equal, fill=1.0,
                                   base=0, pattern=[[-1, P]], channel_multiplier=1).then_inc(S["consts_ready"], 1)
            pool.affine_select(out=causal_bf[:, :], in_=causal_bf[:, :], compare_op=ALU.is_ge, fill=MASKED,
                               base=0, pattern=[[1, P]], channel_multiplier=-1).then_inc(S["consts_ready"], 1)
            pool.memset(before_bf[:, :], 0.0).then_inc(S["iota_done"], 1)
            pool.memset(filler[:, :, :], 0.0).then_inc(S["iota_done"], 1)
            pool.iota(token_at[:, :, :], pattern=[[P, NTT], [NTOK, K]], base=0, channel_multiplier=1,
                      allow_small_or_imprecise_dtypes=True).then_inc(S["iota_done"], 1)
            pool.iota(iota_e[:, :], pattern=[[1, E]], base=0, channel_multiplier=0,
                      allow_small_or_imprecise_dtypes=True).then_inc(S["iota_done"], 1)
            pool.wait_ge(S["iota_done"], 2)
            pool.affine_select(out=before_bf[:, :], in_=before_bf[:, :], compare_op=ALU.is_ge, fill=1.0,
                               base=0, pattern=[[-1, P]], channel_multiplier=1).then_inc(S["iota_done"], 1)
            pool.memset(filler[:, :, M:RW], SKIP).then_inc(S["iota_done"], 1)
            pool.iota(base_e[:, :], pattern=[[REGION, E]], base=0, channel_multiplier=0,
                      allow_small_or_imprecise_dtypes=True).then_inc(S["iota_done"], 1)
            pool.memset(ones_e[:, :], 1.0).then_inc(S["iota_done"], 1)
            pool.iota(iota_t[:, :], pattern=[[1, ENTRIES]], base=0, channel_multiplier=0,
                      allow_small_or_imprecise_dtypes=True).then_inc(S["iota_done"], 1)
            pool.memset(ones_bf[:, :], 1.0).then_inc(S["iota_done"], 1)
            pool.memset(ones_row[:, :], 1.0).then_inc(S["iota_done"], 1)
            pool.memset(counts[0][:, :], 0.0).then_inc(S["iota_done"], 1)
            for k in range(2):
                pool.memset(mv2[k][:, :, :], 1.0).then_inc(S["ones_ready"], 1)
                pool.memset(vals[k][:, :, :, D:VW], 1.0).then_inc(S["ones_ready"], 1)
                pool.memset(ssq[k][:, :], 1.0).then_inc(S["ones_ready"], 1)
                pool.memset(mv[k][:, :, :], 1.0).then_inc(S["ones_ready"], 1)

            def body(half, parity, live):
                n = 2 * half + parity
                _, _, A, B, _, _, _, _, ST = live

                def add(h):
                    u, heads = h // 2, slice(h % 2 * HH * D, (h % 2 + 1) * HH * D)
                    wait(pool, "rope_done", 2 * NU * n + h + 1)
                    pool.tensor_tensor(out=roped[parity][:, u, heads], in0=roped[parity][:, u, heads],
                                       in1=rope_b[:, u % 2, heads], op=ALU.add).then_inc(S["add_done"], 1)
                if A:
                    add(0)
                    add(1)
                if B:
                    b = n - 1
                    wait(pool, "rr_done", n + 2)
                    wait(pool, "add_done", cap(H * n + 2, H * NB))
                    for t in range(TT):
                        v = roped[1 - parity][:, t, :].rearrange("p (h d) -> p h d", h=H)
                        r = rr[1 - parity][:, t * H:(t + 1) * H].rearrange("p (h o) -> p h o", o=1)\
                            .to_broadcast([P, H, D])
                        pool.tensor_tensor(out=v, in0=v, in1=r, op=ALU.mult).then_inc(S["qs_done"], 1)
                if ST:
                    b = n - 6
                    alone(pool, "route_step", STEPS * (b + 1))
                    alone(pool, "rows_copied", K * (b + 1))
                    for t in range(TT):
                        for j in range(K):
                            at = place[parity][:, t * K + j:t * K + j + 1]
                            pool.indirect_dma_start(
                                out=x_rows, out_offset=bass.IndirectOffsetOnAxis(ap=at, axis=0),
                                in_=rows[j][parity][:, t, :], in_offset=None)\
                                .then_inc(S[f"scattered{parity}"], 16)
                if A:
                    for h in range(2, H):
                        add(h)
            iterations(pool, body)
            for k in range(2):
                pool.wait_ge(S[f"scattered{k}"], 16 * TT * K * NB // 2)

        @block.scalar
        def _(act):
            act.wait_ge(S["c_in"], 32)
            nc.scalar.activation(silu_c, c_sb, ACT.Silu).then_inc(S["silu_done"], 1)
            act.wait_ge(S["w_in"], 32)
            for k in range(2):
                nc.scalar.activation(wqk_hi[:, k * HD:(k + 1) * HD], roped[0][:, k, :], ACT.Copy, scale=WS)\
                    .then_inc(S["hi_done"], 1)
            act.wait_ge(S["wvt_done"], 1)
            nc.scalar.activation(roped[1][:, 0, :], UN[0][:, :], ACT.Copy).then_inc(S["wvt_ready"], 1)
            act.wait_ge(S["wvo_done"], 1)
            nc.scalar.activation(roped[1][:, 1, :], UN[1][:, :], ACT.Copy, scale=WS).then_inc(S["wvo_scaled"], 1)
            act.wait_ge(S["wvo_scaled"], 1)
            nc.scalar.activation(wvo_hi[:, :], roped[1][:, 1, :], ACT.Copy).then_inc(S["wvo_hi_done"], 1)
            act.wait_ge(S["ones_ready"], 8)
            act.wait_ge(S["mod_copied"], 2)

            def body(half, parity, live):
                n = 2 * half + parity
                _, X, A, B, C, _, N2, RT, ST = live
                for h in range(H):
                    if C:
                        b = n - 2
                        g = H * b + h
                        if h == 0:
                            wait(act, "rr_done", b + 3)
                        wait(act, "s_done", g + 1)
                        wait(act, "o_done", g - NPR + 1)
                        wait(act, "exp_done", 2 * (g - NPR + 1))
                        r = rr[parity]
                        kc = TT * H + h
                        nc.scalar.activation(probs[:, h % NPR, 0:T], SC[h % 2][:, 0:T], ACT.Exp,
                                             scale=r[:, kc:kc + 1]).then_inc(S["exp_done"], 1)
                        nc.scalar.activation(probs[:, h % NPR, T:T + P], SC[h % 2][:, T:T + P], ACT.Exp,
                                             scale=r[:, kc + H:kc + H + 1]).then_inc(S["exp_done"], 1)
                    if isinstance(n, int) and n in (0, 1):
                        staged, hi, _ = expert_weights(n, h)
                        wait(act, f"w_ex_in{n}", 32)
                        nc.scalar.activation(hi, staged, ACT.Copy, scale=WS).then_inc(S["ex_hi_done"], 1)
                    if ST and h == 0:
                        wait(act, "px_done", n - 5)
                        nc.scalar.activation(ahead[:, :], SC[0][:, BESIDE:BESIDE + TT * E], ACT.Copy)\
                            .then_inc(S["ahead_copied"], 1)
                    if RT and h == 1:
                        b = n - 5
                        wait(act, "rt_done", b + 1)
                        nc.scalar.activation(lg[1 - parity][:, :, :].rearrange("p t e -> p (t e)"),
                                             SC[1][:, BESIDE:BESIDE + TT * E], ACT.Copy).then_inc(S["lg_ready"], 1)
                    if X and h == H_AT:
                        b = n + 1
                        wait(act, "tx_done", b + 1)
                        wait(act, "h_ready", b)
                        nc.scalar.activation(h_t[:, :], UN[1][:, 0:T], ACT.Identity,
                                             scale=mod_t[:, 1, bass.ds(b, 1)],
                                             bias=mod_t[:, 0, bass.ds(b, 1)]).then_inc(S["ht32_done"], 1)
                        wait(act, "ht32_done", b + 1)
                        wait(act, "vw_done", TT * (b - 1))
                        nc.scalar.activation(h_hi[1 - parity][:, :], h_t[:, :], ACT.Copy)\
                            .then_inc(S["hhi_done"], 1)
                    if A:
                        w, u = 2 * NU * n + h, h // 2
                        wait(act, "p_done", w + 1)
                        wait(act, "sq_done", HH * (w - 1))
                        if h == 0:
                            wait(act, "chain_done", (CH - 1) * n + 2)
                        for j in range(HH):
                            c = HH * (h % 2) + j
                            nc.scalar.activation(squares[:, c * D:(c + 1) * D], UN[0][:, c * D:(c + 1) * D],
                                                 ACT.Square, accum_out=ssq[parity][:, u * H + c:u * H + c + 1])\
                                .then_inc(S["sq_done"], 1)
                    if B and h in TURNED:
                        b = n - 1
                        u = TURNED[h]
                        t = u % TT
                        dst = (q_t if u < TT else k_t)[1 - parity]
                        wait(act, "tr_done", NU * b + list(TURNED).index(h) + 1)
                        wait(act, "s_done", H * (b - 1))
                        if isinstance(n, int) and n in (1, 2):
                            wait(act, "ex_split", H * n)
                        nc.scalar.activation(dst[:, :, t * P:(t + 1) * P],
                                             UN[1][:, :].rearrange("p (h c) -> p h c", h=H), ACT.Copy)\
                            .then_inc(S["tr_copied"], 1)
                    if B and h in VALUES:
                        b, t = n - 1, VALUES[h]
                        wait(act, "vw_done", TT * b + t + 1)
                        wait(act, "o_done", H * (b - 1))
                        nc.scalar.activation(vals[1 - parity][:, t, :, 0:D],
                                             UN[1][:, :].rearrange("p (h c) -> p h c", h=H), ACT.Copy,
                                             scale=1.0 / WS).then_inc(S["vals_ready"], 1)
                    if RT and h == 2:
                        b = n - 5
                        wait(act, "h2_ready", b + 1)
                        if not isinstance(b, int) or b >= 2:
                            act.wait_ge(S[f"scattered{1 - parity}"], 16 * TT * K * (half + (parity - 7) // 2 + 1))
                        for j in range(K):
                            nc.scalar.activation(rows[j][1 - parity][:, :, 0:M], h2_rows[:, :, :], ACT.Copy)\
                                .then_inc(S["rows_copied"], 1)
                    if RT and h in (3, 6):
                        b = n - 5
                        src, dst, after = ((lg_m, e_lg, LESS_TOP) if h == 3 else (gap, e_gap, GAP))
                        wait(act, "route_step", STEPS * b + after)
                        nc.scalar.activation(dst[:], src[:], ACT.Exp).then_inc(S["route_exp"], 1)
                    if N2 and h == H2_AT:
                        b = n - 4
                        wait(act, "h2t_done", b + 1)
                        wait(act, "rt_done", b)
                        nc.scalar.activation(h2_t[:, :], UN[1][:, 0:T], ACT.Copy).then_inc(S["h2t_copied"], 1)
            iterations(act, body)
            fill_tails(act, 1)

        @block.vector
        def _(dve):
            dve.wait_ge(S["ct_done"], 1)
            nc.vector.tensor_copy(silu_ct, OP[0][:, 0:NB]).then_inc(S["ct_ready"], 1)
            dve.wait_ge(S["mod_done"], 1)
            nc.vector.tensor_copy(mod_t[:, 0, :], SC[0][:, 0:NB]).then_inc(S["mod_copied"], 1)
            nc.vector.tensor_scalar(mod_t[:, 1, :], SC[0][:, NB:2 * NB], 1.0, None, ALU.add).then_inc(S["mod_copied"], 1)
            nc.vector.tensor_copy(mod_rows[:, :], SC[1][0:NB, :]).then_inc(S["mod_copied"], 1)
            dve.wait_ge(S["mod_copied"], 3)
            gates = mod_rows[:, :].rearrange("b (j m) -> b j m", j=4)[:, 0:4:3, :]
            ga3 = guard_a.rearrange("b (j m) -> b j m", j=2)
            gb3 = guard_b.rearrange("b (j m) -> b j m", j=2)
            nc.vector.tensor_scalar(ga3, gates, 0.0, 2.0, ALU.is_ge, ALU.mult).then_inc(S["guard_done"], 1)
            nc.vector.scalar_tensor_tensor(out=gb3, in0=gates, scalar=-1.0, in1=gates, op0=ALU.mult, op1=ALU.max)\
                .then_inc(S["guard_done"], 1)
            nc.vector.tensor_scalar(mod_rows[:, 2 * M:3 * M], mod_rows[:, 2 * M:3 * M], 1.0, None, ALU.add)\
                .then_inc(S["guard_done"], 1)
            dve.wait_ge(S["guard_done"], 3)
            nc.vector.tensor_scalar(ga3, ga3, 1.0, None, ALU.subtract).then_inc(S["guard_done"], 1)
            dve.wait_ge(S["guard_done"], 4)
            nc.vector.scalar_tensor_tensor(out=gates, in0=gb3, scalar=0.25, in1=ga3, op0=ALU.max, op1=ALU.mult)\
                .then_inc(S["guard_done"], 1)
            dve.wait_ge(S["hi_done"], 2)
            for k in range(2):
                nc.vector.scalar_tensor_tensor(out=wqk_lo[:, k * HD:(k + 1) * HD], in0=roped[0][:, k, :], scalar=WS,
                                               in1=wqk_hi[:, k * HD:(k + 1) * HD], op0=ALU.mult, op1=ALU.subtract)\
                    .then_inc(S["split_done"], 1)
            dve.wait_ge(S["ones_ready"], 8)
            dve.wait_ge(S["const_in"], 32)
            dve.wait_ge(S["iota_done"], 12)
            dve.wait_ge(S["router_in"], 16 * (TT + 1))

            NEWTON = range(GUESS + 1, CH + 1)
            SMALL = {
                (0, 0): (VX_Q, VX_K, VX_X, VX_H),
                (0, 1): (HALF_BITS,), (0, 2): (GUESS,), (0, 3): NEWTON[0:1], (0, 4): NEWTON[1:2],
                (1, 0): NEWTON[2:3], (1, 1): NEWTON[3:4], (1, 2): NEWTON[4:5], (1, 3): NEWTON[5:6],
                (1, 4): NEWTON[6:7], (2, 0): NEWTON[7:8], (2, 1): NEWTON[8:9]}
            ROUTE = {
                (2, 3): (TOP_L0, TOP_L1), (2, 4): (LESS_TOP,),
                (3, 3): (E_SUM,), (3, 4): (E_REC,), (4, 1): (SCORE,), (4, 3): (TOP_S0, TOP_S1),
                (5, 0): (TOP_I0, TOP_I1), (5, 1): (TOP_F, GAP), (5, 2): (ONE_HOT,), (5, 3): (CHOSEN,),
                (6, 1): (COUNT_A,), (6, 3): (COUNT_B,), (7, 0): (W_DEN,), (7, 1): (W_FIRST,),
                (7, 2): (W_SECOND,), (7, 3): (TO_0, TO_1)}
            STORE = {(1, 0): (PLACE_E,), (1, 1): (PLACE_K,), (1, 2): (PLACE_F,), (1, 3): (PLACE_I,)}

            def body(half, parity, live):
                n = 2 * half + parity
                L, X, A, _, C, R, N2, RT, ST = live
                other = 1 - parity
                chain = X or A or live[3] or C or R or N2
                r = rr[other]

                def root(k):
                    base = (CH - 1) * (n + 1)
                    s = WS * WS * RMS_EPS
                    if k == VX_Q:
                        wait(dve, "sq_done", cap(NU * H * n, NU * H * NB))
                        wait(dve, "mv2_done", TT * (n - 3))
                        wait(dve, "mv_done", cap(TT * (n + 2), TT * NB))
                        wait(dve, "chain_done", base)
                        ins = nc.vector.tensor_scalar(vx[:, 0:TT * H], ssq[other][:, 0:TT * H], 1.0 / D, s,
                                                      ALU.mult, ALU.add)
                    elif k == VX_K:
                        ins = nc.vector.tensor_scalar(vx[:, TT * H:NU * H], ssq[other][:, TT * H:NU * H], float(D),
                                                      s * D * D, ALU.mult, ALU.add)
                    elif k in (VX_X, VX_H):
                        m = mv[other] if k == VX_X else mv2[parity]
                        c0 = NU * H + (k - VX_X) * TT
                        ins = nc.vector.tensor_scalar(vx[:, c0:c0 + TT], m[:, :, 1:2].rearrange("p t o -> p (t o)"),
                                                      LN_EPS, None, ALU.add)
                    elif k == HALF_BITS:
                        wait(dve, "chain_done", base + VX_H)
                        ins = nc.vector.tensor_scalar(half_bits[:, :], vx[:, :].bitcast(I32), 1, None,
                                                      ALU.logical_shift_right)
                    elif k == GUESS:
                        wait(dve, "chain_done", base + HALF_BITS)
                        ins = nc.vector.tensor_scalar(y_a[:, :].bitcast(I32), half_bits[:, :], -1.0, float(MAGIC),
                                                      ALU.mult, ALU.add)
                    else:
                        wait(dve, "chain_done", base + k - 1)
                        part_of_step = (k - NEWTON[0]) % 3
                        if part_of_step == 0:
                            ins = nc.vector.scalar_tensor_tensor(out=y_t[:, :], in0=y_a[:, :], scalar=-0.5,
                                                                 in1=y_a[:, :], op0=ALU.mult, op1=ALU.mult)
                        elif part_of_step == 1:
                            ins = nc.vector.tensor_tensor(out=y_t[:, :], in0=y_t[:, :], in1=vx[:, :], op=ALU.mult)
                        else:
                            if k == CH:
                                wait(dve, "exp_done", cap(2 * H * (n - 2), 2 * H * NB))
                            dst = r if k == CH else y_a
                            ins = nc.vector.scalar_tensor_tensor(out=dst[:, :], in0=y_t[:, :], scalar=1.5,
                                                                 in1=y_a[:, :], op0=ALU.add, op1=ALU.mult)
                            if k == CH:
                                ins.then_inc(S["rr_done"], 1)
                                return
                    ins.then_inc(S["chain_done"], 1)

                def normalise():
                    if X:
                        b = n + 1
                        wait(dve, "rr_done", b + 1)
                        wait(dve, "tx_done", b)
                        for t in range(TT):
                            nc.vector.tensor_scalar(xn[:, t, :], x_all[:, bass.ds(TT * b + t, 1), :]
                                                    .rearrange("p o m -> p (o m)"), mv[other][:, t, 0:1],
                                                    r[:, NU * H + t:NU * H + t + 1], ALU.subtract, ALU.mult)\
                                .then_inc(S["xn_ready"], 1)

                def normalise2():
                    if N2:
                        wait(dve, "rr_done", n + 2)
                        for t in range(TT):
                            c0 = NU * H + TT + t
                            nc.vector.tensor_scalar(xn2[:, t, :], x_all[:, bass.ds(TT * (n - 4) + t, 1), :]
                                                    .rearrange("p o m -> p (o m)"), mv2[parity][:, t, 0:1],
                                                    r[:, c0:c0 + 1], ALU.subtract, ALU.mult)\
                                .then_inc(S["xn2_done"], 1)

                def modulate(b, step):
                    row = sbcb_b[parity][:, (1 - step) * M:(2 - step) * M].rearrange("p (o m) -> p o m", o=1)\
                        .to_broadcast([P, TT, M])
                    if step == 0:
                        wait(dve, "xn2_done", 3 * b + 2)
                        dve.wait_ge(S[f"sbcb_in{parity}"], 16 * (half - 1))
                        nc.vector.tensor_tensor(out=xn2[:, :, :], in0=xn2[:, :, :], in1=row, op=ALU.mult)\
                            .then_inc(S["xn2_done"], 1)
                    else:
                        wait(dve, "xn2_done", 3 * b + 3)
                        wait(dve, "h2t_done", b)
                        wait(dve, "rows_copied", K * b)
                        nc.vector.tensor_tensor(out=h2_rows[:, :, :], in0=xn2[:, :, :], in1=row,
                                                op=ALU.add).then_inc(S["h2_ready"], 1)

                def route(b, step):
                    at = STEPS * b

                    def after(k):
                        own = alone if step in (TOP_S0, TOP_S1, TOP_I0, TOP_I1) else wait
                        own(dve, "route_step", at + k)

                    def each_t(v):
                        return v.rearrange("p (t o) -> p t o", o=1)
                    if step in (TOP_L0, TOP_L1):
                        t = step - TOP_L0
                        if t == 0:
                            alone(dve, "lg_ready", b + 1)
                        ins = nc.vector.max(top_l[:, t, :], lg[other][:, t, :])
                    elif step == LESS_TOP:
                        after(TOP_L1)
                        wait(dve, "route_exp", 2 * b)
                        ins = nc.vector.tensor_tensor(out=lg_m[:, :, :], in0=lg[other][:, :, :],
                                                      in1=top_l[:, :, 0:1].to_broadcast([P, TT, E]), op=ALU.subtract)
                    elif step == E_SUM:
                        wait(dve, "route_exp", 2 * b + 1)
                        ins = nc.vector.tensor_reduce(out=e_sum[:, :], in_=e_lg[:, :, :], op=ALU.add, axis=AX.X)
                    elif step == E_REC:
                        after(E_SUM)
                        ins = nc.vector.reciprocal(e_rec[:, :], e_sum[:, :])
                    elif step == SCORE:
                        after(E_REC)
                        ins = nc.vector.tensor_tensor(out=score[:, :, :], in0=e_lg[:, :, :],
                                                      in1=each_t(e_rec[:, :]).to_broadcast([P, TT, E]), op=ALU.mult)
                    elif step in (TOP_S0, TOP_S1):
                        t = step - TOP_S0
                        after(SCORE)
                        ins = nc.vector.max(top_s[:, t, :], score[:, t, :])
                    elif step in (TOP_I0, TOP_I1):
                        t = step - TOP_I0
                        after(TOP_S0 + t)
                        ins = nc.vector.max_index(top_i[:, t, :], top_s[:, t, :], score[:, t, :])
                    elif step == TOP_F:
                        after(TOP_I1)
                        ins = nc.vector.tensor_copy(top_f[:, :, :], top_i[:, :, 0:K])
                    elif step == GAP:
                        after(TOP_S1)
                        ins = nc.vector.tensor_tensor(out=each_t(gap[:, :]), in0=top_s[:, :, 1:2],
                                                      in1=top_s[:, :, 0:1], op=ALU.subtract)
                    elif step == ONE_HOT:
                        after(TOP_F)
                        ins = nc.vector.tensor_tensor(
                            out=one_hot[:, :, :],
                            in0=iota_e[:, :].rearrange("p (o e) -> p o e", o=1).to_broadcast([P, TT * K, E]),
                            in1=top_f[:, :, :].rearrange("p t (j o) -> p (t j) o", o=1)
                                .to_broadcast([P, TT * K, E]), op=ALU.is_equal)
                    elif step == CHOSEN:
                        after(ONE_HOT)
                        wait(dve, "px_done", b)
                        oh = one_hot[:, :, :].rearrange("p (t j) e -> p t j e", j=K)
                        ins = nc.vector.tensor_tensor(out=chosen[:, :, :], in0=oh[:, :, 0, :], in1=oh[:, :, 1, :],
                                                      op=ALU.add)
                    elif step == COUNT_A:
                        after(CHOSEN)
                        ins = nc.vector.tensor_tensor(out=counts[parity][:, :], in0=counts[other][:, :],
                                                      in1=chosen[:, 0, :], op=ALU.add)
                    elif step == COUNT_B:
                        after(COUNT_A)
                        ins = nc.vector.tensor_tensor(out=counts[parity][:, :], in0=counts[parity][:, :],
                                                      in1=chosen[:, 1, :], op=ALU.add)
                    elif step == W_DEN:
                        wait(dve, "route_exp", 2 * b + 2)
                        ins = nc.vector.tensor_scalar(w_den[:, :], e_gap[:, :], 1.0, None, ALU.add)
                    elif step == W_FIRST:
                        after(W_DEN)
                        ins = nc.vector.reciprocal(weights[:, bass.ds(TT * b, TT), 0:1], each_t(w_den[:, :]))
                    elif step == W_SECOND:
                        after(W_FIRST)
                        ins = nc.vector.tensor_tensor(out=weights[:, bass.ds(TT * b, TT), 1:2],
                                                      in0=weights[:, bass.ds(TT * b, TT), 0:1],
                                                      in1=each_t(e_gap[:, :]), op=ALU.mult)
                    elif step in (TO_0, TO_1):
                        j = step - TO_0
                        wait(dve, "rows_copied", K * (b + 1))
                        ins = nc.vector.tensor_copy(rows[j][other][:, :, M:RW],
                                                    token_at[:, bass.ds(TT * b, TT), j:j + 1])
                    elif step == PLACE_E:
                        wait(dve, "ahead_copied", b + 1)
                        ins = nc.vector.tensor_tensor(
                            out=place_e[:, :, :], in0=ahead[:, :].rearrange("p (t e) -> p t e", t=TT),
                            in1=base_e[:, :].rearrange("p (o e) -> p o e", o=1).to_broadcast([P, TT, E]), op=ALU.add)
                    elif step == PLACE_K:
                        after(PLACE_E)
                        pe3 = place_e[:, :, :].rearrange("p t (o e) -> p t o e", o=1).to_broadcast([P, TT, K, E])
                        ins = nc.vector.tensor_tensor(
                            out=place_k[:, :, :].rearrange("p (t j) e -> p t j e", j=K),
                            in0=one_hot[:, :, :].rearrange("p (t j) e -> p t j e", j=K), in1=pe3, op=ALU.mult)
                    elif step == PLACE_F:
                        after(PLACE_K)
                        ins = nc.vector.tensor_reduce(out=place_f[:, :], in_=place_k[:, :, :], op=ALU.add, axis=AX.X)
                    elif step == PLACE_I:
                        after(PLACE_F)
                        ins = nc.vector.tensor_copy(place[parity][:, :], place_f[:, :])
                    ins.then_inc(S["route_step"], 1)

                def denominators(b, h):
                    wait(dve, "o_done", H * b + h + 1)
                    o = OP[h % 2][:, :].rearrange("p (t c) -> p t c", t=TT)
                    nc.vector.reciprocal(den[:, h % 2, :], o[:, :, D:D + 1].rearrange("p t o -> p (t o)"))\
                        .then_inc(S["den_done"], 1)

                def add_head(b, h, t):
                    g = H * b + h
                    o = OP[h % 2][:, :].rearrange("p (t c) -> p t c", t=TT)
                    wait(dve, "den_done", g + 1)
                    if h == 0:
                        if t == 0:
                            wait(dve, "x2_done", 2 * b)
                        ins = nc.vector.tensor_scalar(acc[:, t, :], o[:, t, 0:M], den[:, h % 2, t:t + 1], None,
                                                      ALU.mult)
                    else:
                        wait(dve, "acc_done", TT * (g - 1) + t + 1)
                        ins = nc.vector.scalar_tensor_tensor(out=acc[:, t, :], in0=o[:, t, 0:M],
                                                             scalar=den[:, h % 2, t:t + 1], in1=acc[:, t, :],
                                                             op0=ALU.mult, op1=ALU.add)
                    ins.then_inc(S["acc_done"], 1)

                def small(h, slot):
                    for k in SMALL.get((h, slot), ()):
                        if chain:
                            root(k)
                    for k in STORE.get((h, slot), ()):
                        if ST:
                            route(n - 6, k)
                    for k in ROUTE.get((h, slot), ()):
                        if RT:
                            route(n - 5, k)

                for h in range(H):
                    w, u, bank = 2 * NU * n + h, h // 2, h % 2
                    t = u % TT
                    heads = slice(bank * HH * D, (bank + 1) * HH * D)
                    adds, ended = (C, (n - 2, h - 1)) if h else (R, (n - 3, H - 1))
                    if adds:
                        denominators(*ended)
                    small(h, 0)
                    if R and h == 1:
                        b = n - 3
                        xs = x_all[:, bass.ds(TT * b, TT), :]
                        wait(dve, "x2_done", 2 * b + 1)
                        nc.vector.tensor_tensor(out=xs, in0=xs, in1=acc[:, :, :], op=ALU.add)\
                            .then_inc(S["x2_done"], 1)
                    if A:
                        wait(dve, "sq_done", HH * (w + 1))
                        wait(dve, "tr_done", NU * (n - 1))
                        nc.vector.tensor_tensor(
                            out=roped[parity][:, u, heads].rearrange("p (g c) -> p g c", c=D // 2),
                            in0=UN[0][:, heads].rearrange("p (g c) -> p g c", c=D // 2),
                            in1=cos_sb[:, t:t + 1, :].to_broadcast([P, 2 * HH, D // 2]),
                            op=ALU.mult).then_inc(S["ropea_done"], 1)
                    small(h, 1)
                    if adds:
                        add_head(*ended, 0)
                    small(h, 2)
                    if adds:
                        add_head(*ended, 1)
                    small(h, 3)
                    if A:
                        wait(dve, "add_done", w - 3)
                        nc.vector.tensor_tensor(
                            out=rope_b[:, u % 2, heads].rearrange("p (h s c) -> p h s c", h=HH, s=2),
                            in0=UN[0][:, heads].rearrange("p (h s c) -> p h s c", h=HH, s=2)[:, :, ::-1, :],
                            in1=sin_sb[:, t, :].rearrange("p (o s c) -> p o s c", o=1, s=2)
                                .to_broadcast([P, HH, 2, D // 2]),
                            op=ALU.mult).then_inc(S["rope_done"], 1)
                    small(h, 4)
                    if isinstance(n, int) and n in (0, 1):
                        staged, hi, lo = expert_weights(n, h)
                        wait(dve, "ex_hi_done", H * n + h + 1)
                        nc.vector.scalar_tensor_tensor(out=lo, in0=staged, scalar=WS, in1=hi, op0=ALU.mult,
                                                       op1=ALU.subtract).then_inc(S["ex_split"], 1)
                    if R and h == 0:
                        b = n - 3
                        wait(dve, "acc_done", H * TT * (b + 1))
                        dve.wait_ge(S[f"ga_in{other}"], 16 * (half + (parity - 3) // 2 + 1))
                        nc.vector.tensor_tensor(
                            out=acc[:, :, :], in0=acc[:, :, :],
                            in1=ga_b[other][:, :].rearrange("p (o m) -> p o m", o=1).to_broadcast([P, TT, M]),
                            op=ALU.mult).then_inc(S["x2_done"], 1)
                    if h == 2:
                        normalise()
                    if h == 3:
                        normalise2()
                    if R and h in (2, 3):
                        b = n - 3
                        for t in range(TT):
                            if h == 2:
                                alone(dve, "x2_done", 2 * b + 2)
                                nc.vector.bn_stats(bst2[:, t, :], x_all[:, bass.ds(TT * b + t, 1), :]
                                                   .rearrange("p o m -> p (o m)")).then_inc(S["stat2_done"], 1)
                            else:
                                alone(dve, "stat2_done", TT * b + t + 1)
                                nc.vector.bn_aggr(mv2[other][:, t, :], bst2[:, t, :]).then_inc(S["mv2_done"], 1)
                    if N2 and h in (4, 5):
                        modulate(n - 4, h - 4)
                    if L and h == 6:
                        b = n + 2
                        alone(dve, f"x_in{parity}", 16 * (half + 2))
                        wait(dve, "mv_done", TT * b)
                        for k in range(TT):
                            nc.vector.bn_stats(bst[:, k, :], x_all[:, bass.ds(TT * b + k, 1), :]
                                               .rearrange("p o m -> p (o m)")).then_inc(S["stat_done"], 1)
                    if X and h == 6:
                        b = n + 1
                        wait(dve, "hhi_done", b + 1)
                        wait(dve, "vw_done", TT * (b - 1))
                        nc.vector.tensor_tensor(out=h_lo[other][:, :], in0=h_t[:, :], in1=h_hi[other][:, :],
                                                op=ALU.subtract).then_inc(S["h_ready"], 1)
                    if L and h == 7:
                        for k in range(TT):
                            alone(dve, "stat_done", TT * (n + 2) + k + 1)
                            nc.vector.bn_aggr(mv[parity][:, k, :], bst[:, k, :]).then_inc(S["mv_done"], 1)
                if isinstance(n, int) and n == -1:
                    dve.wait_ge(S["wvo_hi_done"], 1)
                    nc.vector.tensor_tensor(out=wvo_lo[:, :], in0=roped[1][:, 1, :], in1=wvo_hi[:, :],
                                            op=ALU.subtract).then_inc(S["split_done"], 1)
                    dve.wait_ge(S["b1_turned"], 1)
                    nc.vector.tensor_copy(b1_t[:, :], OP[1][:, 0:E * FC]).then_inc(S["b1_ready"], 1)
            iterations(dve, body)

            dve.wait_ge(S["count_done"], 1)
            steps = [0]

            def link(ins):
                steps[0] += 1
                ins.then_inc(S["table_step"], 1)
                dve.wait_ge(S["table_step"], steps[0])
            link(nc.vector.tensor_copy(counts_i[:, :], UN[1][:, 0:E]))
            link(nc.vector.tensor_scalar(tiles_i[:, :], UN[1][:, 0:E], float(TILE - 1), None, ALU.add))
            link(nc.vector.tensor_scalar(tiles_i[:, :], tiles_i[:, :], TILE.bit_length() - 1, None,
                                         ALU.logical_shift_right))
            link(nc.vector.tensor_copy(tiles_f[:, :], tiles_i[:, :]))
            link(nc.vector.tensor_tensor_scan(out=tiles_to[:, :], data0=ones_e[:, :], data1=tiles_f[:, :],
                                              initial=0.0, op0=ALU.mult, op1=ALU.add))

            def by_tile(v):
                return v.rearrange("p (o e) -> p o e", o=1).to_broadcast([P, ENTRIES, E])
            link(nc.vector.tensor_tensor(out=behind,
                                         in0=iota_t[:, :].rearrange("p (i o) -> p i o", o=1)
                                             .to_broadcast([P, ENTRIES, E]),
                                         in1=by_tile(tiles_to[:, :]), op=ALU.is_ge))
            link(nc.vector.tensor_reduce(out=tile_e[:, :], in_=behind, op=ALU.add, axis=AX.X))
            link(nc.vector.tensor_tensor(out=behind, in0=behind, in1=by_tile(tiles_f[:, :]),
                                         op=ALU.mult))
            link(nc.vector.tensor_reduce(out=tile_r[:, :], in_=behind, op=ALU.add, axis=AX.X))
            link(nc.vector.tensor_tensor(out=tile_r[:, :], in0=iota_t[:, :], in1=tile_r[:, :], op=ALU.subtract))
            link(nc.vector.tensor_scalar(tile_r[:, :], tile_r[:, :], float(TILE), None, ALU.mult))
            link(nc.vector.scalar_tensor_tensor(out=table[:, 1, :], in0=tile_e[:, :], scalar=float(REGION),
                                                in1=tile_r[:, :], op0=ALU.mult, op1=ALU.add))
            link(nc.vector.tensor_scalar(table[:, 0, :], tile_e[:, :], float(E - 1), None, ALU.min))
            link(nc.vector.tensor_scalar(table[:, 2, :], tile_e[:, :], float(E - 1), float(F), ALU.min, ALU.mult))

        @block.tensor
        def _(pe):
            pe.wait_ge(S["silu_done"], 1)
            pe.wait_ge(S["consts_ready"], 6)
            nc.tensor.transpose(OP[0][:, 0:NB], silu_c, ident[0:NB, 0:NB]).then_inc(S["ct_done"], 1)
            pe.wait_ge(S["ct_ready"], 1)
            for j in range(2):
                nc.tensor.matmul(SC[0][:, j * NB:(j + 1) * NB], wmod_sb[:, j * M:(j + 1) * M], silu_ct,
                                 start=True, stop=True)
            nc.tensor.matmul(SC[1][0:NB, :], silu_ct, wmod_sb[:, 2 * M:6 * M], start=True, stop=True)\
                .then_inc(S["mod_done"], 1)
            pe.wait_ge(S["wv_in"], 32)
            for h in range(H):
                ins = nc.tensor.transpose(UN[0][:, h * P:(h + 1) * P], roped[0][:, 2, h * D:(h + 1) * D], ident[:, :])
            ins.then_inc(S["wvt_done"], 1)
            pe.wait_ge(S["wvt_ready"], 1)
            for h in range(H):
                ins = nc.tensor.matmul(UN[1][:, h * M:(h + 1) * M], roped[1][:, 0, h * M:(h + 1) * M],
                                       roped[0][:, 3, h * M:(h + 1) * M], start=True, stop=True)
            ins.then_inc(S["wvo_done"], 1)
            pe.wait_ge(S["b_in"], 32)
            nc.tensor.transpose(OP[1][:, 0:E * FC], b1_rows, ident[0:E * FC, 0:E * FC]).then_inc(S["b1_turned"], 1)
            pe.wait_ge(S["wvo_scaled"], 1)
            pe.wait_ge(S["ones_ready"], 8)
            pe.wait_ge(S["iota_done"], 12)
            pe.wait_ge(S["router_in"], 16 * (TT + 1))
            pe.wait_ge(S["mod_copied"], 3)

            def split_product(dst, hi, lo, w_hi, w_lo):
                for k in range(0, w_hi.shape[1], 512):
                    for m, (a, w) in enumerate(((hi, w_hi), (hi, w_lo), (lo, w_hi))):
                        ins = nc.tensor.matmul(dst[:, k:k + 512], a, w[:, k:k + 512], start=(m == 0), stop=(m == 2))
                return ins

            def body(half, parity, live):
                n = 2 * half + parity
                _, X, A, B, C, _, N2, RT, ST = live
                other = 1 - parity

                def values_times_probs(b, h):
                    g = H * b + h
                    if h == 0:
                        wait(pe, "vals_ready", TT * (b + 1))
                    wait(pe, "exp_done", 2 * (g + 1))
                    wait(pe, "acc_done", TT * (g - 1))
                    o, pr, v = OP[h % 2], probs[:, h % NPR, :], vals[parity]
                    nc.tensor.matmul(o[:, 0:D + 1], pr[:, 0:P], v[:, 0, h, 0:D + 1], start=True, stop=True)
                    nc.tensor.matmul(o[:, 256:256 + D + 1], pr[:, P:2 * P], v[:, 0, h, 0:D + 1],
                                     start=True, stop=False)
                    nc.tensor.matmul(o[:, 256:256 + D + 1], pr[:, 2 * P:3 * P], v[:, 1, h, 0:D + 1],
                                     start=False, stop=True).then_inc(S["o_done"], 1)

                for h in range(H):
                    g = H * (n - 2) + h
                    if C or ST and h == 0 or RT and h == 1:
                        wait(pe, "exp_done", cap(2 * (g - 1), 2 * H * NB))
                        if h == 2 or not C:
                            wait(pe, "ahead_copied", n - 5 if h == 2 else n - 6)
                        if h == 3 or not C:
                            wait(pe, "lg_ready", cap(n - 4 if h == 3 else n - 5, NB))
                    if ST and h == 0:
                        b = n - 6
                        wait(pe, "route_step", STEPS * b + CHOSEN)
                        dst = SC[0][:, BESIDE:BESIDE + TT * E]
                        both = counts[parity][:, :].rearrange("p (o e) -> p o e", o=1).to_broadcast([P, TT, E])
                        nc.tensor.matmul(dst, before_bf[:, :], chosen[:, :, :], start=True, stop=False)
                        for t in range(1, TT):
                            for k in range(t):
                                nc.tensor.matmul(dst[:, t * E:(t + 1) * E], ones_bf[:, :], chosen[:, k, :],
                                                 start=False, stop=False)
                        ins = nc.tensor.matmul(dst, ones_bf[:, :], both, start=False, stop=True)
                        ins.then_inc(S["px_done"], 1)
                    if RT and h == 1:
                        b = n - 5
                        wait(pe, "h2t_copied", b + 1)
                        dst = SC[1][:, BESIDE:BESIDE + TT * E]
                        nc.tensor.matmul(dst, ones_row[:, :], br_sb[:, :], start=True, stop=False)
                        for t in range(TT):
                            ins = nc.tensor.matmul(dst[:, t * E:(t + 1) * E], h2_t[:, t * P:(t + 1) * P], wr_sb[:, :],
                                                   start=False, stop=(t == TT - 1))
                        ins.then_inc(S["rt_done"], 1)
                    if C:
                        if h == 0:
                            wait(pe, "tr_copied", NU * (n - 1))
                        s, q, k = SC[h % 2], q_t[parity], k_t[parity]
                        diagonal = s[:, 0:2 * T].rearrange("p (a c) -> p a c", a=TT)[:, :, 0:P]
                        mask = causal_bf[:, :].rearrange("p (o c) -> p o c", o=1).to_broadcast([P, TT, P])
                        nc.tensor.matmul(s[:, P:T], k[:, h, 0:P], q[:, h, P:T], start=True, stop=True)
                        nc.tensor.matmul(diagonal, ident_bf[:, :], mask, start=True, stop=False)
                        nc.tensor.matmul(s[:, 0:P], k[:, h, 0:P], q[:, h, 0:P], start=False, stop=False)
                        nc.tensor.matmul(s[:, T:T + P], k[:, h, P:T], q[:, h, P:T], start=False, stop=True)\
                            .then_inc(S["s_done"], 1)
                    if A:
                        w, u = 2 * NU * n + h, h // 2
                        t, kind = u % TT, u // TT
                        if h == 0:
                            wait(pe, "h_ready", n + 1)
                        if isinstance(n, int) and n == 0 and h == 0:
                            wait(pe, "split_done", 2)
                        wait(pe, "rope_done", w - 1)
                        toks = slice(t * P, (t + 1) * P)
                        c0 = kind * HD + (h % 2) * HH * D
                        split_product(UN[0][:, (h % 2) * HH * D:(h % 2 + 1) * HH * D], h_hi[parity][:, toks],
                                      h_lo[parity][:, toks], wqk_hi[:, c0:c0 + HH * D], wqk_lo[:, c0:c0 + HH * D])\
                            .then_inc(S["p_done"], 1)
                    if (h == 0 and B) or (h == H_AT and X and not B) or (h == H2_AT and N2 and not B):
                        wait(pe, "h2t_copied", cap(n - 4, NB))
                        wait(pe, "ht32_done", cap(n + 1, NB))
                    if B and h in TURNED:
                        b, u = n - 1, TURNED[h]
                        if h == 1:
                            wait(pe, "tr_copied", NU * b + 1)
                        elif h == Q_AT:
                            if X:
                                wait(pe, "ht32_done", n + 2)
                            else:
                                wait(pe, "vals_ready", TT * n)
                        elif h == Q_AT + 1:
                            wait(pe, "tr_copied", NU * b + TT + 1)
                        if u >= TT:
                            wait(pe, "add_done", 2 * (NU * b + u + 1))
                        else:
                            wait(pe, "qs_done", TT * b + u + 1)
                        for j in range(H):
                            ins = nc.tensor.transpose(UN[1][:, j * P:(j + 1) * P],
                                                      roped[other][:, u, j * D:(j + 1) * D], ident[:, :])
                        ins.then_inc(S["tr_done"], 1)
                    if B and h in VALUES:
                        b, t = n - 1, VALUES[h]
                        if isinstance(n, int) and n == 1:
                            wait(pe, "split_done", 3)
                        if t == 0:
                            wait(pe, "tr_copied", NU * b + TT)
                        else:
                            wait(pe, "vals_ready", TT * b + t)
                        toks = slice(t * P, (t + 1) * P)
                        split_product(UN[1], h_hi[other][:, toks], h_lo[other][:, toks],
                                      wvo_hi[:, :], wvo_lo[:, :]).then_inc(S["vw_done"], 1)
                    if X and h == H_AT:
                        b = n + 1
                        if B:
                            wait(pe, "vals_ready", TT * n)
                        wait(pe, "xn_ready", TT * (b + 1))
                        for t in range(TT):
                            ins = nc.tensor.transpose(UN[1][:, t * P:(t + 1) * P], xn[:, t, :], ident[:, :])
                        ins.then_inc(S["tx_done"], 1)
                    if N2 and h == H2_AT:
                        b = n - 4
                        if B:
                            wait(pe, "tr_copied", NU * n)
                        wait(pe, "h2_ready", b + 1)
                        for t in range(TT):
                            ins = nc.tensor.transpose(UN[1][:, t * P:(t + 1) * P], h2_rows[:, t, :],
                                                      ident[:, :])
                        ins.then_inc(S["h2t_done"], 1)
                    if C and h >= 1:
                        values_times_probs(n - 2, h - 1)
                if C:
                    values_times_probs(n - 2, H - 1)
            iterations(pe, body)
            wait(pe, "lg_ready", NB)
            wait(pe, "route_step", STEPS * NB)
            nc.tensor.matmul(UN[1][:, 0:E], ones_bf[:, :], counts[0][:, :], start=True, stop=True)\
                .then_inc(S["count_done"], 1)

        attention.close()

        phase[0] = late = ExitStack()
        gb_all = sb("gb_all", [P, NB, M])
        phase[0] = experts = ExitStack()
        SLOTS = 8
        tile_x = [sb(f"tile_x{k}", [P, TILE // P, RW]) for k in range(SLOTS)]
        place_y = [sb(f"place_y{k}", [P, TILE // P], I32) for k in range(SLOTS)]
        x_hi = [sb(f"x_hi{k}", [P, TILE], F16) for k in range(2)]
        x_lo = [sb(f"x_lo{k}", [P, TILE], F16) for k in range(2)]
        hidden = [sb(f"hidden{k}", [P, FC, TILE]) for k in range(2)]
        hid_hi = [sb(f"hid_hi{k}", [P, FC, TILE], F16) for k in range(2)]
        hid_lo = [sb(f"hid_lo{k}", [P, FC, TILE], F16) for k in range(2)]
        y_sum = sb("y_sum", [P, TILE // P, M])
        y_pos = sb("y_pos", [P, TILE // P, M])
        y_out = [sb(f"y_out{k}", [P, TILE // P, M]) for k in range(SLOTS)]
        XT = [ps(f"xt{k}", [P, 512]) for k in range(1)]
        UP = [ps(f"up{k}", [P, 1024]) for k in range(2)]
        DN = [ps(f"down{k}", [P, 512]) for k in range(2)]
        TS = TILE // P

        def tiles(e, body):
            def live(n):
                return [0 <= n + d < NTILES for d in (SLOTS - 1, 1, 0, -1)]
            rounds = (NTILES - SLOTS + 1) // SLOTS
            for n in range(1 - SLOTS, SLOTS):
                body(n // SLOTS, n % SLOTS, live(n))
            with e.Fori(1, rounds) as turn:
                for slot in range(SLOTS):
                    body(turn, slot, [True] * 4)
            for n in range(rounds * SLOTS, NTILES + 1):
                body(n // SLOTS, n % SLOTS, live(n))

        def round_of(turn, slot, d):
            return turn + (slot + d) // SLOTS, (slot + d) % SLOTS

        def entries(e, column):
            registers = [e.alloc_register(f"entry{k}") for k in range(SLOTS)]
            most = (E - 1, E * REGION + (SPARE - 1) * TILE, (E - 1) * F)[column]

            def value(slot):
                return e.snap(registers[slot % SLOTS], min_val=0, max_val=most)

            def fetch(slot, i):
                if not isinstance(i, int) or 0 <= i < NTILES:
                    e.reg_load(registers[slot % SLOTS], table[0:1, column, bass.ds(i, 1)])
            return value, fetch

        block = experts.enter_context(nc.Block())

        @block.sync
        def _(sp):
            first_row, fetch = entries(sp, 1)
            fetch(0, 0)

            def body(turn, slot, live):
                LOAD, _, _, _ = live
                if LOAD:
                    i = SLOTS * turn + slot + SLOTS - 1
                    before, at = round_of(turn, slot, SLOTS - 1)
                    alone(sp, "places_ready", i - SLOTS + 1)
                    sp.dma_start(tile_x[at][:, :, :], x_rows[bass.ds(first_row(at), TILE), :]
                                 .rearrange("(p s) c -> p s c", p=P)).then_inc(S[f"tile_in{at}"], 16)
                    fetch(at + 1, i + 1)
            tiles(sp, body)
            sp.dma_start(gb_all[:, :, :], mod_dram[:, 3 * M:4 * M].rearrange("(o b) m -> o b m", o=1)
                         .broadcast_to([P, NB, M])).then_inc(S["gates_in"], 16)

        @block.gpsimd
        def _(pool):
            def body(turn, slot, live):
                _, _, _, DOWN = live
                if DOWN:
                    i = SLOTS * turn + slot - 1
                    at = (slot - 1) % SLOTS
                    alone(pool, "y_step", 3 * (i + 1))
                    for s in range(TS):
                        pool.indirect_dma_start(
                            out=y_rows, out_offset=bass.IndirectOffsetOnAxis(ap=place_y[at][:, s:s + 1], axis=0),
                            in_=y_out[at][:, s, :], in_offset=None, bounds_check=K * NTOK - 1, oob_is_err=False)\
                            .then_inc(S[f"y_stored{at}"], 16)
            tiles(pool, body)
            for k in range(SLOTS):
                pool.wait_ge(S[f"y_stored{k}"], 16 * TS * ((NTILES - k + SLOTS - 1) // SLOTS))

        @block.scalar
        def _(act):

            expert, fetch = entries(act, 0)
            fetch(0, 0)

            def body(turn, slot, live):
                n = SLOTS * turn + slot
                _, T1, UPW, _ = live
                parity, other = slot % 2, 1 - slot % 2
                if T1:
                    i = n + 1
                    wait(act, "t_done", i + 1)
                    wait(act, "up_done", FC * (i - 1))
                    nc.scalar.activation(x_hi[other][:, :], XT[0][:, 0:TILE], ACT.Copy).then_inc(S["x_hi_done"], 1)
                if UPW:
                    mine = expert(slot)

                    def gelu(k):
                        wait(act, "up_done", FC * n + k + 1)
                        wait(act, "hid_split", 2 * (n - 1))
                        nc.scalar.activation(hidden[parity][:, k, :], UP[k // 2][:, (k % 2) * 512:(k % 2) * 512 + TILE],
                                             ACT.Gelu, bias=b1_t[:, bass.ds(mine * FC + k, 1)], scale=1.0 / WS)\
                            .then_inc(S["gelu_done"], 1)

                    def high(k):
                        pair = slice(k * FC // 2, (k + 1) * FC // 2)
                        wait(act, "gelu_done", FC * n + (k + 1) * FC // 2)
                        wait(act, "down_done", n - 1)
                        nc.scalar.activation(hid_hi[parity][:, pair, :], hidden[parity][:, pair, :], ACT.Copy)\
                            .then_inc(S["hid_hi_done"], 1)
                    for k in range(FC):
                        gelu(k)
                        if k == FC // 2:
                            high(0)
                            fetch(slot + 1, n + 1)
                    high(1)
            tiles(act, body)

        @block.vector
        def _(dve):

            expert, fetch = entries(dve, 0)
            fetch(0, 0)

            def body(turn, slot, live):
                n = SLOTS * turn + slot
                _, T1, UPW, DOWN = live
                parity, other = slot % 2, 1 - slot % 2
                if T1:
                    i = n + 1
                    wait(dve, "x_hi_done", i + 1)
                    wait(dve, "up_done", FC * (i - 1))
                    nc.vector.tensor_tensor(out=x_lo[other][:, :], in0=XT[0][:, 0:TILE], in1=x_hi[other][:, :],
                                            op=ALU.subtract).then_inc(S["x_split"], 1)
                    before, at = round_of(turn, slot, 1)
                    wait(dve, f"y_stored{at}", 16 * TS * before)
                    nc.vector.tensor_copy(place_y[at][:, :], tile_x[at][:, :, M:RW]
                                          .rearrange("p s o -> p (s o)")).then_inc(S["places_ready"], 1)
                if UPW:
                    for k in range(2):
                        pair = slice(k * FC // 2, (k + 1) * FC // 2)
                        wait(dve, "hid_hi_done", 2 * n + k + 1)
                        wait(dve, "down_done", n - 1)
                        nc.vector.tensor_tensor(out=hid_lo[parity][:, pair, :], in0=hidden[parity][:, pair, :],
                                                in1=hid_hi[parity][:, pair, :], op=ALU.subtract)\
                            .then_inc(S["hid_split"], 1)
                    fetch(slot + 1, n + 1)
                if DOWN:
                    i = n - 1
                    at = (slot - 1) % SLOTS
                    wait(dve, "down_done", i + 1)
                    wait(dve, "y_step", 3 * i)
                    nc.vector.scalar_tensor_tensor(
                        out=y_sum[:, :, :], scalar=1.0 / WS, in0=DN[other][:, 0:TILE].rearrange("p (s m) -> p s m", s=TS),
                        in1=b2_b[:, bass.ds(expert(slot - 1) * M, M)].rearrange("p (o m) -> p o m", o=1)
                            .to_broadcast([P, TS, M]), op0=ALU.mult, op1=ALU.add).then_inc(S["y_step"], 1)
                    wait(dve, "y_step", 3 * i + 1)
                    nc.vector.tensor_scalar(y_pos[:, :, :], y_sum[:, :, :], 0.0, None, ALU.max)\
                        .then_inc(S["y_step"], 1)
                    wait(dve, "y_step", 3 * i + 2)
                    nc.vector.scalar_tensor_tensor(out=y_out[at][:, :, :], in0=y_sum[:, :, :], scalar=0.0,
                                                   in1=y_pos[:, :, :], op0=ALU.min, op1=ALU.add)\
                        .then_inc(S["y_step"], 1)
            tiles(dve, body)

        @block.tensor
        def _(pe):

            columns_of, fetch = entries(pe, 2)
            fetch(0, 0)

            def body(turn, slot, live):
                n = SLOTS * turn + slot
                _, T1, UPW, DOWN = live
                parity, other = slot % 2, 1 - slot % 2
                if T1:
                    i = n + 1
                    before, at = round_of(turn, slot, 1)
                    wait(pe, f"tile_in{at}", 16 * (before + 1))
                    wait(pe, "x_split", i)
                    for s in range(TS):
                        ins = nc.tensor.transpose(XT[0][:, s * P:(s + 1) * P], tile_x[at][:, s, 0:M], ident[:, :])
                    ins.then_inc(S["t_done"], 1)
                if UPW:
                    mine = columns_of(slot)
                    wait(pe, "x_split", n + 1)
                    for k in range(FC):
                        wait(pe, "gelu_done", FC * (n - 1) + k + 1)
                        dst = UP[k // 2][:, (k % 2) * 512:(k % 2) * 512 + TILE]
                        cols = bass.ds(mine + k * P, P)
                        nc.tensor.matmul(dst, w1_hi[:, cols], x_hi[parity][:, :], start=True, stop=False)
                        nc.tensor.matmul(dst, w1_hi[:, cols], x_lo[parity][:, :], start=False, stop=False)
                        nc.tensor.matmul(dst, w1_lo[:, cols], x_hi[parity][:, :], start=False, stop=True)\
                            .then_inc(S["up_done"], 1)
                    fetch(slot + 1, n + 1)
                if DOWN:
                    i = n - 1
                    mine = columns_of(slot - 1)
                    wait(pe, "y_step", 3 * (i - 2) + 1)
                    wait(pe, "hid_split", 2 * (i + 1))
                    for s in range(TS):
                        dst = DN[other][:, s * M:(s + 1) * M]
                        rows_s = slice(s * P, (s + 1) * P)
                        for k in range(FC):
                            cols = bass.ds(mine + k * M, M)
                            nc.tensor.matmul(dst, hid_hi[other][:, k, rows_s], w2_hi[:, cols], start=(k == 0),
                                             stop=False)
                            nc.tensor.matmul(dst, hid_lo[other][:, k, rows_s], w2_hi[:, cols], start=False, stop=False)
                            ins = nc.tensor.matmul(dst, hid_hi[other][:, k, rows_s], w2_lo[:, cols], start=False,
                                                   stop=(k == FC - 1))
                    ins.then_inc(S["down_done"], 1)
            tiles(pe, body)

        experts.close()

        phase[0] = last = ExitStack()
        GROUP = 2
        GT = GROUP * TT
        SLOTS = 4
        GROUPS = NB // GROUP
        back = [[sb(f"back{j}{k}", [P, GT, M]) for k in range(SLOTS)] for j in range(K)]
        first = [sb(f"first{k}", [P, GT, M]) for k in range(2)]
        mixed = [sb(f"mixed{k}", [P, GT, M]) for k in range(2)]
        sums = [sb(f"sums{k}", [P, GT, M]) for k in range(SLOTS)]
        block = last.enter_context(nc.Block())

        def groups(e, body):
            for n in range(SLOTS + 1):
                body(n // SLOTS, n % SLOTS)
            with e.Fori(1, GROUPS // SLOTS - 1) as turn:
                for d in range(1, SLOTS + 1):
                    body(turn + d // SLOTS, d % SLOTS)
            for n in range(GROUPS - SLOTS + 1, GROUPS):
                body(n // SLOTS, n % SLOTS)

        def weight(n, g, k):
            return weights[:, bass.ds(GT * n + g, 1), k:k + 1].rearrange("p o k -> p (o k)")

        @block.sync
        def _(sp):
            yv = y_rows.rearrange("(j g p) m -> j p g m", j=K, p=P)

            def body(turn, slot):
                n = SLOTS * turn + slot
                alone(sp, "sum_done", n - SLOTS + 1)
                for j in range(K):
                    sp.dma_start(back[j][slot][:, :, :], yv[j, :, bass.ds(n * GT, GT), :])\
                        .then_inc(S[f"back_in{slot}"], 16)
            groups(sp, body)

        @block.scalar
        def _(act):
            ov = out.rearrange("b (t p) m -> p (b t) m", p=P)

            def store(turn, slot):
                n = SLOTS * turn + slot
                wait(act, "sum_done", n + 1)
                act.dma_start(ov[:, bass.ds(GT * n, GT), :], sums[slot][:, :, :])\
                    .then_inc(S[f"out_stored{slot}"], 16)

            def body(turn, slot):
                n = SLOTS * turn + slot
                act.wait_ge(S[f"back_in{slot}"], 16 * K * (turn + 1))
                wait(act, "mix_done", GT * (n - 1))
                for g in range(GT):
                    nc.scalar.activation(first[slot % 2][:, g, :], back[0][slot][:, g, :], ACT.Copy,
                                         scale=weight(n, g, 0)).then_inc(S["first_done"], 1)
                if not isinstance(turn, int) or n >= 2:
                    store(turn + (slot - 2) // SLOTS, (slot - 2) % SLOTS)
            groups(act, body)
            for n in range(GROUPS - 2, GROUPS):
                store(n // SLOTS, n % SLOTS)
            for k in range(SLOTS):
                act.wait_ge(S[f"out_stored{k}"], 16 * GROUPS // SLOTS)

        @block.gpsimd
        def _(pool):
            pool.wait_ge(S["gates_in"], 16)

            def body(turn, slot):
                n = SLOTS * turn + slot
                wait(pool, "mix_done", GT * (n + 1))
                mix = mixed[slot % 2][:, :, :].rearrange("p (b t) m -> p b t m", b=GROUP)
                pool.tensor_tensor(out=mix, in0=mix, in1=gb_all[:, bass.ds(GROUP * n, GROUP), :]
                                   .rearrange("p b (o m) -> p b o m", o=1)
                                   .to_broadcast([P, GROUP, TT, M]), op=ALU.mult).then_inc(S["gated"], 1)
            groups(pool, body)

        @block.vector
        def _(dve):
            def residual(turn, slot):
                n = SLOTS * turn + slot
                wait(dve, "gated", n + 1)
                wait(dve, f"out_stored{slot}", 16 * turn)
                nc.vector.tensor_tensor(out=sums[slot][:, :, :], in0=mixed[slot % 2][:, :, :],
                                        in1=x_all[:, bass.ds(GT * n, GT), :], op=ALU.add).then_inc(S["sum_done"], 1)

            def body(turn, slot):
                n = SLOTS * turn + slot
                dve.wait_ge(S[f"back_in{slot}"], 16 * K * (turn + 1))
                wait(dve, "sum_done", n - 1)
                for g in range(GT):
                    wait(dve, "first_done", GT * n + g + 1)
                    nc.vector.scalar_tensor_tensor(out=mixed[slot % 2][:, g, :], in0=back[1][slot][:, g, :],
                                                   scalar=weight(n, g, 1), in1=first[slot % 2][:, g, :],
                                                   op0=ALU.mult, op1=ALU.add).then_inc(S["mix_done"], 1)
                if not isinstance(turn, int) or n >= 1:
                    residual(turn + (slot - 1) // SLOTS, (slot - 1) % SLOTS)
            groups(dve, body)
            residual((GROUPS - 1) // SLOTS, (GROUPS - 1) % SLOTS)
        last.close()
        late.close()


_INS = ["L0_attn_x", "L0_attn_wq", "L0_attn_wk", "L0_attn_wv", "L0_attn_wo", "L0_ffn_Wr", "L0_ffn_br",
        "L0_ffn_W1", "L0_ffn_b1", "L0_ffn_W2", "L0_ffn_b2", "L0_c", "L0_wmod"]


def rope_tables(length, width, base=1250.0):
    half = width // 2
    pos = np.arange(length, dtype=np.float32)[:, None]
    freqs = np.power(np.float32(base), -np.arange(half, dtype=np.float32) / np.float32(half)).astype(np.float32)
    rad = (pos * freqs[None, :]).astype(np.float32)
    cos, sin = np.cos(rad).astype(np.float32), np.sin(rad).astype(np.float32)
    return cos, np.concatenate([-sin, sin], axis=1)


def kernel(**inputs):
    import concourse.bacc as bacc
    from concourse.bass_utils import run_bass_kernel_spmd

    nc = bacc.Bacc("TRN2", target_bir_lowering=False, num_devices=1)
    arrays, args = {}, []
    given = [(name, np.ascontiguousarray(inputs[name])) for name in _INS]
    cos, sin = rope_tables(given[0][1].shape[1], given[1][1].shape[2])
    for name, a in [*given, ("rope_cos", cos), ("rope_sin", sin)]:
        arrays[f"in_{name}"] = a
        args.append(nc.dram_tensor(f"in_{name}", a.shape, mybir.dt.from_np(a.dtype), kind="ExternalInput").ap())
    args.append(nc.dram_tensor("out_x", given[0][1].shape, F32, kind="ExternalOutput").ap())
    adaln_block(nc, *args)
    r = run_bass_kernel_spmd(nc, [arrays], core_ids=[0])
    return r.results[0]["out_x"]
```
